# Optimizing a Trainium2 kernel written in Bass

```python
import numpy as np
import jax
import jax.numpy as jnp

def _softmax(x, axis=-1):
    return jax.nn.softmax(x, axis=axis)

def _gelu(x):
    return jax.nn.gelu(x, approximate=True)

def _silu(x):
    return jax.nn.silu(x)

def _sigmoid(x):
    return jax.nn.sigmoid(x)

def _layernorm(x, axis=-1, eps=1e-05):
    m = jnp.mean(x, axis=axis, keepdims=True)
    v = jnp.var(x, axis=axis, keepdims=True)
    return (x - m) / jnp.sqrt(v + eps)

def _scatter_add(tgt, idx, src, axis=0):
    return tgt.at[idx].add(src)

def _segment_sum(src, seg, n):
    return jax.ops.segment_sum(src, seg, n)
kernel_name = 'mk_gnn_resnorm_d4_gnn_r32_f4661f'

def setup_inputs(seed: int=0):
    np.random.seed(seed)
    _w = jnp.asarray

    def _rec_inputs():
        import jax
        import jax.numpy as jnp
        _gk = jax.random.key(seed)
        x = -0.0003713 + 1 * jax.random.normal(jax.random.fold_in(_gk, 1), (3125, 128), jnp.float32)
        _s = jax.random.randint(jax.random.fold_in(_gk, 2), (25000,), 0, 3125, jnp.int32)
        _d = jax.random.randint(jax.random.fold_in(_gk, 3), (25000,), 0, 3125, jnp.int32)
        _loop = jnp.arange(3125, dtype=jnp.int32)
        src = jnp.concatenate([_s, _d, _loop])
        dst = jnp.concatenate([_d, _s, _loop])
        _o = jnp.argsort(dst, stable=True)
        src = src[_o]
        dst = dst[_o]
        edge_weight = 0.000452788 + 0.999756 * jax.random.normal(jax.random.fold_in(_gk, 13), (53125,), jnp.float32)
        return (x, src, dst, edge_weight)
    x, src, dst, edge_weight = _rec_inputs()

    def _L0_gnn_setup():
        import jax, jax.numpy as jnp
        import numpy as np
        EPS = 1e-05
        key = jax.random.key(seed)
        ks = jax.random.split(key, 6)
        N, E, C, L = (3125, 50000, 128, 4)
        x = jax.random.normal(ks[0], (N, C), dtype=jnp.float32)
        edge_index = jax.random.randint(ks[1], (2, E), 0, N, dtype=jnp.int64)
        Wl = jax.random.normal(ks[2], (L, C, C), dtype=jnp.float32) * (1.0 / np.sqrt(C))
        bl = jax.random.normal(ks[3], (L, C), dtype=jnp.float32) * 0.01
        Wr = jax.random.normal(ks[4], (L, C, C), dtype=jnp.float32) * (1.0 / np.sqrt(C))
        ln_w = jnp.ones((L, C), dtype=jnp.float32)
        ln_b = jnp.zeros((L, C), dtype=jnp.float32)
        return {'x': x, 'edge_index': edge_index, 'Wl': Wl, 'bl': bl, 'Wr': Wr, 'ln_w': ln_w, 'ln_b': ln_b}
    _L0_gnn_all = _L0_gnn_setup()
    _L0_gnn_in = {k: v for k, v in _L0_gnn_all.items() if k in ('Wl', 'bl', 'Wr', 'ln_w', 'ln_b')}
    del _L0_gnn_all

    def _L1_gnn_setup():
        import jax, jax.numpy as jnp
        import numpy as np
        N_NODES = 3125
        N_EDGES = 50000
        D_IN = 128
        D_OUT = 128
        key = jax.random.key(seed)
        k1, k2, k3, k4, k5 = jax.random.split(key, 5)
        x = jax.random.normal(k1, (N_NODES, D_IN), dtype=jnp.float32)
        edge_index = jax.random.randint(k2, (2, N_EDGES), 0, N_NODES, dtype=jnp.int64)
        edge_features = jax.random.normal(k3, (N_EDGES,), dtype=jnp.float32)
        bound = 1.0 / np.sqrt(D_IN)
        W = jax.random.uniform(k4, (D_OUT, D_IN), minval=-bound, maxval=bound, dtype=jnp.float32)
        b = jax.random.uniform(k5, (D_OUT,), minval=-bound, maxval=bound, dtype=jnp.float32)
        return {'x': x, 'edge_index': edge_index, 'edge_features': edge_features, 'W': W, 'b': b}
    _L1_gnn_all = _L1_gnn_setup()
    _L1_gnn_in = {k: v for k, v in _L1_gnn_all.items() if k in ('W', 'b')}
    del _L1_gnn_all

    def _L2_gnn_setup():
        import jax, jax.numpy as jnp
        import numpy as np
        N, E, DIM, H = (50000, 25000, 128, 8)
        HD = DIM // H
        EPS = 1e-05

        def _batch_norm(x, g, b):
            mean = jnp.mean(x, axis=0)
            var = jnp.mean((x - mean) ** 2, axis=0)
            return (x - mean) * jax.lax.rsqrt(var + EPS) * g + b
        key = jax.random.key(seed)
        ks = jax.random.split(key, 12)
        s = 1.0 / np.sqrt(DIM)
        inp = {'h': jax.random.normal(ks[0], (N, DIM), jnp.float32), 'src': jax.random.randint(ks[1], (E,), 0, N, jnp.int32), 'dst': jax.random.randint(ks[2], (E,), 0, N, jnp.int32), 'Wq': jax.random.normal(ks[3], (DIM, DIM), jnp.float32) * s, 'Wk': jax.random.normal(ks[4], (DIM, DIM), jnp.float32) * s, 'Wv': jax.random.normal(ks[5], (DIM, DIM), jnp.float32) * s, 'Wo': jax.random.normal(ks[6], (DIM, DIM), jnp.float32) * s, 'bo': jnp.zeros((DIM,), jnp.float32), 'bn1_g': jnp.ones((DIM,), jnp.float32), 'bn1_b': jnp.zeros((DIM,), jnp.float32), 'bn2_g': jnp.ones((DIM,), jnp.float32), 'bn2_b': jnp.zeros((DIM,), jnp.float32), 'W1': jax.random.normal(ks[7], (DIM, 2 * DIM), jnp.float32) * s, 'b1': jnp.zeros((2 * DIM,), jnp.float32), 'W2': jax.random.normal(ks[8], (2 * DIM, DIM), jnp.float32) * (1.0 / np.sqrt(2 * DIM)), 'b2': jnp.zeros((DIM,), jnp.float32)}
        return inp
    _L2_gnn_all = _L2_gnn_setup()
    _L2_gnn_in = {k: v for k, v in _L2_gnn_all.items() if k in ('Wq', 'Wk', 'Wv', 'Wo', 'bo', 'bn1_g', 'bn1_b', 'bn2_g', 'bn2_b', 'W1', 'b1', 'W2', 'b2')}
    del _L2_gnn_all

    def _L3_gnn_setup():
        import jax, jax.numpy as jnp
        import numpy as np
        N_NODES = 3125
        D_IN = 128
        D_OUT = 128
        N_EDGES = 50000
        key = jax.random.key(seed)
        k1, k2, k3, k4 = jax.random.split(key, 4)
        x = jax.random.normal(k1, (N_NODES, D_IN), dtype=jnp.float32)
        edges = jax.random.randint(k2, (2, N_EDGES), 0, N_NODES, dtype=jnp.int32)
        bound = 1.0 / np.sqrt(D_IN)
        W = jax.random.uniform(k3, (D_OUT, D_IN), minval=-bound, maxval=bound, dtype=jnp.float32)
        b = jax.random.uniform(k4, (D_OUT,), minval=-bound, maxval=bound, dtype=jnp.float32)
        return {'x': x, 'edges': edges, 'W': W, 'b': b}
    _L3_gnn_all = _L3_gnn_setup()
    _L3_gnn_in = {k: v for k, v in _L3_gnn_all.items() if k in ('W', 'b')}
    del _L3_gnn_all
    return {'x': x, 'src': src, 'dst': dst, 'edge_weight': edge_weight, 'L0_gnn_Wl': _L0_gnn_in['Wl'], 'L0_gnn_bl': _L0_gnn_in['bl'], 'L0_gnn_Wr': _L0_gnn_in['Wr'], 'L0_gnn_ln_w': _L0_gnn_in['ln_w'], 'L0_gnn_ln_b': _L0_gnn_in['ln_b'], 'L1_gnn_W': _L1_gnn_in['W'], 'L1_gnn_b': _L1_gnn_in['b'], 'L2_gnn_Wq': _L2_gnn_in['Wq'], 'L2_gnn_Wk': _L2_gnn_in['Wk'], 'L2_gnn_Wv': _L2_gnn_in['Wv'], 'L2_gnn_Wo': _L2_gnn_in['Wo'], 'L2_gnn_bo': _L2_gnn_in['bo'], 'L2_gnn_bn1_g': _L2_gnn_in['bn1_g'], 'L2_gnn_bn1_b': _L2_gnn_in['bn1_b'], 'L2_gnn_bn2_g': _L2_gnn_in['bn2_g'], 'L2_gnn_bn2_b': _L2_gnn_in['bn2_b'], 'L2_gnn_W1': _L2_gnn_in['W1'], 'L2_gnn_b1': _L2_gnn_in['b1'], 'L2_gnn_W2': _L2_gnn_in['W2'], 'L2_gnn_b2': _L2_gnn_in['b2'], 'L3_gnn_W': _L3_gnn_in['W'], 'L3_gnn_b': _L3_gnn_in['b']}

def reference(x, src, dst, edge_weight, L0_gnn_Wl, L0_gnn_bl, L0_gnn_Wr, L0_gnn_ln_w, L0_gnn_ln_b, L1_gnn_W, L1_gnn_b, L2_gnn_Wq, L2_gnn_Wk, L2_gnn_Wv, L2_gnn_Wo, L2_gnn_bo, L2_gnn_bn1_g, L2_gnn_bn1_b, L2_gnn_bn2_g, L2_gnn_bn2_b, L2_gnn_W1, L2_gnn_b1, L2_gnn_W2, L2_gnn_b2, L3_gnn_W, L3_gnn_b):
    import jax
    import jax.numpy as jnp

    def _L0_gnn_ref(x, edge_index, Wl, bl, Wr, ln_w, ln_b):
        import jax, jax.numpy as jnp
        import numpy as np
        EPS = 1e-05
        N = x.shape[0]
        src, dst = (edge_index[0], edge_index[1])
        deg = jax.ops.segment_sum(jnp.ones_like(dst, dtype=x.dtype), dst, num_segments=N)
        inv_deg = jnp.where(deg > 0, 1.0 / deg, 0.0)[:, None]
        for l in range(Wl.shape[0]):
            agg = jax.ops.segment_sum(x[src], dst, num_segments=N) * inv_deg
            h = agg @ Wl[l].T + bl[l] + x @ Wr[l].T
            mu = jnp.mean(h, axis=-1, keepdims=True)
            var = jnp.mean(jnp.square(h - mu), axis=-1, keepdims=True)
            h = (h - mu) * jax.lax.rsqrt(var + EPS) * ln_w[l] + ln_b[l]
            x = jax.nn.relu(h)
        return x

    def _L1_gnn_ref(x, edge_index, edge_features, W, b):
        import jax, jax.numpy as jnp
        import numpy as np
        N_NODES = 3125
        N_EDGES = 50000
        D_IN = 128
        D_OUT = 128
        src, dst = (edge_index[0], edge_index[1])
        n = x.shape[0]
        messages = x[src] @ W.T + b
        out = jax.ops.segment_sum(messages, dst, num_segments=n)
        counts = jax.ops.segment_sum(jnp.ones_like(dst, dtype=messages.dtype), dst, num_segments=n)
        counts = jnp.maximum(counts, 1.0)
        out = out / counts[:, None]
        return jax.nn.relu(out)

    def _L2_gnn_ref(h, src, dst, Wq, Wk, Wv, Wo, bo, bn1_g, bn1_b, bn2_g, bn2_b, W1, b1, W2, b2):
        import jax, jax.numpy as jnp
        import numpy as np
        N, E, DIM, H = (50000, 25000, 128, 8)
        HD = DIM // H
        EPS = 1e-05

        def _batch_norm(x, g, b):
            mean = jnp.mean(x, axis=0)
            var = jnp.mean((x - mean) ** 2, axis=0)
            return (x - mean) * jax.lax.rsqrt(var + EPS) * g + b
        n = h.shape[0]
        h_in1 = h
        hn = _batch_norm(h, bn1_g, bn1_b)
        Q = (hn @ Wq).reshape(n, H, HD)
        K = (hn @ Wk).reshape(n, H, HD)
        V = (hn @ Wv).reshape(n, H, HD)
        score = jnp.einsum('ehd,ehd->eh', K[src], Q[dst]) / np.sqrt(HD)
        score = jnp.clip(score, -5.0, 5.0)
        smax = jax.ops.segment_max(score, dst, num_segments=n)
        a = jnp.exp(score - smax[dst])
        asum = jax.ops.segment_sum(a, dst, num_segments=n)
        a = a / asum[dst]
        m = V[src] * a[:, :, None]
        wV = jax.ops.segment_sum(m, dst, num_segments=n).reshape(n, DIM)
        h2 = wV @ Wo + bo
        h2 = h_in1 + h2
        h_in2 = h2
        h3 = _batch_norm(h2, bn2_g, bn2_b)
        h3 = jax.nn.relu(h3 @ W1 + b1) @ W2 + b2
        return h_in2 + h3

    def _L3_gnn_ref(x, edges, W, b):
        import jax, jax.numpy as jnp
        import numpy as np
        N_NODES = 3125
        D_IN = 128
        D_OUT = 128
        N_EDGES = 50000
        num_nodes = x.shape[0]
        src, tgt = (edges[0], edges[1])
        aggregated = jax.ops.segment_sum(x[src], tgt, num_segments=num_nodes)
        counts = jax.ops.segment_sum(jnp.ones_like(tgt, dtype=x.dtype), tgt, num_segments=num_nodes)
        counts = jnp.maximum(counts, 1.0)
        combined = x + aggregated / counts[:, None]
        out = combined @ W.T + b
        return jax.nn.relu(out)
    edge_index = jnp.stack([src, dst])
    x = _layernorm(x + _L0_gnn_ref(x, edge_index, L0_gnn_Wl, L0_gnn_bl, L0_gnn_Wr, L0_gnn_ln_w, L0_gnn_ln_b), axis=-1)
    x = _layernorm(x + _L1_gnn_ref(x, edge_index, edge_weight, L1_gnn_W, L1_gnn_b), axis=-1)
    x = _layernorm(x + _L2_gnn_ref(x, src, dst, L2_gnn_Wq, L2_gnn_Wk, L2_gnn_Wv, L2_gnn_Wo, L2_gnn_bo, L2_gnn_bn1_g, L2_gnn_bn1_b, L2_gnn_bn2_g, L2_gnn_bn2_b, L2_gnn_W1, L2_gnn_b1, L2_gnn_W2, L2_gnn_b2), axis=-1)
    x = _layernorm(x + _L3_gnn_ref(x, edge_index, L3_gnn_W, L3_gnn_b), axis=-1)
    return x

_drawn_inputs = setup_inputs


def setup_inputs(seed=0):
    import zlib

    import numpy as np

    out = dict(_drawn_inputs(seed))
    spreads = {'L0_gnn_ln_w': (1.0, 0.2),
     'L0_gnn_ln_b': (0.0, 0.1),
     'L2_gnn_bo': (0.0, 0.1),
     'L2_gnn_bn1_g': (1.0, 0.2),
     'L2_gnn_bn1_b': (0.0, 0.1),
     'L2_gnn_bn2_g': (1.0, 0.2),
     'L2_gnn_bn2_b': (0.0, 0.1),
     'L2_gnn_b1': (0.0, 0.1),
     'L2_gnn_b2': (0.0, 0.1)}
    factors = {'L0_gnn_bl': 3.876}
    for name, (base, spread) in spreads.items():
        noise = np.random.default_rng([zlib.crc32(name.encode()), seed]).standard_normal(out[name].shape)
        drawn = base * np.exp(spread * noise) if base else spread * noise
        out[name] = jnp.asarray(drawn.astype(out[name].dtype))
    for name, factor in factors.items():
        out[name] = (out[name] * factor).astype(out[name].dtype)
    return out
```

```python
import numpy as np
import concourse.bass as bass
from concourse import mybir
from contextlib import ExitStack, contextmanager

fp32, fp16, bf16, i32 = mybir.dt.float32, mybir.dt.float16, mybir.dt.bfloat16, mybir.dt.int32
ALU = mybir.AluOpType
ACT = mybir.ActivationFunctionType
AX = mybir.AxisListType

N, E, C = 3125, 53125, 128
HEADS, HD = 8, 16
TILE = 125
NT = N // TILE
LANES = 128
CH = -(-E // LANES)
CHP = CH + 24
ROWS, ROWG = 104, CH // 104
NO_NODE = 4000.0
BWN = 25
BW = N // BWN
BKEYS = BWN * NT
BHALF = 13 * NT
BK = 5
CHUNK_OFF = 60000
BLK = 500
NBLK = N // BLK
EPS = 1e-5
GRP = 4
NG = CH // GRP
VW = C + HEADS
SPILL = 15
ALPHA_LN = 4096.0
LN_BOUND = 11.4


class Steps:

    def __init__(self, eng, sem):
        self.eng, self.sem, self.n, self.base = eng, sem, 0, 0

    def done(self, ins):
        ins.then_inc(self.sem, 1)
        self.n += 1

    def wait(self):
        self.eng.wait_ge(self.sem, self.base + self.n)

    def run(self, ins):
        self.done(ins)
        self.wait()

    @contextmanager
    def loop(self, count, per):
        n0, base0 = self.n, self.base
        with self.eng.Fori(0, count) as i:
            self.base = base0 + i * per
            yield i
            assert self.n - n0 == per, (self.n - n0, per)
        self.base = base0
        self.n = n0 + per * count


def load_registers(nc, engine, row, hi):
    _, vals = nc.values_load_multi_w_load_instructions(row, engines=[engine], min_val=0, max_val=hi)
    return vals


def build(nc, x, src, dst, Wl, bl, Wr, ln_w, ln_b, W1g, b1g, Wq, Wk, Wv, Wo, bo, bn1_g, bn1_b,
          bn2_g, bn2_b, W1, b1, W2, b2, W3g, b3g, out):
    ET = mybir.EngineType
    V, S, G, T = nc.vector, nc.scalar, nc.gpsimd, nc.tensor
    dram = lambda name, shape, dt: nc.dram_tensor(name, shape, dt, kind="Internal").ap()
    build_table_d = dram("build_table_d", (BW, 4), i32)
    key_d = dram("key_d", (LANES, CHP), fp32)
    sl_d = dram("sl_d", (LANES, CHP), fp32)
    wt_d = dram("wt_d", (C, 10, C), fp32)
    srcidx_d = dram("srcidx_d", (LANES, CHP), i32)
    dstf_d = dram("dstf_d", (LANES, CHP), fp32)
    reldst_d = dram("reldst_d", (LANES, CHP), fp32)
    win_table_d = dram("win_table_d", (1, 128), i32)
    kv_d = dram("kv_d", (N, 2 * C), fp32)
    q_d = dram("q_d", (N, C), fp32)
    counts_d = dram("counts_d", (TILE, (NT - SPILL) * N), fp16)

    ctx = ExitStack()
    with ctx:
        def sb(name, shape, dt, scope=ctx):
            return scope.enter_context(nc.sbuf_tensor(name, shape, dt))

        def sem(name):
            return ctx.enter_context(nc.semaphore(name))

        ps = [ctx.enter_context(nc.psum_tensor(f"bank{i}", [128, 512], fp32)) for i in range(8)]

        ident = sb("ident", [128, 128], fp32)
        alpha = sb("alpha", [128, 8], fp32)
        inv_alpha = sb("inv_alpha", [128, 8], fp32)
        ident_a = sb("ident_a", [128, 5, TILE], bf16)
        eps_t = sb("eps_t", [128, 1], fp32)
        ones_row = sb("ones_row", [1, TILE], fp32)
        has_edge = sb("has_edge", [TILE, NT], fp32)
        parts_all = [sb(f"parts{i}", [128, NT, 2, C], fp16) for i in range(2)]  
        parts = [p[0:TILE] for p in parts_all]

        s1 = ExitStack()
        with s1:
            t = lambda name, shape, dt: sb(name, shape, dt, s1)
            src_rows = t("src_rows", [ROWS, ROWG, LANES], i32)
            dst_rows = t("dst_rows", [ROWS, ROWG, LANES], i32)
            src_rf = t("src_rf", [ROWS, ROWG, LANES], fp32)
            dst_rf = t("dst_rf", [ROWS, ROWG, LANES], fp32)
            real = t("real", [ROWS, ROWG, LANES], fp32)
            mm = t("mm", [ROWS, 2, ROWG], fp32)
            diag = t("diag", [ROWS, 2, ROWG, ROWS], fp32)
            ones = t("ones", [128, 128], fp32)
            iota_f = t("iota_f", [128, 128], fp32)
            iota_p = t("iota_p", [128, 1], fp32)
            iota_c1 = t("iota_c1", [128, CH], fp32)
            tri = t("tri", [128, 128], fp32)
            win = t("win", [128, 2], fp32)
            hit1 = t("hit1", [128, CH], fp32)
            hit = t("hit", [128, CH], fp32)
            cand = t("cand", [128, CH], fp32)
            cand2 = t("cand2", [128, CH], fp32)
            lohi = t("lohi", [128, 8], fp32)
            ng_i = t("ng_i", [128, 2], i32)
            tab_i = t("tab_i", [128, 4], i32)
            srcN = t("srcN", [LANES, CHP], fp32)
            dstN = t("dstN", [LANES, CHP], fp32)
            src_i = t("src_i", [LANES, CHP], i32)
            shi = t("shi", [LANES, CHP], i32)
            shf = t("shf", [LANES, CHP], fp32)
            fix = t("fix", [LANES, CHP], fp32)
            slN0 = t("slN0", [LANES, CHP], fp32)
            keyN0 = t("keyN0", [LANES, CHP], fp32)
            w_raw = t("w_raw", [128, 10, C], fp32)
            lnw_all = t("lnw_all", [128, 4, C], fp32)
            lnb_all = t("lnb_all", [128, 4, C], fp32)
            xf = t("xf", [TILE, NT, C], fp32)
            gmm = t("gmm", [128, 2, NG], fp32)
            gq = t("gq", [128, 2, NG], fp32)
            gqi = t("gqi", [128, 2, NG], i32)
            gr = t("gr", [128, 2, NG], fp32)
            gf = t("gf", [128, 2, NG], fp32)
            w0_i = t("w0_i", [128, 128], i32)
            w0_f = t("w0_f", [128, 128], fp32)
            reldst = t("reldst", [LANES, CHP], fp32)
            absmax = t("absmax", [128, 16], fp32)
            absmax_r = t("absmax_r", [128, 16], fp32)
            bound = t("bound", [128, 8], fp32)
            WT = t("WT", [128, 10, C], fp32)

            rows_cleared = sem("rows_cleared")
            edges_in = sem("edges_in")
            x_in = sem("x_in")
            w_in = sem("w_in")
            consts_ready = sem("consts_ready")
            setup_step = sem("setup_step")
            edges_f = sem("edges_f")
            edges_t = sem("edges_t")
            diag_ready = sem("diag_ready")
            minmax_bc = sem("minmax_bc")
            ng_ready = sem("ng_ready")
            base_ready = sem("base_ready")
            wt_done = sem("wt_done")
            wt_copied = sem("wt_copied")
            absmax_ready = sem("absmax_ready")
            absmax_all = sem("absmax_all")
            alpha_ready = sem("alpha_ready")
            pool_step = sem("pool_step")
            setup_out = sem("setup_out")
            keys_ready = sem("keys_ready")
            table_ready = sem("table_ready")
            windows_ready = sem("windows_ready")
            table_out = sem("table_out")

            with nc.Block() as block:
                @block.sync
                def _(sp):
                    sp.wait_ge(rows_cleared, 1)
                    for rows, arr in ((dst_rows, dst), (src_rows, src)):
                        n3 = (ROWG - 1) * ROWS * LANES
                        sp.dma_start(rows[:, 0:ROWG - 1, :],
                                     arr[0:n3].rearrange("(t r p) -> r t p", r=ROWS, p=LANES)).then_inc(edges_in, 16)
                        full = (E - n3) // LANES
                        sp.dma_start(rows[0:full, ROWG - 1, :],
                                     arr[n3:n3 + full * LANES].rearrange("(r p) -> r p", p=LANES)).then_inc(edges_in, 16)
                        rest = E - n3 - full * LANES
                        sp.dma_start(rows[full:full + 1, ROWG - 1, 0:rest],
                                     arr[E - rest:E].unsqueeze(0)).then_inc(edges_in, 16)
                    sp.dma_start(xf[:, :, :], x.rearrange("(t p) c -> p t c", p=TILE)).then_inc(x_in, 16)
                    sp.wait_ge(keys_ready, 1)
                    sp.dma_start(key_d, keyN0[:, :]).then_inc(setup_out, 16)
                    sp.dma_start(sl_d, slN0[:, :]).then_inc(setup_out, 16)
                    sp.dma_start(srcidx_d, src_i[:, :]).then_inc(setup_out, 16)
                    sp.dma_start(dstf_d, dstN[:, :]).then_inc(setup_out, 16)
                    sp.wait_ge(table_ready, 1)
                    sp.dma_start(build_table_d, tab_i[0:BW, :]).then_inc(table_out, 16)
                    sp.wait_ge(windows_ready, 1)
                    sp.dma_start(reldst_d, reldst[:, :]).then_inc(setup_out, 16)
                    sp.dma_start(win_table_d, w0_i[0:1, :]).then_inc(setup_out, 16)
                    sp.wait_ge(wt_copied, 3)
                    sp.dma_start(wt_d, WT[:, :, :]).then_inc(setup_out, 16)
                    sp.wait_ge(table_out, 16)
                    sp.wait_ge(setup_out, 112)

                @block.scalar
                def _(act):
                    act.dma_start(w_raw[:, 0:4, :], Wl.rearrange("l o c -> o l c")).then_inc(w_in, 16)
                    act.dma_start(w_raw[:, 4:8, :], Wr.rearrange("l o c -> o l c")).then_inc(w_in, 16)
                    act.dma_start(w_raw[:, 8, :], W1g).then_inc(w_in, 16)
                    act.dma_start(w_raw[:, 9, :], W3g).then_inc(w_in, 16)
                    act.dma_start(lnw_all[:, :, :].rearrange("p l c -> p (l c)"),
                                  ln_w.rearrange("l c -> (l c)").unsqueeze(0).to_broadcast([128, 4 * C])).then_inc(w_in, 16)
                    act.dma_start(lnb_all[:, :, :].rearrange("p l c -> p (l c)"),
                                  ln_b.rearrange("l c -> (l c)").unsqueeze(0).to_broadcast([128, 4 * C])).then_inc(w_in, 16)
                    for j in range(3):
                        k = min(4, 10 - 4 * j)
                        act.wait_ge(wt_done, j + 1)
                        S.copy(WT[:, 4 * j:4 * j + k, :].rearrange("p w c -> p (w c)"), ps[j][:, 0:k * C]).then_inc(wt_copied, 1)
                    act.wait_ge(w_in, 16 * 6)

                @block.gpsimd
                def _(pool):
                    iota = lambda o, pat, b, cm: G.iota(o, pattern=pat, base=b, channel_multiplier=cm,
                                                        allow_small_or_imprecise_dtypes=True)
                    iota(iota_f[:, :], [[1, 128]], 0, 0).then_inc(consts_ready, 1)
                    iota(iota_p[:, :], [[0, 1]], 0, 1).then_inc(consts_ready, 1)
                    iota(iota_c1[:, :], [[1, CH]], 1, 0).then_inc(consts_ready, 1)
                    pool.wait_ge(absmax_ready, 1)
                    G.partition_all_reduce(absmax_r[:, :], absmax[:, :], 128,
                                           bass.bass_isa.ReduceOp.absmax).then_inc(absmax_all, 1)
                    st = Steps(pool, pool_step)
                    pool.wait_ge(alpha_ready, 1)
                    pool.wait_ge(x_in, 16)
                    st.run(G.tensor_scalar(xf[:, :, :], xf[:, :, :], alpha[0:TILE, 0:1], None, ALU.mult))
                    st.run(G.tensor_copy(parts[0][:, :, 0, :], xf[:, :, :]))
                    st.run(G.tensor_tensor(parts[0][:, :, 1, :], xf[:, :, :], parts[0][:, :, 0, :], ALU.subtract))

                @block.vector
                def _(dve):
                    st = Steps(dve, setup_step)
                    st.done(V.memset(src_rows[:, :, :], 0))
                    st.done(V.memset(absmax[:, :], 0.0))
                    V.memset(dst_rows[:, :, :], int(NO_NODE)).then_inc(rows_cleared, 1)
                    st.done(V.memset(ones[:, :], 1.0))
                    st.done(V.memset(ones_row[:, :], 1.0))
                    st.done(V.memset(eps_t[:, :], EPS))
                    st.done(V.memset(srcN[:, :], 0.0))
                    st.done(V.memset(dstN[:, :], NO_NODE))
                    dve.wait_ge(consts_ready, 3)
                    st.done(V.tensor_scalar(ident[:, :], iota_f[:, :], iota_p[:, 0:1], None, ALU.is_equal))
                    st.done(V.tensor_scalar(tri[:, :], iota_f[:, :], iota_p[:, 0:1], None, ALU.is_gt))
                    st.done(V.tensor_scalar(win[:, 0:1], iota_p[:, :], float(BWN), None, ALU.mult))
                    st.done(V.tensor_scalar(win[:, 1:2], iota_p[:, :], float(BWN), float(BWN), ALU.mult, ALU.add))
                    st.wait()
                    dve.wait_ge(edges_in, 16 * 6)
                    st.done(V.tensor_copy(dst_rf[:, :, :], dst_rows[:, :, :]))
                    st.wait()
                    V.tensor_copy(src_rf[:, :, :], src_rows[:, :, :]).then_inc(edges_f, 1)
                    st.done(V.tensor_reduce(out=mm[:, 0, :], in_=dst_rf[:, :, :], axis=AX.X, op=ALU.min))
                    st.run(V.scalar_tensor_tensor(real[:, :, :], dst_rf[:, :, :], NO_NODE - 1, dst_rf[:, :, :],
                                                  ALU.is_lt, ALU.mult))
                    st.run(V.tensor_reduce(out=mm[:, 1, :], in_=real[:, :, :], axis=AX.X, op=ALU.max))
                    for m in range(2):
                        for g in range(ROWG):
                            last = V.tensor_scalar(diag[:, m, g, :], ident[0:ROWS, 0:ROWS], mm[:, m, g:g + 1], None, ALU.mult)
                            if (m, g) == (1, ROWG - 1):
                                last.then_inc(diag_ready, 1)
                    dve.wait_ge(edges_t, 2)
                    st.done(V.tensor_copy(dstN[:, 0:CH], ps[4][:, 0:CH]))
                    st.run(V.tensor_copy(srcN[:, 0:CH], ps[5][:, 0:CH]))
                    st.done(V.tensor_copy(src_i[:, :], srcN[:, :]))
                    st.run(V.tensor_scalar(fix[:, :], srcN[:, :], 1.0 / TILE, None, ALU.mult))
                    st.run(V.tensor_copy(shi[:, :], fix[:, :]))
                    st.run(V.tensor_copy(shf[:, :], shi[:, :]))
                    st.run(V.scalar_tensor_tensor(slN0[:, :], shf[:, :], -float(TILE), srcN[:, :], ALU.mult, ALU.add))
                    st.run(V.tensor_scalar(fix[:, :], slN0[:, :], 0.0, None, ALU.is_lt))
                    st.run(V.tensor_tensor(shf[:, :], shf[:, :], fix[:, :], ALU.subtract))
                    st.run(V.tensor_scalar(fix[:, :], slN0[:, :], float(TILE), None, ALU.is_ge))
                    st.run(V.tensor_tensor(shf[:, :], shf[:, :], fix[:, :], ALU.add))
                    st.run(V.scalar_tensor_tensor(slN0[:, :], shf[:, :], -float(TILE), srcN[:, :], ALU.mult, ALU.add))
                    V.scalar_tensor_tensor(keyN0[:, :], dstN[:, :], float(NT), shf[:, :], ALU.mult, ALU.add).then_inc(keys_ready, 1)
                    dve.wait_ge(minmax_bc, 2)
                    st.run(V.tensor_scalar(hit1[:, :], ps[7][:, 0:CH], win[:, 0:1], None, ALU.is_ge))
                    st.run(V.scalar_tensor_tensor(hit[:, :], ps[6][:, 0:CH], win[:, 1:2], hit1[:, :], ALU.is_lt, ALU.mult))
                    st.done(V.tensor_tensor(cand[:, :], hit[:, :], iota_c1[:, :], ALU.mult))
                    st.run(V.scalar_tensor_tensor(cand2[:, :], hit[:, :], -1.0e6, iota_c1[:, :], ALU.mult, ALU.add))
                    st.done(V.tensor_reduce(out=lohi[:, 1:2], in_=cand[:, :], axis=AX.X, op=ALU.max))
                    st.run(V.tensor_reduce(out=lohi[:, 0:1], in_=cand2[:, :], axis=AX.X, op=ALU.min))
                    st.run(V.tensor_scalar(lohi[:, 0:1], lohi[:, 0:1], 1.0e6 - 1.0, float(CH - 1), ALU.add, ALU.min))
                    st.run(V.tensor_tensor(lohi[:, 2:3], lohi[:, 1:2], lohi[:, 0:1], ALU.subtract))
                    st.run(V.tensor_scalar(lohi[:, 2:3], lohi[:, 2:3], 1.0, float(BK - 1), ALU.max, ALU.add))
                    st.run(V.tensor_scalar(lohi[:, 3:4], lohi[:, 2:3], 205.0, None, ALU.mult))
                    st.run(V.tensor_copy(ng_i[:, 0:1], lohi[:, 3:4]))
                    st.run(V.tensor_scalar(ng_i[:, 1:2], ng_i[:, 0:1], 10, None, ALU.logical_shift_right))
                    V.tensor_copy(lohi[:, 4:5], ng_i[:, 1:2]).then_inc(ng_ready, 1)
                    dve.wait_ge(base_ready, 1)
                    dve.wait_ge(ng_ready, 1)
                    st.run(V.tensor_copy(lohi[:, 5:6], ps[3][:, 0:1]))
                    st.done(V.tensor_tensor(lohi[:, 6:7], lohi[:, 5:6], lohi[:, 4:5], ALU.add))
                    st.run(V.scalar_tensor_tensor(lohi[:, 7:8], lohi[:, 5:6], -float(BK), lohi[:, 0:1], ALU.mult, ALU.add))
                    st.run(V.tensor_scalar(lohi[:, 4:5], lohi[:, 7:8], float(CHUNK_OFF), None, ALU.add))
                    st.done(V.memset(tab_i[:, 3:4], 0))
                    V.tensor_copy(tab_i[:, 0:3], lohi[:, 4:7]).then_inc(table_ready, 1)
                    st.done(V.tensor_reduce(out=gmm[:, 0, :], in_=ps[6][:, 0:CH].rearrange("p (g k) -> p g k", k=GRP),
                                            axis=AX.X, op=ALU.min))
                    st.run(V.tensor_reduce(out=gmm[:, 1, :], in_=ps[7][:, 0:CH].rearrange("p (g k) -> p g k", k=GRP),
                                           axis=AX.X, op=ALU.max))
                    st.run(V.tensor_scalar(gr[:, :, :], gmm[:, :, :], 1.0 / TILE, None, ALU.mult))
                    st.run(V.tensor_copy(gqi[:, :, :], gr[:, :, :]))
                    st.run(V.tensor_copy(gq[:, :, :], gqi[:, :, :]))
                    st.run(V.scalar_tensor_tensor(gr[:, :, :], gq[:, :, :], -float(TILE), gmm[:, :, :], ALU.mult, ALU.add))
                    st.run(V.tensor_scalar(gf[:, :, :], gr[:, :, :], 0.0, None, ALU.is_lt))
                    st.run(V.tensor_tensor(gq[:, :, :], gq[:, :, :], gf[:, :, :], ALU.subtract))
                    st.run(V.tensor_scalar(gf[:, :, :], gr[:, :, :], float(TILE), None, ALU.is_ge))
                    st.run(V.tensor_tensor(gq[:, :, :], gq[:, :, :], gf[:, :, :], ALU.add))
                    st.run(V.memset(w0_f[:, :], 0.0))
                    st.done(V.tensor_copy(w0_f[:, 2:2 + NG], gq[:, 0, :]))
                    st.run(V.tensor_tensor(gf[:, 0, :], gq[:, 1, :], gq[:, 0, :], ALU.subtract))
                    st.run(V.tensor_reduce(out=w0_f[:, 127:128], in_=gf[:, 0, :], axis=AX.X, op=ALU.max))
                    st.done(V.tensor_copy(w0_i[:, :], w0_f[:, :]))
                    st.run(V.memset(reldst[:, :], NO_NODE))
                    V.scalar_tensor_tensor(reldst[:, 0:CH].rearrange("p (g k) -> p g k", k=GRP),
                                           gq[:, 0, :].unsqueeze(2).to_broadcast([LANES, NG, GRP]), -float(TILE),
                                           dstN[:, 0:CH].rearrange("p (g k) -> p g k", k=GRP),
                                           ALU.mult, ALU.add).then_inc(windows_ready, 1)
                    dve.wait_ge(x_in, 16)
                    dve.wait_ge(w_in, 16 * 6)
                    st.run(V.tensor_reduce(out=absmax[0:TILE, 0:1], in_=xf[:, :, :], axis=AX.XY, op=ALU.max,
                                           apply_absolute_value=True))
                    for l in range(3):
                        st.done(V.tensor_reduce(out=bound[:, l:l + 1], in_=lnw_all[:, l, :], axis=AX.X, op=ALU.max,
                                                apply_absolute_value=True))
                        st.run(V.tensor_reduce(out=bound[:, 4 + l:5 + l], in_=lnb_all[:, l, :], axis=AX.X, op=ALU.max,
                                               apply_absolute_value=True))
                        if l == 0:
                            V.tensor_copy(absmax[:, 1:2], absmax[:, 0:1]).then_inc(absmax_ready, 1)
                    st.run(V.tensor_scalar(cand[:, 0:3], bound[:, 0:3], LN_BOUND, None, ALU.mult))
                    st.run(V.tensor_tensor(cand[:, 4:7], cand[:, 0:3], bound[:, 4:7], ALU.add))
                    st.run(V.tensor_copy(bound[:, 1:4], cand[:, 4:7]))
                    dve.wait_ge(absmax_all, 1)
                    st.run(V.tensor_copy(bound[:, 0:1], absmax_r[:, 0:1]))
                    st.run(V.tensor_scalar(bound[:, 0:4], bound[:, 0:4], 1e-30, None, ALU.max))
                    st.run(V.tensor_scalar(bound[:, 0:4].bitcast(i32), bound[:, 0:4].bitcast(i32), 0x7F800000, None, ALU.bitwise_and))
                    st.done(V.tensor_scalar(inv_alpha[:, 0:4], bound[:, 0:4], 2.0 ** -13, None, ALU.mult))
                    st.done(V.memset(inv_alpha[:, 4:8], 1.0 / ALPHA_LN))
                    st.wait()
                    st.run(V.reciprocal(alpha[:, :], inv_alpha[:, :]))
                    for l in range(5):
                        last = V.tensor_scalar(ident_a[:, l, :], ident[:, 0:TILE], inv_alpha[:, l:l + 1], None, ALU.mult)
                    last.then_inc(alpha_ready, 1)

                @block.tensor
                def _(pe):
                    pe.wait_ge(w_in, 16 * 6)
                    pe.wait_ge(setup_step, 12)
                    for j in range(3):
                        for k in range(min(4, 10 - 4 * j)):
                            last = T.transpose(ps[j][:, k * C:(k + 1) * C], w_raw[:, 4 * j + k, :], ident[:, :])
                        last.then_inc(wt_done, 1)
                    pe.wait_ge(edges_f, 1)
                    for p, rows in ((4, dst_rf), (5, src_rf)):
                        for g in range(ROWG):
                            last = T.transpose(ps[p][:, g * ROWS:(g + 1) * ROWS], rows[:, g, :], ident[0:ROWS, 0:ROWS])
                        last.then_inc(edges_t, 1)
                    pe.wait_ge(diag_ready, 1)
                    for m in range(2):
                        for g in range(ROWG):
                            last = T.matmul(ps[6 + m][:, g * ROWS:(g + 1) * ROWS], ones[0:ROWS, :], diag[:, m, g, :],
                                            start=True, stop=True)
                        last.then_inc(minmax_bc, 1)
                    pe.wait_ge(ng_ready, 1)
                    pe.wait_ge(wt_copied, 3)
                    T.matmul(ps[3][0:128, 0:1], tri[0:128, 0:128], lohi[0:128, 4:5], start=True, stop=True).then_inc(base_ready, 1)

        counts_all = sb("counts_all", [128, NT * N + 3], fp16)
        counts = counts_all[0:TILE, 0:NT * N].rearrange("p (s d) -> p s d", s=NT)
        s2 = ExitStack()
        with s2:
            t = lambda name, shape, dt: sb(name, shape, dt, s2)
            keyN = t("keyN", [LANES, CHP], fp32)
            slN = t("slN", [LANES, CHP], fp32)
            iota_k = t("iota_k", [LANES, BKEYS], fp16)
            win_off = t("win_off", [LANES, BW], fp32)
            rel_key = t("rel_key", [LANES, BK], fp32)
            rel_sl = t("rel_sl", [LANES, BK], fp32)
            oh_key = t("oh_key", [LANES, BK, BKEYS + 1], fp16)
            oh_sl = t("oh_sl", [LANES, BK, TILE + 1], fp16)
            zeros = t("zeros", [LANES, TILE], fp16)
            table = t("table", [1, BW * 4], i32)

            keys_in = sem("keys_in")
            build_consts = sem("build_consts")
            rel_ready = sem("rel_ready")
            pair_ready = sem("pair_ready")
            pair_free = sem("pair_free")
            window_done = sem("window_done")
            window_free = sem("window_free")

            with nc.Block() as block:
                @block.sync
                def _(sp):
                    sp.dma_start(keyN[:, :], key_d).then_inc(keys_in, 16)
                    sp.dma_start(slN[:, :], sl_d).then_inc(keys_in, 16)
                    sp.dma_start(table[0:1, :], build_table_d.rearrange("w f -> (w f)").unsqueeze(0)).then_inc(keys_in, 16)

                @block.gpsimd
                def _(pool):
                    G.iota(iota_k[:, :], pattern=[[1, BKEYS]], base=0, channel_multiplier=0,
                           allow_small_or_imprecise_dtypes=True).then_inc(build_consts, 1)
                    G.iota(win_off[:, :], pattern=[[-BKEYS, BW]], base=0, channel_multiplier=0,
                           allow_small_or_imprecise_dtypes=True).then_inc(build_consts, 1)

                @block.vector
                def _(dve):
                    V.memset(zeros[:, :], 0.0).then_inc(build_consts, 1)
                    dve.wait_ge(build_consts, 3)
                    dve.wait_ge(keys_in, 48)
                    with dve.Fori(0, BW) as w:
                        off, first, end, _z = load_registers(nc, ET.DVE, table[0:1, bass.ds(w * 4, 4)], 2 * CHUNK_OFF)
                        with dve.Fori(first, end) as i:
                            chunk = nc.s_assert_within(off + i * BK - CHUNK_OFF, 0, CHP - BK)
                            dve.wait_ge(pair_ready, i * BK)
                            V.tensor_scalar(rel_key[:, :], keyN[:, bass.ds(chunk, BK)], win_off[:, bass.ds(w, 1)], None,
                                            ALU.add).then_inc(rel_ready, 1)
                            V.tensor_copy(rel_sl[:, :], slN[:, bass.ds(chunk, BK)]).then_inc(rel_ready, 1)
                            dve.wait_ge(rel_ready, i * 2 + 2)
                            for k in range(BK):
                                dve.wait_ge(pair_free, i * BK + k + 1)
                                V.tensor_scalar(oh_sl[:, k, 0:TILE], iota_k[:, 0:TILE], rel_sl[:, k:k + 1], None, ALU.is_equal)
                                V.tensor_scalar(oh_key[:, k, 0:BKEYS], iota_k[:, :], rel_key[:, k:k + 1], None,
                                                ALU.is_equal).then_inc(pair_ready, 1)

                @block.tensor
                def _(pe):
                    pe.sem_inc(pair_free, BK)
                    pe.wait_ge(build_consts, 3)
                    pe.wait_ge(keys_in, 48)

                    def window(w, slot):
                        a, b = ps[2 * slot], ps[2 * slot + 1]
                        _o, first, end, _z = load_registers(nc, ET.PE, table[0:1, bass.ds(w * 4, 4)], 2 * CHUNK_OFF)
                        pe.wait_ge(window_free, w + 1)
                        T.matmul(a[0:TILE, 0:BHALF], zeros[:, :], iota_k[:, 0:BHALF], start=True, stop=False, skip_group_check=True)
                        T.matmul(b[0:TILE, 0:BKEYS - BHALF], zeros[:, :], iota_k[:, BHALF:BKEYS], start=True, stop=False,
                                 skip_group_check=True)
                        with pe.Fori(first, end) as i:
                            for k in range(BK):
                                pe.wait_ge(pair_ready, i * BK + k + 1)
                                T.matmul(a[0:TILE, 0:BHALF], oh_sl[:, k, 0:TILE], oh_key[:, k, 0:BHALF], start=False, stop=False,
                                         skip_group_check=True)
                                T.matmul(b[0:TILE, 0:BKEYS - BHALF], oh_sl[:, k, 0:TILE], oh_key[:, k, BHALF:BKEYS], start=False,
                                         stop=False, skip_group_check=True).then_inc(pair_free, 1)
                        T.matmul(a[0:TILE, 0:2], zeros[:, :], iota_k[:, 0:2], start=False, stop=True, skip_group_check=True)
                        T.matmul(b[0:TILE, 0:2], zeros[:, :], iota_k[:, 0:2], start=False, stop=True,
                                 skip_group_check=True).then_inc(window_done, 1)

                    with pe.Fori(0, BW // 2) as j:
                        window(j * 2, 0)
                        window(j * 2 + 1, 1)
                    window(BW - 1, 0)

                @block.scalar
                def _(act):
                    act.sem_inc(window_free, 2)

                    def evacuate(w, slot):
                        a, b = ps[2 * slot], ps[2 * slot + 1]
                        h = BHALF // NT
                        act.wait_ge(window_done, w + 1)
                        S.copy(counts[:, :, bass.ds(w * BWN, h)].rearrange("p s d -> p d s"),
                               a[0:TILE, 0:BHALF].rearrange("p (d s) -> p d s", s=NT))
                        S.copy(counts[:, :, bass.ds(w * BWN + h, BWN - h)].rearrange("p s d -> p d s"),
                               b[0:TILE, 0:BKEYS - BHALF].rearrange("p (d s) -> p d s", s=NT)).then_inc(window_free, 1)

                    with act.Fori(0, BW // 2) as j:
                        evacuate(j * 2, 0)
                        evacuate(j * 2 + 1, 1)
                    evacuate(BW - 1, 0)

        inv_deg = sb("inv_deg", [128, N], fp32)
        counts_saved = sem("counts_saved")
        s3 = ExitStack()
        with s3:
            ones_h = sb("ones_h", [TILE, 128], fp16, s3)
            deg_row = sb("deg_row", [1, BLK], fp32, s3)
            deg_ones = sem("deg_ones")
            deg_done = sem("deg_done")
            deg_row_ready = sem("deg_row_ready")
            deg_cols = sem("deg_cols")
            deg_step = sem("deg_step")
            with nc.Block() as block:
                @block.sync
                def _(sp):
                    sp.dma_start(counts_d, counts_all[0:TILE, SPILL * N:NT * N]).then_inc(counts_saved, 16)

                def deg_blocks():
                    for b in range(NBLK + 1):
                        yield b, b * BLK, min(BLK, N - b * BLK)

                @block.tensor
                def _(pe):
                    pe.wait_ge(deg_ones, 1)
                    for b, d0, w in deg_blocks():
                        if b >= 2:
                            pe.wait_ge(deg_row_ready, b - 1)
                        for s in range(NT):
                            last = T.matmul(ps[b % 2][:, 0:w], ones_h[:, :], counts[:, s, d0:d0 + w],
                                            start=(s == 0), stop=(s == NT - 1))
                        last.then_inc(deg_done, 1)
                        pe.wait_ge(deg_row_ready, b + 1)
                        for j in range(w // TILE):
                            tile = (d0 // TILE) + j
                            last = T.matmul(ps[2][0:TILE, tile:tile + 1], deg_row[0:1, j * TILE:(j + 1) * TILE],
                                            ones_row[0:1, 0:1], start=True, stop=True)
                        last.then_inc(deg_cols, 1)

                @block.vector
                def _(dve):
                    V.memset(ones_h[:, :], 1.0).then_inc(deg_ones, 1)
                    st = Steps(dve, deg_step)
                    for b, d0, w in deg_blocks():
                        dve.wait_ge(deg_done, b + 1)
                        if b:
                            dve.wait_ge(deg_cols, b)
                        st.run(V.tensor_scalar(inv_deg[:, d0:d0 + w], ps[b % 2][:, 0:w], 1.0, None, ALU.max))
                        V.tensor_copy(deg_row[0:1, 0:w], ps[b % 2][0:1, 0:w]).then_inc(deg_row_ready, 1)
                        st.done(V.reciprocal(inv_deg[:, d0:d0 + w], inv_deg[:, d0:d0 + w]))
                    dve.wait_ge(deg_cols, NBLK + 1)
                    st.run(V.tensor_scalar(has_edge[:, :], ps[2][0:TILE, 0:NT], 1.0, None, ALU.min))

        PER = {
            "sage": dict(agg_done=1, agg_scaled=1, xt_done=1, xt_copied=1, y_done=1, y_free=1, stats_ready=1,
                         std_ready=1, z_ready=1, relu_ready=1, parts_ready=1, ln_step=3 + 0, x0_in=0, out_done=0),
            "sage_res": dict(agg_done=1, agg_scaled=1, xt_done=1, xt_copied=1, y_done=1, y_free=1, stats_ready=2,
                             std_ready=2, z_ready=2, relu_ready=2, parts_ready=1, ln_step=6, x0_in=16, out_done=0),
            "message": dict(agg_done=1, agg_scaled=1, xt_done=0, xt_copied=0, y_done=1, y_free=1, stats_ready=1,
                            std_ready=1, z_ready=2, relu_ready=2, parts_ready=1, ln_step=4, x0_in=0, out_done=0),
            "final": dict(agg_done=1, agg_scaled=1, xt_done=1, xt_copied=1, y_done=1, y_free=1, stats_ready=1,
                          std_ready=1, z_ready=1, relu_ready=1, parts_ready=0, ln_step=4, x0_in=0, out_done=16),
        }
        KINDS = ["sage", "sage", "sage", "sage_res", "message", "final"]
        PIN = [0, 1, 0, 1, 0, 1]
        W_AGG = [0, 1, 2, 3, 8, 9]
        W_SELF = [4, 5, 6, 7, None, 9]
        SEMS = {name: sem(name) for name in PER["sage"]}

        def at(name, l, b, k=0):
            before = sum((NBLK + 1) * PER[KINDS[m]][name] for m in range(l))
            return before + k + b * PER[KINDS[l]][name]

        def over_blocks(eng, body):
            with eng.Fori(0, NBLK) as b:
                body(b, BLK // TILE)
            body(NBLK, (N - NBLK * BLK) // TILE)

        def layers(ls):
            sl = ExitStack()
            with sl:
                t = lambda name, shape, dt: sb(name, shape, dt, sl)
                tag = f"_{ls[0]}"
                q = BLK // TILE
                agg_sb = t("agg_sb" + tag, [C, BLK], fp32)
                xt_sb = t("xt_sb" + tag, [C, BLK], fp32)
                z = t("z" + tag, [TILE, q, C], fp32)
                u = t("u" + tag, [TILE, q, C], fp32)
                stats = t("stats" + tag, [TILE, q, 6], fp32)
                mv = t("mv" + tag, [TILE, q, 2], fp32)
                std = t("std" + tag, [TILE, q], fp32)
                rstd = t("rstd" + tag, [TILE, q], fp32)
                lnw = t("lnw" + tag, [TILE, C], fp32)
                lnb = t("lnb" + tag, [TILE, C], fp32)
                x0 = t("x0" + tag, [TILE, q, C], fp32) if 3 in ls else None
                wt = t("wt" + tag, [C, 2, C], fp32)
                bias = t("bias" + tag, [1, C], fp32)
                layer_in = sem("layer_in" + tag)
                stats_taken = sem("stats_taken" + tag)
                agg_ps, xt_ps, y_ps = ps[0], ps[1], ps[2]
                LOADS = {"sage": 5, "sage_res": 5, "message": 2, "final": 3}
                loaded = lambda l: 16 * sum(LOADS[KINDS[m]] for m in ls if m <= l)
                w_S = lambda name: SEMS[name]

                with nc.Block() as block:
                    @block.tensor
                    def _(pe):
                        def body(l, b, nt):
                            pin, w = parts[PIN[l]], nt * TILE
                            pe.wait_ge(w_S("agg_scaled"), at("agg_scaled", l, b))
                            for s in range(NT):
                                if l > ls[0] and s % q == 0:
                                    pe.wait_ge(w_S("parts_ready"), at("parts_ready", l - 1, s // q, 1))
                                for part in range(2):
                                    last = T.matmul(agg_ps[:, 0:w], pin[:, s, part, :], counts[:, s, bass.ds(b * BLK, w)],
                                                    start=(s + part == 0), stop=(s + part == NT))
                            last.then_inc(w_S("agg_done"), 1)
                            if W_SELF[l] is not None:
                                pe.wait_ge(w_S("xt_copied"), at("xt_copied", l, b))
                                for j in range(nt):
                                    for part in range(2):
                                        last = T.matmul(xt_ps[:, j * TILE:(j + 1) * TILE], pin[:, b * q + j, part, :],
                                                        ident_a[0:TILE, min(l, 4), :], start=(part == 0), stop=(part == 1))
                                last.then_inc(w_S("xt_done"), 1)
                                pe.wait_ge(w_S("xt_copied"), at("xt_copied", l, b, 1))
                            pe.wait_ge(w_S("agg_scaled"), at("agg_scaled", l, b, 1))
                            pe.wait_ge(w_S("y_free"), at("y_free", l, b))
                            pe.wait_ge(layer_in, loaded(l))
                            for j in range(nt):
                                y = y_ps[0:TILE, j * C:(j + 1) * C]
                                cols = slice(j * TILE, (j + 1) * TILE)
                                last = T.matmul(y, agg_sb[:, cols], wt[:, 0, :], start=True, stop=W_SELF[l] is None)
                                if W_SELF[l] is not None:
                                    T.matmul(y, xt_sb[:, cols], wt[:, 1, :], start=False, stop=False)
                                    last = T.matmul(y, ones_row[0:1, :], bias[0:1, :], start=False, stop=True)
                            last.then_inc(w_S("y_done"), 1)

                        for l in ls:
                            over_blocks(pe, lambda b, nt: body(l, b, nt))

                    @block.scalar
                    def _(act):
                        def body(l, b, nt):
                            pout, w, kind = parts[1 - PIN[l]], nt * TILE, KINDS[l]
                            tiles = bass.ds(b * q, nt)
                            z_, u_ = z[:, 0:nt, :], u[:, 0:nt, :]

                            def std_of(k):
                                act.wait_ge(w_S("stats_ready"), at("stats_ready", l, b, k))
                                S.activation(std[:, 0:nt], mv[:, 0:nt, 1], ACT.Sqrt, bias=eps_t[0:TILE, 0:1]).then_inc(w_S("std_ready"), 1)

                            if W_SELF[l] is not None:
                                act.wait_ge(w_S("xt_done"), at("xt_done", l, b, 1))
                                S.copy(xt_sb[:, 0:w], xt_ps[:, 0:w]).then_inc(w_S("xt_copied"), 1)
                            if kind == "sage":
                                std_of(1)
                                act.wait_ge(w_S("z_ready"), at("z_ready", l, b, 1))
                                S.activation(pout[:, tiles, 0, :], z_, ACT.Relu, scale=alpha[0:TILE, l + 1:l + 2])
                                S.activation(u_, z_, ACT.Relu).then_inc(w_S("relu_ready"), 1)
                                return
                            if kind == "sage_res":
                                std_of(1)
                            if kind == "final":
                                act.wait_ge(w_S("y_done"), at("y_done", l, b, 1))
                                S.activation(u_, y_ps[0:TILE, 0:nt * C].rearrange("p (j c) -> p j c", c=C),
                                             ACT.Relu).then_inc(w_S("relu_ready"), 1)
                            else:
                                act.wait_ge(w_S("z_ready"), at("z_ready", l, b, 1))
                                S.activation(u_, z_, ACT.Relu).then_inc(w_S("relu_ready"), 1)
                            std_of(PER[kind]["stats_ready"])
                            if kind != "final":
                                act.wait_ge(w_S("z_ready"), at("z_ready", l, b, 2))
                                S.activation(pout[:, tiles, 0, :], z_, ACT.Copy, scale=ALPHA_LN).then_inc(w_S("relu_ready"), 1)

                        for l in ls:
                            over_blocks(act, lambda b, nt: body(l, b, nt))

                    @block.vector
                    def _(dve):
                        st = Steps(dve, w_S("ln_step"))
                        st.n = at("ln_step", ls[0], 0)

                        def body(l, b, nt):
                            pin, pout, w, kind = parts[PIN[l]], parts[1 - PIN[l]], nt * TILE, KINDS[l]
                            tiles = bass.ds(b * q, nt)
                            z_, u_ = z[:, 0:nt, :], u[:, 0:nt, :]
                            y = lambda j: y_ps[0:TILE, j * C:(j + 1) * C]
                            st.base = b * PER[kind]["ln_step"]

                            def statistics(of, k):
                                for j in range(nt):
                                    last = V.bn_stats(stats[:, j, :], of(j))
                                st.run(last)
                                dve.sem_inc(stats_taken, 1)
                                for j in range(nt):
                                    last = V.bn_aggr(mv[:, j, :], stats[:, j, :])
                                last.then_inc(w_S("stats_ready"), 1)
                                dve.wait_ge(w_S("std_ready"), at("std_ready", l, b, k))
                                st.run(V.reciprocal(rstd[:, 0:nt], std[:, 0:nt]))

                            def normalize(of):
                                for j in range(nt):
                                    last = V.tensor_scalar(z[:, j, :], of(j), mv[:, j, 0:1], rstd[:, j:j + 1], ALU.subtract, ALU.mult)
                                return last

                            dve.wait_ge(w_S("agg_done"), at("agg_done", l, b, 1))
                            V.scalar_tensor_tensor(agg_sb[:, 0:w], agg_ps[:, 0:w], inv_alpha[:, l:l + 1],
                                                   inv_deg[:, bass.ds(b * BLK, w)], ALU.mult, ALU.mult).then_inc(w_S("agg_scaled"), 1)
                            if kind != "final":
                                dve.wait_ge(w_S("y_done"), at("y_done", l, b, 1))
                            if kind in ("sage", "sage_res"):
                                statistics(y, 1)
                                normalize(y).then_inc(w_S("y_free"), 1)
                                dve.wait_ge(w_S("y_free"), at("y_free", l, b, 1))
                                st.run(V.tensor_tensor(z_, z_, lnw[:, :].unsqueeze(1).to_broadcast([TILE, nt, C]), ALU.mult))
                                V.tensor_tensor(z_, z_, lnb[:, :].unsqueeze(1).to_broadcast([TILE, nt, C]), ALU.add).then_inc(w_S("z_ready"), 1)
                            if kind == "sage":
                                dve.wait_ge(w_S("relu_ready"), at("relu_ready", l, b, 1))
                                V.scalar_tensor_tensor(pout[:, tiles, 1, :], u_, alpha[0:TILE, l + 1:l + 2], pout[:, tiles, 0, :],
                                                       ALU.mult, ALU.subtract).then_inc(w_S("parts_ready"), 1)
                                return
                            if kind == "sage_res":
                                dve.wait_ge(w_S("x0_in"), at("x0_in", l, b, 16))
                                dve.wait_ge(w_S("relu_ready"), at("relu_ready", l, b, 1))
                                st.run(V.tensor_tensor(u_, u_, x0[:, 0:nt, :], ALU.add))
                            if kind == "message":
                                for j in range(nt):
                                    last = V.scalar_tensor_tensor(z[:, j, :], lnw[:, :], has_edge[:, bass.ds(b * q + j, 1)], y(j),
                                                                  ALU.mult, ALU.add)
                                last.then_inc(w_S("z_ready"), 1)
                                V.memset(stats[:, 0, 0:1], 0.0).then_inc(w_S("y_free"), 1)
                            if kind in ("message", "final"):
                                dve.wait_ge(w_S("relu_ready"), at("relu_ready", l, b, 1))
                                if kind == "final":
                                    V.memset(stats[:, 0, 0:1], 0.0).then_inc(w_S("y_free"), 1)
                                    dve.wait_ge(w_S("out_done"), at("out_done", l, b))
                                st.run(V.tensor_tensor(z_, pin[:, tiles, 0, :], pin[:, tiles, 1, :], ALU.add))
                                st.run(V.scalar_tensor_tensor(u_, z_, 1.0 / ALPHA_LN, u_, ALU.mult, ALU.add))
                            statistics(lambda j: u[:, j, :], PER[kind]["std_ready"])
                            normalize(lambda j: u[:, j, :]).then_inc(w_S("z_ready"), 1)
                            if kind == "final":
                                return
                            dve.wait_ge(w_S("relu_ready"), at("relu_ready", l, b, 2))
                            V.scalar_tensor_tensor(pout[:, tiles, 1, :], z_, ALPHA_LN, pout[:, tiles, 0, :],
                                                   ALU.mult, ALU.subtract).then_inc(w_S("parts_ready"), 1)

                        for n, l in enumerate(ls):
                            dve.wait_ge(layer_in, loaded(l))
                            n0 = st.n
                            per = PER[KINDS[l]]["ln_step"]
                            with dve.Fori(0, NBLK) as b:
                                body(l, b, q)
                                assert st.n - n0 == per, (l, st.n - n0)
                            st.n = n0
                            body(l, NBLK, (N - NBLK * BLK) // TILE)
                            st.n, st.base = n0 + per * (NBLK + 1), 0

                    @block.sync
                    def _(sp):
                        for n, l in enumerate(ls):
                            if l > ls[0]:
                                sp.wait_ge(w_S("parts_ready"), at("parts_ready", l, 0))
                            sp.dma_start(wt[:, 0, :], wt_d[:, W_AGG[l], :]).then_inc(layer_in, 16)
                            if W_SELF[l] is None:
                                sp.dma_start(lnw[:, :], b1g.unsqueeze(0).to_broadcast([TILE, C])).then_inc(layer_in, 16)
                            else:
                                sp.dma_start(wt[:, 1, :], wt_d[:, W_SELF[l], :]).then_inc(layer_in, 16)
                                sp.dma_start(bias[0:1, :], (bl[l, :] if l < 4 else b3g).unsqueeze(0)).then_inc(layer_in, 16)
                            if l < 4:
                                sp.dma_start(lnw[:, :], ln_w[l, :].unsqueeze(0).to_broadcast([TILE, C])).then_inc(layer_in, 16)
                                sp.dma_start(lnb[:, :], ln_b[l, :].unsqueeze(0).to_broadcast([TILE, C])).then_inc(layer_in, 16)
                            if KINDS[l] == "sage_res":
                                def body(b, nt):
                                    sp.wait_ge(w_S("parts_ready"), at("parts_ready", l, b))
                                    sp.dma_start(x0[:, 0:nt, :], x[bass.ds(b * BLK, nt * TILE), :].rearrange("(t p) c -> p t c", p=TILE)
                                                 ).then_inc(w_S("x0_in"), 16)
                                over_blocks(sp, body)
                            if KINDS[l] == "final":
                                def body(b, nt):
                                    sp.wait_ge(w_S("z_ready"), at("z_ready", l, b, 1))
                                    sp.dma_start(out[bass.ds(b * BLK, nt * TILE), :].rearrange("(t p) c -> p t c", p=TILE),
                                                 z[:, 0:nt, :]).then_inc(w_S("out_done"), 16)
                                over_blocks(sp, body)
                                sp.wait_ge(w_S("out_done"), at("out_done", l, NBLK, 16))

        layers([0, 1, 2, 3, 4])

        arena_at = [SPILL * N + 16 - (SPILL * N) % 16]

        def carve(shape, dt=fp32):
            lanes, dims = shape[0], shape[1:]
            n = 2 * int(np.prod(dims))
            view = counts_all[0:lanes, arena_at[0]:arena_at[0] + n].bitcast(dt)
            arena_at[0] += n + (-n) % 16
            assert arena_at[0] <= NT * N + 3
            names = "abcde"[:len(dims)]
            if len(dims) == 1:
                return view
            return view.rearrange(f"p ({' '.join(names)}) -> p {' '.join(names)}", **{k: d for k, d in zip(names, dims)})

        Q = carve([TILE, NT + 1, C])
        acc = carve([TILE, NT + 1, VW])
        arena_mid = arena_at[0]
        x2 = parts[1]

        def transposed(pe, out_ps, tiles, nt):
            for j in range(nt):
                for part in range(2):
                    last = T.matmul(out_ps[:, j * TILE:(j + 1) * TILE], x2[:, tiles + j, part, :], ident_a[0:TILE, 4, :],
                                    start=(part == 0), stop=(part == 1))
            return last

        def blocks():
            for b in range(NBLK + 1):
                yield b, b * BLK, min(BLK, N - b * BLK), b * (BLK // TILE), min(BLK, N - b * BLK) // TILE

        def column(ap):
            return ap.unsqueeze(1)

        s4 = ExitStack()
        with s4:
            wkvq = carve([C, 3, C])
            hn_T = [carve([C, BLK]) for _ in range(2)]
            kv_out = [carve([TILE, 4, 2 * C]) for _ in range(2)]
            bst = carve([C, NBLK + 1, 6])
            bmv = carve([C, 2])
            bcol = carve([C, 8])
            bn_in = sem("bn_in")
            xb_done = sem("xb_done")
            xb_taken = sem("xb_taken")
            bn_step = sem("bn_step")
            bn_var = sem("bn_var")
            bn_std = sem("bn_std")
            bn_ready = sem("bn_ready")
            hn_ready = sem("hn_ready")
            qkv_done = sem("qkv_done")
            kv_copied = sem("kv_copied")
            q_copied = sem("q_copied")
            kv_out_done = [sem("kv_out_done0"), sem("kv_out_done1")]
            q_out_done = sem("q_out_done")
            with nc.Block() as block:
                @block.sync
                def _(sp):
                    sp.wait_ge(counts_saved, 16)
                    for i, w in enumerate((Wk, Wv, Wq)):
                        sp.dma_start(wkvq[:, i, :], w).then_inc(bn_in, 16)
                    sp.dma_start(bcol[:, 0:1], column(bn1_g)).then_inc(bn_in, 16)
                    sp.dma_start(bcol[:, 1:2], column(bn1_b)).then_inc(bn_in, 16)
                    for b, d0, w, t0, nt in blocks():
                        sp.wait_ge(kv_copied, t0 + nt)
                        sp.dma_start(kv_d[d0:d0 + w, :].rearrange("(t p) c -> p t c", p=TILE),
                                     kv_out[b % 2][:, 0:nt, :]).then_inc(kv_out_done[b % 2], 16)
                    sp.wait_ge(q_copied, NT)
                    sp.dma_start(q_d.rearrange("(t p) c -> p t c", p=TILE), Q[:, 0:NT, :]).then_inc(q_out_done, 16)
                    sp.wait_ge(q_out_done, 16)
                    sp.wait_ge(kv_out_done[0], 16 * (NBLK // 2 + 1))
                    sp.wait_ge(kv_out_done[1], 16 * (NBLK // 2))

                @block.tensor
                def _(pe):
                    for b, d0, w, t0, nt in blocks():
                        if b >= 2:
                            pe.wait_ge(xb_taken, b - 1)
                        transposed(pe, ps[b % 2], t0, nt).then_inc(xb_done, 1)
                    for b, d0, w, t0, nt in blocks():
                        pe.wait_ge(xb_taken, NBLK + b)
                        transposed(pe, ps[(NBLK + 1 + b) % 2], t0, nt).then_inc(xb_done, 1)
                        if b == 0:
                            pe.wait_ge(bn_in, 80)
                        pe.wait_ge(hn_ready, b + 1)
                        for j in range(nt):
                            tile = t0 + j
                            hn = hn_T[b % 2][:, j * TILE:(j + 1) * TILE]
                            if tile >= 3:
                                pe.wait_ge(kv_copied, tile - 2)
                                pe.wait_ge(q_copied, tile - 2)
                            T.matmul(ps[2 + tile % 3][0:TILE, 0:2 * C], hn, wkvq[:, 0:2, :].rearrange("p w c -> p (w c)"),
                                     start=True, stop=True)
                            T.matmul(ps[5 + tile % 3][0:TILE, 0:C], hn, wkvq[:, 2, :], start=True, stop=True).then_inc(qkv_done, 1)

                @block.vector
                def _(dve):
                    st = Steps(dve, bn_step)
                    for b, d0, w, t0, nt in blocks():
                        dve.wait_ge(xb_done, b + 1)
                        V.bn_stats(bst[:, b, :], ps[b % 2][:, 0:w]).then_inc(xb_taken, 1)
                    dve.wait_ge(xb_taken, NBLK + 1)
                    V.bn_aggr(bmv[:, :], bst[:, :, :].rearrange("p b s -> p (b s)")).then_inc(bn_var, 1)
                    dve.wait_ge(bn_var, 1)
                    dve.wait_ge(bn_std, 1)
                    dve.wait_ge(bn_in, 80)
                    st.run(V.reciprocal(bcol[:, 3:4], bcol[:, 2:3]))
                    st.run(V.tensor_tensor(bcol[:, 4:5], bcol[:, 3:4], bcol[:, 0:1], ALU.mult))
                    st.run(V.tensor_tensor(bcol[:, 6:7], bmv[:, 0:1], bcol[:, 4:5], ALU.mult))
                    V.tensor_tensor(bcol[:, 5:6], bcol[:, 1:2], bcol[:, 6:7], ALU.subtract).then_inc(bn_ready, 1)
                    V.memset(Q[:, NT, :], 0.0)
                    for b, d0, w, t0, nt in blocks():
                        for j in range(nt):
                            dve.wait_ge(qkv_done, t0 + j + 1)
                            V.tensor_scalar(Q[:, t0 + j, :], ps[5 + (t0 + j) % 3][0:TILE, 0:C], 1.0 / float(np.sqrt(HD)),
                                            None, ALU.mult).then_inc(q_copied, 1)

                @block.scalar
                def _(act):
                    act.wait_ge(bn_var, 1)
                    S.activation(bcol[:, 2:3], bmv[:, 1:2], ACT.Sqrt, bias=eps_t[:, 0:1]).then_inc(bn_std, 1)
                    act.wait_ge(bn_ready, 1)
                    for b, d0, w, t0, nt in blocks():
                        act.wait_ge(xb_done, NBLK + 2 + b)
                        if b >= 2:
                            act.wait_ge(qkv_done, 4 * (b - 1))
                        S.activation(hn_T[b % 2][:, 0:w], ps[(NBLK + 1 + b) % 2][:, 0:w], ACT.Identity,
                                     scale=bcol[:, 4:5], bias=bcol[:, 5:6])
                        S.copy(bcol[:, 7:8], bcol[:, 5:6]).then_inc(hn_ready, 1)
                        act.wait_ge(hn_ready, b + 1)
                        S.copy(bcol[:, 7:8], bcol[:, 5:6]).then_inc(xb_taken, 1)
                        if b >= 2:
                            act.wait_ge(kv_out_done[b % 2], 16 * (b // 2))
                        for j in range(nt):
                            act.wait_ge(qkv_done, t0 + j + 1)
                            S.copy(kv_out[b % 2][:, j, :], ps[2 + (t0 + j) % 3][0:TILE, 0:2 * C]).then_inc(kv_copied, 1)

        arena_at[0] = arena_mid
        s5 = ExitStack()
        with s5:
            t = lambda name, shape, dt: sb(name, shape, dt, s5)
            RING = 4
            kv = carve([LANES, RING, GRP, 2 * C])
            prod = carve([LANES, GRP, C])
            VA = [carve([LANES, GRP, VW]) for _ in range(2)]
            ohT = [carve([TILE, 2, GRP, LANES]) for _ in range(2)]
            oh16 = parts_all[0][:, :, :, :].rearrange("p t h c -> p (t h c)")[:, 0:4 * GRP * 2 * TILE].rearrange(
                "p (r k n) -> p r k n", r=4, k=GRP)
            oh32 = [t(f"oh32_{i}", [LANES, GRP, 2 * TILE], fp32) for i in range(2)]
            iota_n = t("iota_n", [LANES, 2 * TILE], fp16)
            ident_h = t("ident_h", [LANES, LANES], fp16)
            idx = [t(f"idx{i}", [LANES, 4 * GRP], i32) for i in range(2)]
            score = [t(f"score{i}", [LANES, GRP * HEADS], fp32) for i in range(2)]
            wtab = t("wtab", [1, 128], i32)
            srcidx = carve([LANES, CHP], i32)
            reldst = carve([LANES, CHP])
            dst_l = t("dst_l", [LANES, CH], fp32)
            qidx = t("qidx", [LANES, CH], i32)
            qidx_f = t("qidx_f", [LANES, CH], fp32)
            win_start = t("win_start", [LANES, NT], fp32)
            rel_all = t("rel_all", [LANES, NT], fp32)

            att_in = sem("att_in")
            att_consts = sem("att_consts")
            kv_in = [sem(f"kv_in{i}") for i in range(RING)]
            idx_ready = sem("idx_ready")
            pool_waits = sem("pool_waits")
            prod_ready = sem("prod_ready")
            score_sum = sem("score_sum")
            score_ready = sem("score_ready")
            a_ready = sem("a_ready")
            va_ready = sem("va_ready")
            oh_ready = sem("oh_ready")
            tr_done = sem("tr_done")
            ohT_ready = sem("ohT_ready")
            qe_done = sem("qe_done")
            oh32_ready = sem("oh32_ready")
            seg_done = sem("seg_done")
            seg_added = sem("seg_added")
            gen_idx = sem("gen_idx")
            gen_in = sem("gen_in")
            gen_step = sem("gen_step")
            gen_score = sem("gen_score")
            gen_a = sem("gen_a")
            gen_oh = sem("gen_oh")
            gen_seg = sem("gen_seg")
            gen_added = sem("gen_added")

            def windows_spanned(engine):
                return load_registers(nc, engine, wtab[0:1, 124:128], NT)[3]

            with nc.Block() as block:
                @block.sync
                def _(sp):
                    sp.dma_start(wtab[0:1, :], win_table_d).then_inc(att_in, 16)
                    sp.dma_start(srcidx[:, :], srcidx_d).then_inc(att_in, 16)
                    sp.dma_start(reldst[:, :], reldst_d).then_inc(att_in, 16)
                    sp.dma_start(dst_l[:, :], dstf_d[:, 0:CH]).then_inc(att_in, 16)

                @block.gpsimd
                def _(pool):
                    G.iota(iota_n[:, :], pattern=[[1, 2 * TILE]], base=0, channel_multiplier=0,
                           allow_small_or_imprecise_dtypes=True).then_inc(att_consts, 1)
                    G.iota(win_start[:, :], pattern=[[-TILE, NT]], base=0, channel_multiplier=0,
                           allow_small_or_imprecise_dtypes=True).then_inc(att_consts, 1)
                    pool.wait_ge(att_in, 64)
                    wide = windows_spanned(ET.Pool)

                    def gather(out_rows, table_d, index, signal):
                        G.indirect_dma_start(out=out_rows, out_offset=None, in_=table_d,
                                             in_offset=bass.IndirectOffsetOnAxis(ap=index, axis=0)).then_inc(signal, 16)

                    with pool.If(wide <= 1):
                        with pool.Fori(0, NG // (2 * RING)) as i:
                            for h in range(2):
                                g0 = i * 2 * RING + h * RING
                                pool.wait_ge(va_ready, g0)
                                pool.sem_inc(pool_waits, 1)
                                G.tensor_copy(idx[h][:, :], srcidx[:, bass.ds(i * (2 * RING * GRP) + h * RING * GRP, RING * GRP)]
                                              ).then_inc(idx_ready, 1)
                                pool.wait_ge(idx_ready, i * 2 + h + 1)
                                pool.sem_inc(pool_waits, 1)
                                for r in range(RING):
                                    pool.wait_ge(va_ready, g0 + r + 1)
                                    pool.sem_inc(pool_waits, 1)
                                    for k in range(GRP):
                                        gather(kv[:, r, k, :], kv_d, idx[h][:, r * GRP + k:r * GRP + k + 1], kv_in[r])
                    with pool.Else():
                        pool.wait_ge(oh_ready, 1)
                        with pool.Fori(0, CH) as c:
                            pool.wait_ge(gen_added, c * NT)
                            pool.sem_inc(pool_waits, 1)
                            G.tensor_copy(idx[0][:, 0:1], srcidx[:, bass.ds(c, 1)]).then_inc(gen_idx, 1)
                            G.tensor_copy(idx[0][:, 1:2], qidx[:, bass.ds(c, 1)]).then_inc(gen_idx, 1)
                            pool.wait_ge(gen_idx, c * 2 + 2)
                            pool.sem_inc(pool_waits, 1)
                            gather(kv[:, 0, 0, :], kv_d, idx[0][:, 0:1], gen_in)
                            gather(kv[:, 0, 1, 0:C], q_d, idx[0][:, 1:2], gen_in)

                @block.vector
                def _(dve):
                    st = Steps(dve, gen_step)
                    st.done(V.memset(acc[:, :, :], 0.0))
                    st.done(V.memset(VA[1][:, :, :], 0.0))
                    st.done(V.memset(oh32[1][:, :, :], 0.0))
                    st.done(V.memset(ps[4][:, :], 0.0))
                    V.tensor_copy(ident_h[:, :], ident[:, :]).then_inc(att_consts, 1)
                    dve.wait_ge(att_in, 64)
                    dve.wait_ge(att_consts, 3)
                    st.run(V.tensor_scalar(qidx_f[:, :], dst_l[:, :], float(N - 1), None, ALU.min))
                    st.run(V.tensor_copy(qidx[:, :], qidx_f[:, :]))
                    wide = windows_spanned(ET.DVE)

                    def one_hots(column, place):
                        for k in range(GRP):
                            last = V.tensor_scalar(oh16[:, place, k, :], iota_n[:, :], reldst[:, bass.ds(column + k, 1)],
                                                   None, ALU.is_equal)
                        last.then_inc(oh_ready, 1)

                    def add(w0, bank, added):
                        dve.wait_ge(seg_added, added)
                        V.tensor_tensor(acc[:, bass.ds(w0, 2), :], acc[:, bass.ds(w0, 2), :],
                                        ps[4 + bank][0:TILE, 0:2 * VW].rearrange("p (w c) -> p w c", w=2),
                                        ALU.add).then_inc(seg_added, 1)

                    with dve.If(wide <= 1):
                        dve.sem_inc(va_ready, RING)
                        one_hots(0, 0)
                        one_hots(GRP, 1)
                        with dve.Fori(0, NG // 4) as i:
                            w0 = load_registers(nc, ET.DVE, wtab[0:1, bass.ds(i * 4, 4)], NT - 1)
                            for r in range(4):
                                g = i * 4 + r
                                dve.wait_ge(kv_in[r], (i + 1) * 16 * GRP)
                                dve.wait_ge(qe_done, g + 1)
                                dve.wait_ge(score_sum, g)
                                V.tensor_tensor(prod[:, :, :], kv[:, r, :, 0:C],
                                                ps[2 + r % 2][:, 0:GRP * C].rearrange("p (k c) -> p k c", k=GRP),
                                                ALU.mult).then_inc(prod_ready, 1)
                                dve.wait_ge(prod_ready, g + 1)
                                V.tensor_reduce(out=score[r % 2][:, :], in_=prod[:, :, :].rearrange("p k (h c) -> p (k h) c", h=HEADS),
                                                axis=AX.X, op=ALU.add).then_inc(score_sum, 1)
                                dve.wait_ge(score_sum, g + 1)
                                V.tensor_scalar(score[r % 2][:, :], score[r % 2][:, :], 5.0, -5.0, ALU.min, ALU.max).then_inc(score_ready, 1)
                                dve.wait_ge(seg_done, g)
                                add(w0[r], r % 2, g)
                                one_hots((g + 2) * GRP, (r + 2) % 4)
                                dve.wait_ge(a_ready, g + 1)
                                V.tensor_tensor(VA[r % 2][:, :, 0:C].rearrange("p k (h c) -> p k h c", h=HEADS),
                                                kv[:, r, :, C:2 * C].rearrange("p k (h c) -> p k h c", h=HEADS),
                                                VA[r % 2][:, :, C:VW].unsqueeze(3).to_broadcast([LANES, GRP, HEADS, HD]),
                                                ALU.mult).then_inc(va_ready, 1)
                        w0 = load_registers(nc, ET.DVE, wtab[0:1, NG:NG + 4], NT - 1)
                        for r in range(2):
                            dve.wait_ge(seg_done, NG + r)
                            add(w0[r], r, NG + r)
                    with dve.Else():
                        dve.sem_inc(oh_ready, 1)
                        with dve.Fori(0, CH) as c:
                            dve.wait_ge(gen_in, (c + 1) * 32)
                            V.tensor_tensor(prod[:, 0, :], kv[:, 0, 0, 0:C], kv[:, 0, 1, 0:C], ALU.mult).then_inc(prod_ready, 1)
                            V.tensor_scalar(rel_all[:, :], win_start[:, :], dst_l[:, bass.ds(c, 1)], None, ALU.add)
                            dve.wait_ge(prod_ready, c + 1)
                            V.tensor_reduce(out=score[0][:, 0:HEADS], in_=prod[:, 0, :].rearrange("p (h c) -> p h c", h=HEADS),
                                            axis=AX.X, op=ALU.add).then_inc(score_sum, 1)
                            dve.wait_ge(score_sum, c + 1)
                            V.tensor_scalar(score[0][:, 0:HEADS], score[0][:, 0:HEADS], 5.0, -5.0, ALU.min, ALU.max).then_inc(gen_score, 1)
                            dve.wait_ge(gen_a, c + 1)
                            V.tensor_tensor(VA[0][:, 0, 0:C].rearrange("p (h c) -> p h c", h=HEADS),
                                            kv[:, 0, 0, C:2 * C].rearrange("p (h c) -> p h c", h=HEADS),
                                            VA[0][:, 0, C:VW].unsqueeze(2).to_broadcast([LANES, HEADS, HD]), ALU.mult)
                            with dve.Fori(0, NT) as w:
                                dve.wait_ge(gen_added, c * NT + w)
                                V.tensor_scalar(oh32[0][:, 0, 0:TILE], iota_n[:, 0:TILE], rel_all[:, bass.ds(w, 1)], None,
                                                ALU.is_equal).then_inc(gen_oh, 1)
                                dve.wait_ge(gen_seg, c * NT + w + 1)
                                V.tensor_tensor(acc[:, bass.ds(w, 1), :], acc[:, bass.ds(w, 1), :],
                                                ps[4][0:TILE, 0:VW].unsqueeze(1), ALU.add).then_inc(gen_added, 1)

                @block.tensor
                def _(pe):
                    pe.wait_ge(att_in, 64)
                    pe.wait_ge(att_consts, 3)
                    wide = windows_spanned(ET.PE)

                    def turn(place, n):
                        pe.wait_ge(oh_ready, n + 1)
                        bank = ps[place % 2][:, :].bitcast(fp16)
                        for w in range(2):
                            for k in range(GRP):
                                last = T.transpose(bank[0:TILE, (w * GRP + k) * LANES:(w * GRP + k + 1) * LANES],
                                                   oh16[:, place, k, w * TILE:(w + 1) * TILE], ident_h[:, :])
                        last.then_inc(tr_done, 1)

                    def pick(place, n, w0):
                        pe.wait_ge(ohT_ready, n + 1)
                        for k in range(GRP):
                            for w in range(2):
                                last = T.matmul(ps[2 + place % 2][:, k * C:(k + 1) * C], ohT[place % 2][:, w, k, :],
                                                Q[:, bass.ds(w0 + w, 1), :].rearrange("p w c -> p (w c)"), start=(w == 0), stop=(w == 1))
                        last.then_inc(qe_done, 1)

                    def sums(place, n):
                        pe.wait_ge(va_ready, RING + n + 1)
                        pe.wait_ge(oh32_ready, n + 1)
                        pe.wait_ge(seg_added, n + 1)
                        for w in range(2):
                            for k in range(GRP):
                                last = T.matmul(ps[4 + place % 2][0:TILE, w * VW:(w + 1) * VW],
                                                oh32[place % 2][:, k, w * TILE:(w + 1) * TILE], VA[place % 2][:, k, :],
                                                start=(k == 0), stop=(k == GRP - 1))
                        last.then_inc(seg_done, 1)

                    with pe.If(wide <= 1):
                        w0 = load_registers(nc, ET.PE, wtab[0:1, 0:4], NT - 1)
                        for r in range(2):
                            turn(r, r)
                            pick(r, r, w0[2 + r])
                        with pe.Fori(0, NG // 4) as i:
                            w0 = load_registers(nc, ET.PE, wtab[0:1, bass.ds(i * 4 + 4, 4)], NT - 1)
                            for r in range(4):
                                g = i * 4 + r
                                pe.wait_ge(ohT_ready, g + 1)
                                turn((r + 2) % 4, g + 2)
                                sums(r + 3, g - 1)
                                pe.wait_ge(prod_ready, g + 1)
                                pick((r + 2) % 4, g + 2, w0[r])
                        sums(3, NG - 1)
                    with pe.Else():
                        with pe.Fori(0, CH) as c:
                            with pe.Fori(0, NT) as w:
                                pe.wait_ge(gen_oh, c * NT + w + 1)
                                T.matmul(ps[4][0:TILE, 0:VW], oh32[0][:, 0, 0:TILE], VA[0][:, 0, :], start=True,
                                         stop=True).then_inc(gen_seg, 1)

                @block.scalar
                def _(act):
                    act.wait_ge(att_in, 64)
                    act.wait_ge(att_consts, 3)
                    wide = windows_spanned(ET.Activation)

                    def copy_turned(place, n):
                        act.wait_ge(tr_done, n + 1)
                        S.copy(ohT[place % 2][:, :, :, :].rearrange("p w k n -> p (w k n)"),
                               ps[place % 2][:, :].bitcast(fp16)[0:TILE, :]).then_inc(ohT_ready, 1)

                    def widen(place, n):
                        act.wait_ge(oh_ready, n + 1)
                        S.copy(oh32[place % 2][:, :, :], oh16[:, place, :, :]).then_inc(oh32_ready, 1)

                    with act.If(wide <= 1):
                        copy_turned(0, 0)
                        copy_turned(1, 1)
                        widen(0, 0)
                        with act.Fori(0, NG // 4) as i:
                            for r in range(4):
                                g = i * 4 + r
                                act.wait_ge(score_ready, g + 1)
                                act.wait_ge(seg_done, g)
                                S.activation(VA[r % 2][:, :, C:VW], score[r % 2][:, :].rearrange("p (k h) -> p k h", h=HEADS),
                                             ACT.Exp).then_inc(a_ready, 1)
                                act.wait_ge(qe_done, g + 1)
                                copy_turned(r + 2, g + 2)
                                act.wait_ge(seg_done, g + 1)
                                widen((r + 1) % 4, g + 1)
                    with act.Else():
                        with act.Fori(0, CH) as c:
                            act.wait_ge(gen_score, c + 1)
                            S.activation(VA[0][:, 0, C:VW], score[0][:, 0:HEADS], ACT.Exp).then_inc(gen_a, 1)

        arena_at[0] = arena_mid
        s6 = ExitStack()
        with s6:
            t = lambda name, shape, dt: sb(name, shape, dt, s6)
            wvT = [carve([C, BLK]) for _ in range(2)]
            h2T = parts_all[0][:, :, :, :].rearrange("p t h c -> p (t h c)").bitcast(fp32)
            rden = carve([TILE, NT, HEADS])
            wo = carve([C, C])
            w1 = t("w1", [C, 2 * C], fp32)
            w2 = t("w2", [C, 2, C], fp32)
            b2_row = t("b2_row", [1, C], fp32)
            hn = t("hn", [C, BLK], fp32)
            hid = [t(f"hid{i}", [C, 2, BLK], fp32) for i in range(2)]
            u = t("u6", [TILE, BLK // TILE, C], fp32)
            bst = t("bst6", [C, NBLK + 1, 6], fp32)
            bmv = t("bmv6", [C, 2], fp32)
            bcol = t("bcol6", [C, 10], fp32)
            stats = t("stats6", [TILE, 4, 6], fp32)
            mv = t("mv6", [TILE, 4, 2], fp32)
            std = t("std6", [TILE, 4], fp32)
            rstd = t("rstd6", [TILE, 4], fp32)
            ff_in = sem("ff_in")
            rden_step = sem("rden_step")
            wv_ready = sem("wv_ready")
            wvt_done = sem("wvt_done")
            wvt_copied = sem("wvt_copied")
            h2_done = sem("h2_done")
            h2_copied = sem("h2_copied")
            h2_stats = sem("h2_stats")
            bn2_step = sem("bn2_step")
            bn2_var = sem("bn2_var")
            bn2_std = sem("bn2_std")
            bn2_ready = sem("bn2_ready")
            hn2_ready = sem("hn2_ready")
            hid_done = sem("hid_done")
            hid_copied = sem("hid_copied")
            ff_done = sem("ff_done")
            u_ready = sem("u_ready")
            u_stats = sem("u_stats")
            u_std = sem("u_std")
            u_normed = sem("u_normed")
            hi_ready = sem("hi_ready")
            u_step = sem("u_step")
            counts_back = sem("counts_back")
            with nc.Block() as block:
                @block.sync
                def _(sp):
                    sp.dma_start(wo[:, :], Wo).then_inc(ff_in, 16)
                    sp.dma_start(w1[:, :], W1).then_inc(ff_in, 16)
                    sp.dma_start(w2[:, :, :], W2.rearrange("(j f) c -> f j c", j=2)).then_inc(ff_in, 16)
                    sp.dma_start(b2_row[0:1, :], b2.unsqueeze(0)).then_inc(ff_in, 16)
                    for i, col in ((0, bn2_g), (1, bn2_b), (7, bo), (8, b1[0:C]), (9, b1[C:2 * C])):
                        sp.dma_start(bcol[:, i:i + 1], column(col)).then_inc(ff_in, 16)
                    sp.wait_ge(h2_copied, NBLK + 1)
                    sp.dma_start(counts_all[0:TILE, SPILL * N:NT * N], counts_d).then_inc(counts_back, 16)
                    sp.wait_ge(counts_back, 16)

                @block.tensor
                def _(pe):
                    def turn(b, nt, t0):
                        pe.wait_ge(wv_ready, b + 1)
                        if b >= 2:
                            pe.wait_ge(wvt_copied, b - 1)
                        for j in range(nt):
                            last = T.transpose(ps[b % 2][:, j * TILE:(j + 1) * TILE], acc[:, t0 + j, 0:C], ident[0:TILE, 0:TILE])
                        last.then_inc(wvt_done, 1)

                    def hidden(b, w):
                        pe.wait_ge(hn2_ready, b + 1)
                        if b:
                            pe.wait_ge(hid_copied, b)
                        for j in range(2):
                            last = T.matmul(ps[4 + j][:, 0:w], w1[:, j * C:(j + 1) * C], hn[:, 0:w], start=True, stop=True)
                        last.then_inc(hid_done, 1)

                    every = list(blocks())
                    pe.wait_ge(ff_in, 16 * 9)
                    turn(0, 4, 0)
                    for b, d0, w, t0, nt in every:
                        if b < NBLK:
                            turn(b + 1, every[b + 1][4], every[b + 1][3])
                        pe.wait_ge(wvt_copied, b + 1)
                        if b >= 2:
                            pe.wait_ge(h2_copied, b - 1)
                        for j in range(nt):
                            o = ps[2 + b % 2][:, j * TILE:(j + 1) * TILE]
                            T.matmul(o, wo[:, :], wvT[b % 2][:, j * TILE:(j + 1) * TILE], start=True, stop=False)
                            for part in range(2):
                                last = T.matmul(o, x2[:, t0 + j, part, :], ident_a[0:TILE, 4, :], start=False, stop=(part == 1))
                        last.then_inc(h2_done, 1)
                    hidden(0, BLK)
                    for b, d0, w, t0, nt in every:
                        if b < NBLK:
                            hidden(b + 1, every[b + 1][2])
                        pe.wait_ge(hid_copied, b + 1)
                        if b >= 2:
                            pe.wait_ge(u_ready, b - 1)
                        for j in range(nt):
                            y = ps[6 + b % 2][0:TILE, j * C:(j + 1) * C]
                            cols = slice(j * TILE, (j + 1) * TILE)
                            T.matmul(y, hid[b % 2][:, 0, cols], w2[:, 0, :], start=True, stop=False)
                            T.matmul(y, hid[b % 2][:, 1, cols], w2[:, 1, :], start=False, stop=False)
                            T.matmul(y, h2T[:, d0 + j * TILE:d0 + (j + 1) * TILE], ident[:, :], start=False, stop=False)
                            last = T.matmul(y, ones_row[0:1, :], b2_row[0:1, :], start=False, stop=True)
                        last.then_inc(ff_done, 1)

                @block.scalar
                def _(act):
                    act.wait_ge(ff_in, 16 * 9)
                    for b, d0, w, t0, nt in blocks():
                        act.wait_ge(wvt_done, b + 1)
                        if b >= 2:
                            act.wait_ge(h2_done, b - 1)
                        S.copy(wvT[b % 2][:, 0:w], ps[b % 2][:, 0:w]).then_inc(wvt_copied, 1)
                        act.wait_ge(h2_done, b + 1)
                        S.activation(h2T[:, d0:d0 + w], ps[2 + b % 2][:, 0:w], ACT.Identity, bias=bcol[:, 7:8]).then_inc(h2_copied, 1)
                    act.wait_ge(bn2_var, 1)
                    S.activation(bcol[:, 2:3], bmv[:, 1:2], ACT.Sqrt, bias=eps_t[:, 0:1]).then_inc(bn2_std, 1)
                    act.wait_ge(bn2_ready, 1)
                    act.wait_ge(h2_copied, NBLK + 1)
                    every = list(blocks())

                    def norm(b, d0, w):
                        if b:
                            act.wait_ge(hid_done, b)
                        S.activation(hn[:, 0:w], h2T[:, d0:d0 + w], ACT.Identity, scale=bcol[:, 4:5],
                                     bias=bcol[:, 5:6]).then_inc(hn2_ready, 1)

                    def relu(b, w):
                        act.wait_ge(hid_done, b + 1)
                        if b >= 2:
                            act.wait_ge(ff_done, b - 1)
                        for j in range(2):
                            last = S.activation(hid[b % 2][:, j, 0:w], ps[4 + j][:, 0:w], ACT.Relu, bias=bcol[:, 8 + j:9 + j])
                        last.then_inc(hid_copied, 1)

                    norm(*every[0][:3])
                    relu(0, BLK)
                    norm(*every[1][:3])
                    for b, d0, w, t0, nt in every:
                        if b < NBLK:
                            relu(b + 1, every[b + 1][2])
                        if b < NBLK - 1:
                            norm(*every[b + 2][:3])
                        act.wait_ge(u_stats, b + 1)
                        S.activation(std[:, 0:nt], mv[:, 0:nt, 1], ACT.Sqrt, bias=eps_t[0:TILE, 0:1]).then_inc(u_std, 1)
                        act.wait_ge(u_normed, b + 1)
                        S.activation(x2[:, t0:t0 + nt, 0, :], u[:, 0:nt, :], ACT.Copy, scale=ALPHA_LN).then_inc(hi_ready, 1)

                @block.vector
                def _(dve):
                    st = Steps(dve, rden_step)
                    st.run(V.tensor_scalar(rden[:, :, :], acc[:, 0:NT, C:VW], 1e-30, None, ALU.max))
                    st.run(V.reciprocal(rden[:, :, :], rden[:, :, :]))
                    for b, d0, w, t0, nt in blocks():
                        wv = acc[:, t0:t0 + nt, 0:C].rearrange("p t (h c) -> p t h c", h=HEADS)
                        V.tensor_tensor(wv, wv, rden[:, t0:t0 + nt, :].unsqueeze(3).to_broadcast([TILE, nt, HEADS, HD]),
                                        ALU.mult).then_inc(wv_ready, 1)
                    for b, d0, w, t0, nt in blocks():
                        dve.wait_ge(h2_copied, b + 1)
                        V.bn_stats(bst[:, b, :], h2T[:, d0:d0 + w]).then_inc(h2_stats, 1)
                    dve.wait_ge(h2_stats, NBLK + 1)
                    V.bn_aggr(bmv[:, :], bst[:, :, :].rearrange("p b s -> p (b s)")).then_inc(bn2_var, 1)
                    dve.wait_ge(bn2_var, 1)
                    dve.wait_ge(bn2_std, 1)
                    dve.wait_ge(ff_in, 16 * 9)
                    s2_ = Steps(dve, bn2_step)
                    s2_.run(V.reciprocal(bcol[:, 3:4], bcol[:, 2:3]))
                    s2_.run(V.tensor_tensor(bcol[:, 4:5], bcol[:, 3:4], bcol[:, 0:1], ALU.mult))
                    s2_.run(V.tensor_tensor(bcol[:, 6:7], bmv[:, 0:1], bcol[:, 4:5], ALU.mult))
                    V.tensor_tensor(bcol[:, 5:6], bcol[:, 1:2], bcol[:, 6:7], ALU.subtract).then_inc(bn2_ready, 1)
                    s3_ = Steps(dve, u_step)
                    for b, d0, w, t0, nt in blocks():
                        u_ = u[:, 0:nt, :]
                        s3_.run(V.tensor_tensor(u_, x2[:, t0:t0 + nt, 0, :], x2[:, t0:t0 + nt, 1, :], ALU.add))
                        dve.wait_ge(ff_done, b + 1)
                        V.scalar_tensor_tensor(u_, u_, 1.0 / ALPHA_LN,
                                               ps[6 + b % 2][0:TILE, 0:nt * C].rearrange("p (j c) -> p j c", c=C),
                                               ALU.mult, ALU.add).then_inc(u_ready, 1)
                        dve.wait_ge(u_ready, b + 1)
                        for j in range(nt):
                            last = V.bn_stats(stats[:, j, :], u[:, j, :])
                        s3_.run(last)
                        for j in range(nt):
                            last = V.bn_aggr(mv[:, j, :], stats[:, j, :])
                        last.then_inc(u_stats, 1)
                        dve.wait_ge(u_std, b + 1)
                        s3_.run(V.reciprocal(rstd[:, 0:nt], std[:, 0:nt]))
                        for j in range(nt):
                            last = V.tensor_scalar(u[:, j, :], u[:, j, :], mv[:, j, 0:1], rstd[:, j:j + 1], ALU.subtract, ALU.mult)
                        last.then_inc(u_normed, 1)
                        dve.wait_ge(hi_ready, b + 1)
                        s3_.run(V.scalar_tensor_tensor(x2[:, t0:t0 + nt, 1, :], u_, ALPHA_LN, x2[:, t0:t0 + nt, 0, :],
                                                       ALU.mult, ALU.subtract))
        layers([5])


_INS = ["x", "src", "dst", "L0_gnn_Wl", "L0_gnn_bl", "L0_gnn_Wr", "L0_gnn_ln_w", "L0_gnn_ln_b", "L1_gnn_W", "L1_gnn_b",
        "L2_gnn_Wq", "L2_gnn_Wk", "L2_gnn_Wv", "L2_gnn_Wo", "L2_gnn_bo", "L2_gnn_bn1_g", "L2_gnn_bn1_b",
        "L2_gnn_bn2_g", "L2_gnn_bn2_b", "L2_gnn_W1", "L2_gnn_b1", "L2_gnn_W2", "L2_gnn_b2", "L3_gnn_W", "L3_gnn_b"]


def kernel(**inputs):
    import concourse.bacc as bacc
    from concourse.bass_utils import run_bass_kernel_spmd

    nc = bacc.Bacc("TRN2", target_bir_lowering=False, num_devices=1)
    arrays, args = {}, []
    for name in _INS:
        a = np.ascontiguousarray(inputs[name])
        arrays[f"in_{name}"] = a
        args.append(nc.dram_tensor(f"in_{name}", a.shape, mybir.dt.from_np(a.dtype), kind="ExternalInput").ap())
    out = nc.dram_tensor("out", (N, C), fp32, kind="ExternalOutput").ap()
    build(nc, *args, out)
    return run_bass_kernel_spmd(nc, [arrays], core_ids=[0]).results[0]["out"]
```

```python
import numpy as np
import concourse.bass as bass
from concourse import mybir
from contextlib import ExitStack, contextmanager

fp32, fp16, bf16, i32 = mybir.dt.float32, mybir.dt.float16, mybir.dt.bfloat16, mybir.dt.int32
ALU = mybir.AluOpType
ACT = mybir.ActivationFunctionType
AX = mybir.AxisListType

N, E, C = 3125, 53125, 128
HEADS, HD = 8, 16
TILE = 125
NT = N // TILE
LANES = 128
CH = -(-E // LANES)
CHP = CH + 24
ROWS, ROWG = 104, CH // 104
NO_NODE = 4000.0
BWN = 25
BW = N // BWN
BKEYS = BWN * NT
BHALF = 13 * NT
BK = 5
AK = 2
DS = 5
DW = 4 * BWN
CHUNK_OFF = 60000
BLK = 500
NBLK = N // BLK
EPS = 1e-5
GRP = 4
NG = CH // GRP
VW = C + HEADS
SPILL = 15
ALPHA_LN = 4096.0
LN_BOUND = 11.4


class Steps:

    def __init__(self, eng, sem):
        self.eng, self.sem, self.n, self.base = eng, sem, 0, 0

    def done(self, ins):
        ins.then_inc(self.sem, 1)
        self.n += 1

    def wait(self):
        self.eng.wait_ge(self.sem, self.base + self.n)

    def run(self, ins):
        self.done(ins)
        self.wait()

    @contextmanager
    def loop(self, count, per):
        n0, base0 = self.n, self.base
        with self.eng.Fori(0, count) as i:
            self.base = base0 + i * per
            yield i
            assert self.n - n0 == per, (self.n - n0, per)
        self.base = base0
        self.n = n0 + per * count


def load_registers(nc, engine, row, hi):
    _, vals = nc.values_load_multi_w_load_instructions(row, engines=[engine], min_val=0, max_val=hi)
    return vals


def build(nc, x, src, dst, Wl, bl, Wr, ln_w, ln_b, W1g, b1g, Wq, Wk, Wv, Wo, bo, bn1_g, bn1_b,
          bn2_g, bn2_b, W1, b1, W2, b2, W3g, b3g, out):
    ET = mybir.EngineType
    V, S, G, T = nc.vector, nc.scalar, nc.gpsimd, nc.tensor
    dram = lambda name, shape, dt: nc.dram_tensor(name, shape, dt, kind="Internal").ap()
    build_table_d = dram("build_table_d", (BW, 4), i32)
    key_d = dram("key_d", (LANES, CHP), fp32)
    sl_d = dram("sl_d", (LANES, CHP), fp32)
    wt_d = dram("wt_d", (C, 10, C), fp32)
    srcidx_d = dram("srcidx_d", (LANES, CHP), i32)
    dstf_d = dram("dstf_d", (LANES, CHP), fp32)
    reldst_d = dram("reldst_d", (LANES, CHP), fp32)
    win_table_d = dram("win_table_d", (1, 128), i32)
    kv_d = dram("kv_d", (N, 2 * C), fp32)
    q_d = dram("q_d", (N, C), fp32)
    counts_d = dram("counts_d", (TILE, (NT - SPILL) * N), fp16)

    ctx = ExitStack()
    with ctx:
        def sb(name, shape, dt, scope=ctx):
            return scope.enter_context(nc.sbuf_tensor(name, shape, dt))

        def sem(name):
            return ctx.enter_context(nc.semaphore(name))

        ps = [ctx.enter_context(nc.psum_tensor(f"bank{i}", [128, 512], fp32)) for i in range(8)]

        ident = sb("ident", [128, 128], fp32)
        alpha = sb("alpha", [128, 8], fp32)
        inv_alpha = sb("inv_alpha", [128, 8], fp32)
        ident_a = sb("ident_a", [128, 5, TILE], bf16)
        eps_t = sb("eps_t", [128, 1], fp32)
        ones_row = sb("ones_row", [1, TILE], fp32)
        has_edge = sb("has_edge", [TILE, NT], fp32)
        parts_all = [sb(f"parts{i}", [128, NT, 2, C], fp16) for i in range(2)]  
        parts = [p[0:TILE] for p in parts_all]
        inv_deg = sb("inv_deg", [128, NT * C], fp32)
        xf = inv_deg[0:TILE, :].rearrange("p (t c) -> p t c", c=C)

        s1 = ExitStack()
        with s1:
            t = lambda name, shape, dt: sb(name, shape, dt, s1)
            src_rows = t("src_rows", [ROWS, ROWG, LANES], i32)
            dst_rows = t("dst_rows", [ROWS, ROWG, LANES], i32)
            src_rf = t("src_rf", [ROWS, ROWG, LANES], fp32)
            dst_rf = t("dst_rf", [ROWS, ROWG, LANES], fp32)
            real = t("real", [ROWS, ROWG, LANES], fp32)
            mm = t("mm", [ROWS, 2, ROWG], fp32)
            diag = t("diag", [ROWS, 2, ROWG, ROWS], fp32)
            ones = t("ones", [128, 128], fp32)
            iota_f = t("iota_f", [128, 128], fp32)
            iota_p = t("iota_p", [128, 1], fp32)
            iota_c1 = t("iota_c1", [128, CH], fp32)
            tri = t("tri", [128, 128], fp32)
            win = t("win", [128, 2], fp32)
            hit1 = t("hit1", [128, CH], fp32)
            hit = t("hit", [128, CH], fp32)
            cand = t("cand", [128, CH], fp32)
            cand2 = t("cand2", [128, CH], fp32)
            lohi = t("lohi", [128, 8], fp32)
            ng_i = t("ng_i", [128, 2], i32)
            tab_i = t("tab_i", [128, 4], i32)
            srcN = t("srcN", [LANES, CHP], fp32)
            dstN = t("dstN", [LANES, CHP], fp32)
            src_i = t("src_i", [LANES, CHP], i32)
            shi = t("shi", [LANES, CHP], i32)
            shf = t("shf", [LANES, CHP], fp32)
            fix = t("fix", [LANES, CHP], fp32)
            slN0 = t("slN0", [LANES, CHP], fp32)
            keyN0 = t("keyN0", [LANES, CHP], fp32)
            w_raw = t("w_raw", [128, 10, C], fp32)
            lnw_all = t("lnw_all", [128, 4, C], fp32)
            lnb_all = t("lnb_all", [128, 4, C], fp32)
            gmm = t("gmm", [128, 2, NG], fp32)
            gq = t("gq", [128, 2, NG], fp32)
            gqi = t("gqi", [128, 2, NG], i32)
            gr = t("gr", [128, 2, NG], fp32)
            gf = t("gf", [128, 2, NG], fp32)
            w0_i = t("w0_i", [128, 128], i32)
            w0_f = t("w0_f", [128, 128], fp32)
            reldst = t("reldst", [LANES, CHP], fp32)
            absmax = t("absmax", [128, 16], fp32)
            absmax_r = t("absmax_r", [128, 16], fp32)
            bound = t("bound", [128, 8], fp32)
            WT = t("WT", [128, 10, C], fp32)

            rows_cleared = sem("rows_cleared")
            edges_in = sem("edges_in")
            x_in = sem("x_in")
            w_in = sem("w_in")
            consts_ready = sem("consts_ready")
            setup_step = sem("setup_step")
            edges_f = sem("edges_f")
            edges_t = sem("edges_t")
            diag_ready = sem("diag_ready")
            minmax_bc = sem("minmax_bc")
            ng_ready = sem("ng_ready")
            base_ready = sem("base_ready")
            wt_done = sem("wt_done")
            wt_copied = sem("wt_copied")
            absmax_ready = sem("absmax_ready")
            absmax_all = sem("absmax_all")
            alpha_ready = sem("alpha_ready")
            setup_out = sem("setup_out")
            keys_ready = sem("keys_ready")
            table_ready = sem("table_ready")
            windows_ready = sem("windows_ready")
            table_out = sem("table_out")

            with nc.Block() as block:
                @block.sync
                def _(sp):
                    sp.wait_ge(rows_cleared, 1)
                    for rows, arr in ((dst_rows, dst), (src_rows, src)):
                        n3 = (ROWG - 1) * ROWS * LANES
                        sp.dma_start(rows[:, 0:ROWG - 1, :],
                                     arr[0:n3].rearrange("(t r p) -> r t p", r=ROWS, p=LANES)).then_inc(edges_in, 16)
                        full = (E - n3) // LANES
                        sp.dma_start(rows[0:full, ROWG - 1, :],
                                     arr[n3:n3 + full * LANES].rearrange("(r p) -> r p", p=LANES)).then_inc(edges_in, 16)
                        rest = E - n3 - full * LANES
                        sp.dma_start(rows[full:full + 1, ROWG - 1, 0:rest],
                                     arr[E - rest:E].unsqueeze(0)).then_inc(edges_in, 16)
                    sp.dma_start(xf[:, :, :], x.rearrange("(t p) c -> p t c", p=TILE)).then_inc(x_in, 16)
                    sp.wait_ge(keys_ready, 1)
                    sp.dma_start(key_d, keyN0[:, :]).then_inc(setup_out, 16)
                    sp.dma_start(sl_d, slN0[:, :]).then_inc(setup_out, 16)
                    sp.dma_start(srcidx_d, src_i[:, :]).then_inc(setup_out, 16)
                    sp.dma_start(dstf_d, dstN[:, :]).then_inc(setup_out, 16)
                    sp.wait_ge(table_ready, 1)
                    sp.dma_start(build_table_d, tab_i[0:BW, :]).then_inc(table_out, 16)
                    sp.wait_ge(windows_ready, 1)
                    sp.dma_start(reldst_d, reldst[:, :]).then_inc(setup_out, 16)
                    sp.dma_start(win_table_d, w0_i[0:1, :]).then_inc(setup_out, 16)
                    sp.wait_ge(wt_copied, 3)
                    sp.dma_start(wt_d, WT[:, :, :]).then_inc(setup_out, 16)
                    sp.wait_ge(table_out, 16)
                    sp.wait_ge(setup_out, 112)

                @block.scalar
                def _(act):
                    act.dma_start(w_raw[:, 0:4, :], Wl.rearrange("l o c -> o l c")).then_inc(w_in, 16)
                    act.dma_start(w_raw[:, 4:8, :], Wr.rearrange("l o c -> o l c")).then_inc(w_in, 16)
                    act.dma_start(w_raw[:, 8, :], W1g).then_inc(w_in, 16)
                    act.dma_start(w_raw[:, 9, :], W3g).then_inc(w_in, 16)
                    act.dma_start(lnw_all[:, :, :].rearrange("p l c -> p (l c)"),
                                  ln_w.rearrange("l c -> (l c)").unsqueeze(0).to_broadcast([128, 4 * C])).then_inc(w_in, 16)
                    act.dma_start(lnb_all[:, :, :].rearrange("p l c -> p (l c)"),
                                  ln_b.rearrange("l c -> (l c)").unsqueeze(0).to_broadcast([128, 4 * C])).then_inc(w_in, 16)
                    for j in range(3):
                        k = min(4, 10 - 4 * j)
                        act.wait_ge(wt_done, j + 1)
                        S.copy(WT[:, 4 * j:4 * j + k, :].rearrange("p w c -> p (w c)"), ps[j][:, 0:k * C]).then_inc(wt_copied, 1)
                    act.wait_ge(w_in, 16 * 6)

                @block.gpsimd
                def _(pool):
                    iota = lambda o, pat, b, cm: G.iota(o, pattern=pat, base=b, channel_multiplier=cm,
                                                        allow_small_or_imprecise_dtypes=True)
                    iota(iota_f[:, :], [[1, 128]], 0, 0).then_inc(consts_ready, 1)
                    iota(iota_p[:, :], [[0, 1]], 0, 1).then_inc(consts_ready, 1)
                    iota(iota_c1[:, :], [[1, CH]], 1, 0).then_inc(consts_ready, 1)
                    pool.wait_ge(absmax_ready, 1)
                    G.partition_all_reduce(absmax_r[:, :], absmax[:, :], 128,
                                           bass.bass_isa.ReduceOp.absmax).then_inc(absmax_all, 1)

                @block.vector
                def _(dve):
                    st = Steps(dve, setup_step)
                    st.done(V.memset(src_rows[:, :, :], 0))
                    st.done(V.memset(absmax[:, :], 0.0))
                    V.memset(dst_rows[:, :, :], int(NO_NODE)).then_inc(rows_cleared, 1)
                    st.done(V.memset(ones[:, :], 1.0))
                    st.done(V.memset(ones_row[:, :], 1.0))
                    st.done(V.memset(eps_t[:, :], EPS))
                    st.done(V.memset(srcN[:, :], 0.0))
                    st.done(V.memset(dstN[:, :], NO_NODE))
                    dve.wait_ge(consts_ready, 3)
                    st.done(V.tensor_scalar(ident[:, :], iota_f[:, :], iota_p[:, 0:1], None, ALU.is_equal))
                    st.done(V.tensor_scalar(tri[:, :], iota_f[:, :], iota_p[:, 0:1], None, ALU.is_gt))
                    st.done(V.tensor_scalar(win[:, 0:1], iota_p[:, :], float(BWN), None, ALU.mult))
                    st.done(V.tensor_scalar(win[:, 1:2], iota_p[:, :], float(BWN), float(BWN), ALU.mult, ALU.add))
                    st.wait()
                    dve.wait_ge(edges_in, 16 * 6)
                    st.done(V.tensor_copy(dst_rf[:, :, :], dst_rows[:, :, :]))
                    st.wait()
                    V.tensor_copy(src_rf[:, :, :], src_rows[:, :, :]).then_inc(edges_f, 1)
                    st.done(V.tensor_reduce(out=mm[:, 0, :], in_=dst_rf[:, :, :], axis=AX.X, op=ALU.min))
                    st.run(V.scalar_tensor_tensor(real[:, :, :], dst_rf[:, :, :], NO_NODE - 1, dst_rf[:, :, :],
                                                  ALU.is_lt, ALU.mult))
                    st.run(V.tensor_reduce(out=mm[:, 1, :], in_=real[:, :, :], axis=AX.X, op=ALU.max))
                    for m in range(2):
                        for g in range(ROWG):
                            last = V.tensor_scalar(diag[:, m, g, :], ident[0:ROWS, 0:ROWS], mm[:, m, g:g + 1], None, ALU.mult)
                            if (m, g) == (1, ROWG - 1):
                                last.then_inc(diag_ready, 1)
                    dve.wait_ge(edges_t, 2)
                    st.done(V.tensor_copy(dstN[:, 0:CH], ps[4][:, 0:CH]))
                    st.run(V.tensor_copy(srcN[:, 0:CH], ps[5][:, 0:CH]))
                    st.done(V.tensor_copy(src_i[:, :], srcN[:, :]))
                    st.run(V.tensor_scalar(fix[:, :], srcN[:, :], 1.0 / TILE, None, ALU.mult))
                    st.run(V.tensor_copy(shi[:, :], fix[:, :]))
                    st.run(V.tensor_copy(shf[:, :], shi[:, :]))
                    st.run(V.scalar_tensor_tensor(slN0[:, :], shf[:, :], -float(TILE), srcN[:, :], ALU.mult, ALU.add))
                    st.run(V.tensor_scalar(fix[:, :], slN0[:, :], 0.0, None, ALU.is_lt))
                    st.run(V.tensor_tensor(shf[:, :], shf[:, :], fix[:, :], ALU.subtract))
                    st.run(V.tensor_scalar(fix[:, :], slN0[:, :], float(TILE), None, ALU.is_ge))
                    st.run(V.tensor_tensor(shf[:, :], shf[:, :], fix[:, :], ALU.add))
                    st.run(V.scalar_tensor_tensor(slN0[:, :], shf[:, :], -float(TILE), srcN[:, :], ALU.mult, ALU.add))
                    V.scalar_tensor_tensor(keyN0[:, :], dstN[:, :], float(NT), shf[:, :], ALU.mult, ALU.add).then_inc(keys_ready, 1)
                    dve.wait_ge(minmax_bc, 2)
                    st.run(V.tensor_scalar(hit1[:, :], ps[7][:, 0:CH], win[:, 0:1], None, ALU.is_ge))
                    st.run(V.scalar_tensor_tensor(hit[:, :], ps[6][:, 0:CH], win[:, 1:2], hit1[:, :], ALU.is_lt, ALU.mult))
                    st.done(V.tensor_tensor(cand[:, :], hit[:, :], iota_c1[:, :], ALU.mult))
                    st.run(V.scalar_tensor_tensor(cand2[:, :], hit[:, :], -1.0e6, iota_c1[:, :], ALU.mult, ALU.add))
                    st.done(V.tensor_reduce(out=lohi[:, 1:2], in_=cand[:, :], axis=AX.X, op=ALU.max))
                    st.run(V.tensor_reduce(out=lohi[:, 0:1], in_=cand2[:, :], axis=AX.X, op=ALU.min))
                    st.run(V.tensor_scalar(lohi[:, 0:1], lohi[:, 0:1], 1.0e6 - 1.0, float(CH - 1), ALU.add, ALU.min))
                    st.run(V.tensor_tensor(lohi[:, 2:3], lohi[:, 1:2], lohi[:, 0:1], ALU.subtract))
                    st.run(V.tensor_scalar(lohi[:, 2:3], lohi[:, 2:3], 1.0, float(BK - 1), ALU.max, ALU.add))
                    st.run(V.tensor_scalar(lohi[:, 3:4], lohi[:, 2:3], 205.0, None, ALU.mult))
                    st.run(V.tensor_copy(ng_i[:, 0:1], lohi[:, 3:4]))
                    st.run(V.tensor_scalar(ng_i[:, 1:2], ng_i[:, 0:1], 10, None, ALU.logical_shift_right))
                    V.tensor_copy(lohi[:, 4:5], ng_i[:, 1:2]).then_inc(ng_ready, 1)
                    dve.wait_ge(base_ready, 1)
                    dve.wait_ge(ng_ready, 1)
                    st.run(V.tensor_copy(lohi[:, 5:6], ps[3][:, 0:1]))
                    st.done(V.tensor_tensor(lohi[:, 6:7], lohi[:, 5:6], lohi[:, 4:5], ALU.add))
                    st.run(V.scalar_tensor_tensor(lohi[:, 7:8], lohi[:, 5:6], -float(BK), lohi[:, 0:1], ALU.mult, ALU.add))
                    st.run(V.tensor_scalar(lohi[:, 4:5], lohi[:, 7:8], float(CHUNK_OFF), None, ALU.add))
                    st.done(V.tensor_copy(tab_i[:, 3:4], lohi[:, 0:1]))
                    V.tensor_copy(tab_i[:, 0:3], lohi[:, 4:7]).then_inc(table_ready, 1)
                    st.done(V.tensor_reduce(out=gmm[:, 0, :], in_=ps[6][:, 0:CH].rearrange("p (g k) -> p g k", k=GRP),
                                            axis=AX.X, op=ALU.min))
                    st.run(V.tensor_reduce(out=gmm[:, 1, :], in_=ps[7][:, 0:CH].rearrange("p (g k) -> p g k", k=GRP),
                                           axis=AX.X, op=ALU.max))
                    st.run(V.tensor_scalar(gr[:, :, :], gmm[:, :, :], 1.0 / TILE, None, ALU.mult))
                    st.run(V.tensor_copy(gqi[:, :, :], gr[:, :, :]))
                    st.run(V.tensor_copy(gq[:, :, :], gqi[:, :, :]))
                    st.run(V.scalar_tensor_tensor(gr[:, :, :], gq[:, :, :], -float(TILE), gmm[:, :, :], ALU.mult, ALU.add))
                    st.run(V.tensor_scalar(gf[:, :, :], gr[:, :, :], 0.0, None, ALU.is_lt))
                    st.run(V.tensor_tensor(gq[:, :, :], gq[:, :, :], gf[:, :, :], ALU.subtract))
                    st.run(V.tensor_scalar(gf[:, :, :], gr[:, :, :], float(TILE), None, ALU.is_ge))
                    st.run(V.tensor_tensor(gq[:, :, :], gq[:, :, :], gf[:, :, :], ALU.add))
                    st.run(V.memset(w0_f[:, :], 0.0))
                    st.done(V.tensor_copy(w0_f[:, 2:2 + NG], gq[:, 0, :]))
                    st.run(V.tensor_tensor(gf[:, 0, :], gq[:, 1, :], gq[:, 0, :], ALU.subtract))
                    st.run(V.tensor_reduce(out=w0_f[:, 127:128], in_=gf[:, 0, :], axis=AX.X, op=ALU.max))
                    st.done(V.tensor_copy(w0_i[:, :], w0_f[:, :]))
                    st.run(V.memset(reldst[:, :], NO_NODE))
                    V.scalar_tensor_tensor(reldst[:, 0:CH].rearrange("p (g k) -> p g k", k=GRP),
                                           gq[:, 0, :].unsqueeze(2).to_broadcast([LANES, NG, GRP]), -float(TILE),
                                           dstN[:, 0:CH].rearrange("p (g k) -> p g k", k=GRP),
                                           ALU.mult, ALU.add).then_inc(windows_ready, 1)
                    dve.wait_ge(x_in, 16)
                    dve.wait_ge(w_in, 16 * 6)
                    st.run(V.tensor_reduce(out=absmax[0:TILE, 0:1], in_=xf[:, :, :], axis=AX.XY, op=ALU.max,
                                           apply_absolute_value=True))
                    for l in range(3):
                        st.done(V.tensor_reduce(out=bound[:, l:l + 1], in_=lnw_all[:, l, :], axis=AX.X, op=ALU.max,
                                                apply_absolute_value=True))
                        st.run(V.tensor_reduce(out=bound[:, 4 + l:5 + l], in_=lnb_all[:, l, :], axis=AX.X, op=ALU.max,
                                               apply_absolute_value=True))
                        if l == 0:
                            V.tensor_copy(absmax[:, 1:2], absmax[:, 0:1]).then_inc(absmax_ready, 1)
                    st.run(V.tensor_scalar(cand[:, 0:3], bound[:, 0:3], LN_BOUND, None, ALU.mult))
                    st.run(V.tensor_tensor(cand[:, 4:7], cand[:, 0:3], bound[:, 4:7], ALU.add))
                    st.run(V.tensor_copy(bound[:, 1:4], cand[:, 4:7]))
                    dve.wait_ge(absmax_all, 1)
                    st.run(V.tensor_copy(bound[:, 0:1], absmax_r[:, 0:1]))
                    st.run(V.tensor_scalar(bound[:, 0:4], bound[:, 0:4], 1e-30, None, ALU.max))
                    st.run(V.tensor_scalar(bound[:, 0:4].bitcast(i32), bound[:, 0:4].bitcast(i32), 0x7F800000, None, ALU.bitwise_and))
                    st.done(V.tensor_scalar(inv_alpha[:, 0:4], bound[:, 0:4], 2.0 ** -13, None, ALU.mult))
                    st.done(V.memset(inv_alpha[:, 4:8], 1.0 / ALPHA_LN))
                    st.wait()
                    st.run(V.reciprocal(alpha[:, :], inv_alpha[:, :]))
                    for l in range(5):
                        last = V.tensor_scalar(ident_a[:, l, :], ident[:, 0:TILE], inv_alpha[:, l:l + 1], None, ALU.mult)
                    last.then_inc(alpha_ready, 1)

                @block.tensor
                def _(pe):
                    pe.wait_ge(w_in, 16 * 6)
                    pe.wait_ge(setup_step, 12)
                    for j in range(3):
                        for k in range(min(4, 10 - 4 * j)):
                            last = T.transpose(ps[j][:, k * C:(k + 1) * C], w_raw[:, 4 * j + k, :], ident[:, :])
                        last.then_inc(wt_done, 1)
                    pe.wait_ge(edges_f, 1)
                    for p, rows in ((4, dst_rf), (5, src_rf)):
                        for g in range(ROWG):
                            last = T.transpose(ps[p][:, g * ROWS:(g + 1) * ROWS], rows[:, g, :], ident[0:ROWS, 0:ROWS])
                        last.then_inc(edges_t, 1)
                    pe.wait_ge(diag_ready, 1)
                    for m in range(2):
                        for g in range(ROWG):
                            last = T.matmul(ps[6 + m][:, g * ROWS:(g + 1) * ROWS], ones[0:ROWS, :], diag[:, m, g, :],
                                            start=True, stop=True)
                        last.then_inc(minmax_bc, 1)
                    pe.wait_ge(ng_ready, 1)
                    pe.wait_ge(wt_copied, 3)
                    T.matmul(ps[3][0:128, 0:1], tri[0:128, 0:128], lohi[0:128, 4:5], start=True, stop=True).then_inc(base_ready, 1)

        counts_all = sb("counts_all", [128, NT * N + 3], fp16)
        counts = counts_all[0:TILE, 0:NT * N].rearrange("p (s d) -> p s d", s=NT)
        s2 = ExitStack()
        with s2:
            t = lambda name, shape, dt: sb(name, shape, dt, s2)
            keyN = t("keyN", [LANES, CHP], fp32)
            slN = t("slN", [LANES, CHP], fp32)
            iota_k = t("iota_k", [LANES, BKEYS], fp16)
            win_off = t("win_off", [LANES, BW], fp32)
            rel_key = [t(f"rel_key{i}", [LANES, BK], fp32) for i in range(2)]
            rel_sl = t("rel_sl", [LANES, BK], fp32)
            oh_key = parts_all[1][:, :, :, :].rearrange("p t h c -> p (t h c)")[:, 0:2 * BK * (BKEYS + 1)].rearrange(
                "p (u k n) -> p u k n", u=2, k=BK)
            oh_key = [oh_key[:, i] for i in range(2)]
            ones_h = t("ones_h", [TILE, 128], fp16)
            ones_col = t("ones_col", [LANES, 1], fp32)
            dist = t("dist", [LANES, AK, TILE + 1], fp16)
            oh_sl = [t(f"oh_sl{i}", [LANES, BK, TILE + 1], fp16) for i in range(2)]
            sl_h = t("sl_h", [LANES, CHP], fp16)
            zeros = t("zeros", [LANES, TILE], fp16)
            table = t("table", [1, BW * 4], i32)
            firsts = t("firsts", [1, BW + 3], i32)

            keys_in = sem("keys_in")
            build_consts = sem("build_consts")
            rel_ready = sem("rel_ready")
            dist_ready = sem("dist_ready")
            sl_ready = sem("sl_ready")
            split_step = sem("split_step")
            deg_done = sem("deg_done")
            deg_copied = sem("deg_copied")
            pair_ready = sem("pair_ready")
            pair_free = sem("pair_free")
            window_done = sem("window_done")
            window_free = sem("window_free")

            def total_steps(engine):
                return load_registers(nc, engine, table[0:1, (BW - 1) * 4:BW * 4], 2 * CHUNK_OFF)[1]

            def over_windows(eng, engine, body, ahead=0):
                first = load_registers(nc, engine, firsts[0:1, ahead:ahead + 4], CH - 1)
                for r in range(4):
                    body(0, r, r, first[r])
                with eng.Fori(1, BW // 4) as j:
                    first = load_registers(nc, engine, firsts[0:1, bass.ds(j * 4 + ahead, 4)], CH - 1)
                    for r in range(4):
                        body(j, j * 4 + r, r, first[r])
                first = load_registers(nc, engine, firsts[0:1, BW - 1:BW + 3], CH - 1)
                body(BW // 4, BW - 1, 0, first[0])

            def banks(slot):
                return ps[2 * slot][0:TILE, 0:BHALF], ps[2 * slot + 1][0:TILE, 0:BKEYS - BHALF]

            with nc.Block() as block:
                @block.sync
                def _(sp):
                    sp.dma_start(keyN[:, :], key_d).then_inc(keys_in, 16)
                    sp.dma_start(slN[:, :], sl_d).then_inc(keys_in, 16)
                    sp.dma_start(table[0:1, :], build_table_d.rearrange("w f -> (w f)").unsqueeze(0)).then_inc(keys_in, 16)

                @block.gpsimd
                def _(pool):
                    G.iota(iota_k[:, :], pattern=[[1, BKEYS]], base=0, channel_multiplier=0,
                           allow_small_or_imprecise_dtypes=True).then_inc(build_consts, 1)
                    G.iota(win_off[:, :], pattern=[[-BKEYS, BW]], base=0, channel_multiplier=0,
                           allow_small_or_imprecise_dtypes=True).then_inc(build_consts, 1)

                    st = Steps(pool, split_step)
                    st.run(G.tensor_scalar(xf[:, :, :], xf[:, :, :], alpha[0:TILE, 0:1], None, ALU.mult))
                    st.run(G.tensor_copy(parts[0][:, :, 0, :], xf[:, :, :]))
                    st.run(G.tensor_tensor(parts[0][:, :, 1, :], xf[:, :, :], parts[0][:, :, 0, :], ALU.subtract))

                @block.vector
                def _(dve):
                    V.memset(zeros[:, :], 0.0)
                    V.memset(ones_h[:, :], 1.0)
                    V.memset(ones_col[:, :], 1.0)
                    V.memset(firsts[0:1, BW:BW + 3], 0)
                    dve.sem_inc(pair_ready, 1)
                    dve.sem_inc(deg_copied, 1)
                    dve.wait_ge(keys_in, 48)
                    V.tensor_copy(sl_h[:, :], slN[:, :])
                    V.tensor_copy(firsts[0:1, 0:BW], table[0:1, :].rearrange("p (w f) -> p w f", f=4)[:, :, 3]).then_inc(build_consts, 1)
                    dve.wait_ge(build_consts, 3)
                    total = total_steps(ET.DVE)

                    def add_degrees(j, n):
                        dve.wait_ge(split_step, 3)
                        dve.wait_ge(deg_done, j + 1)
                        V.tensor_reduce(out=inv_deg[:, bass.ds(j * DW, n)], in_=ps[4][:, 0:DS * n].rearrange("p (s n) -> p n s", n=n),
                                        axis=AX.X, op=ALU.add).then_inc(deg_copied, 1)

                    def keys(j, w, r, first):
                        slot = r % 2
                        dve.wait_ge(rel_ready, w + 1)
                        dve.wait_ge(window_done, w + 1)
                        for k in range(BK):
                            if k == AK:
                                shape = [LANES, BK - AK, TILE]
                                V.tensor_tensor(oh_sl[slot][:, AK:BK, 0:TILE], iota_k[:, 0:TILE].unsqueeze(1).to_broadcast(shape),
                                                sl_h[:, bass.ds(first + AK, BK - AK)].unsqueeze(2).to_broadcast(shape), ALU.is_equal)
                            V.tensor_scalar(oh_key[slot][:, k, 0:BKEYS], iota_k[:, :], rel_key[slot][:, k:k + 1], None,
                                            ALU.is_equal).then_inc(pair_ready, 1)
                        if r == 3 and not isinstance(j, int):
                            add_degrees(j - 1, DW)

                    with dve.If(total <= BW):
                        over_windows(dve, ET.DVE, keys)
                        add_degrees(BW // 4 - 1, DW)
                        add_degrees(BW // 4, N - BW // 4 * DW)
                    with dve.Else():
                        with dve.Fori(0, BW) as w:
                            off, first, end, _z = load_registers(nc, ET.DVE, table[0:1, bass.ds(w * 4, 4)], 2 * CHUNK_OFF)
                            with dve.Fori(first, end) as i:
                                chunk = nc.s_assert_within(off + i * BK - CHUNK_OFF, 0, CHP - BK)
                                dve.wait_ge(pair_ready, i * BK + 1)
                                V.tensor_scalar(rel_key[0][:, :], keyN[:, bass.ds(chunk, BK)], win_off[:, bass.ds(w, 1)], None,
                                                ALU.add).then_inc(rel_ready, 1)
                                V.tensor_copy(rel_sl[:, :], slN[:, bass.ds(chunk, BK)]).then_inc(rel_ready, 1)
                                dve.wait_ge(rel_ready, i * 2 + 2)
                                for k in range(BK):
                                    dve.wait_ge(pair_free, i * BK + k + 1)
                                    V.tensor_scalar(oh_sl[0][:, k, 0:TILE], iota_k[:, 0:TILE], rel_sl[:, k:k + 1], None, ALU.is_equal)
                                    V.tensor_scalar(oh_key[0][:, k, 0:BKEYS], iota_k[:, :], rel_key[0][:, k:k + 1], None,
                                                    ALU.is_equal).then_inc(pair_ready, 1)
                        with dve.Fori(0, BW // 4) as j:
                            add_degrees(j, DW)
                        add_degrees(BW // 4, N - BW // 4 * DW)

                @block.tensor
                def _(pe):
                    pe.sem_inc(window_done, 2)
                    pe.wait_ge(build_consts, 3)
                    pe.wait_ge(keys_in, 48)
                    total = total_steps(ET.PE)

                    def degrees(j, n):
                        pe.wait_ge(deg_copied, j + 1)
                        for s in range(0, NT, DS):
                            last = T.matmul(ps[4][:, 0:DS * n], ones_h[:, :], counts[:, s:s + DS, bass.ds(j * DW, n)],
                                            start=(s == 0), stop=(s == NT - DS))
                        last.then_inc(deg_done, 1)

                    def count(j, w, r, _first):
                        slot = r % 2
                        a, b = banks(slot)
                        pe.wait_ge(window_free, w + 1)
                        pe.wait_ge(sl_ready, w + 2)
                        for k in range(BK):
                            pe.wait_ge(pair_ready, w * BK + k + 2)
                            for o, cols in ((a, slice(0, BHALF)), (b, slice(BHALF, BKEYS))):
                                last = T.matmul(o, oh_sl[slot][:, k, 0:TILE], oh_key[slot][:, k, cols], start=(k == 0),
                                                stop=(k == BK - 1))
                        last.then_inc(window_done, 1)
                        if r == 1 and not isinstance(j, int):
                            degrees(j - 1, DW)

                    def window(w, slot):
                        a, b = banks(slot)
                        _o, first, end, _z = load_registers(nc, ET.PE, table[0:1, bass.ds(w * 4, 4)], 2 * CHUNK_OFF)
                        pe.wait_ge(window_free, w + 1)
                        for o in (a, b):
                            T.matmul(o, zeros[:, :], iota_k[:, 0:o.shape[1]], start=True, stop=False, skip_group_check=True)
                        with pe.Fori(first, end) as i:
                            for k in range(BK):
                                pe.wait_ge(pair_ready, i * BK + k + 2)
                                T.matmul(a, oh_sl[0][:, k, 0:TILE], oh_key[0][:, k, 0:BHALF], start=False, stop=False,
                                         skip_group_check=True)
                                T.matmul(b, oh_sl[0][:, k, 0:TILE], oh_key[0][:, k, BHALF:BKEYS], start=False,
                                         stop=False, skip_group_check=True).then_inc(pair_free, 1)
                        for o in (a, b):
                            last = T.matmul(o[:, 0:2], zeros[:, :], iota_k[:, 0:2], start=False, stop=True, skip_group_check=True)
                        last.then_inc(window_done, 1)

                    with pe.If(total <= BW):
                        over_windows(pe, ET.PE, count)
                        pe.wait_ge(window_free, BW + 2)
                        degrees(BW // 4 - 1, DW)
                        degrees(BW // 4, N - BW // 4 * DW)
                    with pe.Else():
                        pe.sem_inc(pair_free, BK)
                        with pe.Fori(0, BW // 2) as j:
                            window(j * 2, 0)
                            window(j * 2 + 1, 1)
                        window(BW - 1, 0)
                        pe.wait_ge(window_free, BW + 2)
                        with pe.Fori(0, BW // 4) as j:
                            degrees(j, DW)
                        degrees(BW // 4, N - BW // 4 * DW)

                @block.scalar
                def _(act):
                    act.sem_inc(window_free, 2)
                    act.wait_ge(build_consts, 3)
                    act.wait_ge(keys_in, 48)
                    total = total_steps(ET.Activation)

                    def evacuate(w, slot, _first=None):
                        h = BHALF // NT
                        a, b = banks(slot)
                        act.wait_ge(window_done, w + 3)
                        S.copy(counts[:, :, bass.ds(w * BWN, h)].rearrange("p s d -> p d s"), a.rearrange("p (d s) -> p d s", s=NT))
                        S.copy(counts[:, :, bass.ds(w * BWN + h, BWN - h)].rearrange("p s d -> p d s"),
                               b.rearrange("p (d s) -> p d s", s=NT)).then_inc(window_free, 1)

                    def prepare(w, slot, first):
                        act.wait_ge(window_done, w + 1)
                        S.activation(rel_key[slot][:, :], keyN[:, bass.ds(first, BK)], ACT.Identity,
                                     bias=win_off[:, bass.ds(w, 1)]).then_inc(rel_ready, 1)
                        act.wait_ge(sl_ready, w + 1)
                        for k in range(AK):
                            last = S.activation(dist[:, k, 0:TILE], iota_k[:, 0:TILE], ACT.Abs, scale=-1.0,
                                                bias=slN[:, bass.ds(first + k, 1)])
                        last.then_inc(dist_ready, 1)
                        act.wait_ge(dist_ready, w + 1)
                        S.activation(oh_sl[slot][:, 0:AK, 0:TILE], dist[:, :, 0:TILE], ACT.Relu, scale=-1.0,
                                     bias=ones_col[:, 0:1]).then_inc(sl_ready, 1)

                    def step(j, w, r, first):
                        if not (isinstance(w, int) and w == BW - 1):
                            prepare(w + 1, (r + 1) % 2, first)
                        evacuate(w, r % 2)

                    with act.If(total <= BW):
                        act.sem_inc(sl_ready, 1)
                        first = load_registers(nc, ET.Activation, firsts[0:1, 0:4], CH - 1)
                        prepare(0, 0, first[0])
                        over_windows(act, ET.Activation, step, ahead=1)
                    with act.Else():
                        with act.Fori(0, BW // 2) as j:
                            evacuate(j * 2, 0)
                            evacuate(j * 2 + 1, 1)
                        evacuate(BW - 1, 0)

        PER = {
            "sage": dict(agg_done=1, agg_scaled=1, xt_done=1, xt_copied=1, y_done=1, y_free=1, stats_ready=1,
                         std_ready=1, z_ready=1, relu_ready=1, parts_ready=1, ln_step=3 + 0, x0_in=0, out_done=0),
            "sage_res": dict(agg_done=1, agg_scaled=1, xt_done=1, xt_copied=1, y_done=1, y_free=1, stats_ready=2,
                             std_ready=2, z_ready=2, relu_ready=2, parts_ready=1, ln_step=6, x0_in=16, out_done=0),
            "message": dict(agg_done=1, agg_scaled=1, xt_done=0, xt_copied=0, y_done=1, y_free=1, stats_ready=1,
                            std_ready=1, z_ready=2, relu_ready=2, parts_ready=1, ln_step=4, x0_in=0, out_done=0),
            "final": dict(agg_done=1, agg_scaled=1, xt_done=1, xt_copied=1, y_done=1, y_free=1, stats_ready=1,
                          std_ready=1, z_ready=1, relu_ready=1, parts_ready=0, ln_step=4, x0_in=0, out_done=16),
        }
        KINDS = ["sage", "sage", "sage", "sage_res", "message", "final"]
        PIN = [0, 1, 0, 1, 0, 1]
        W_AGG = [0, 1, 2, 3, 8, 9]
        W_SELF = [4, 5, 6, 7, None, 9]
        SEMS = {name: sem(name) for name in PER["sage"]}
        FROM_ONE = ("agg_scaled", "y_free", "y_done", "xt_copied", "out_done")

        def at(name, l, b, k=0):
            before = sum((NBLK + 1) * PER[KINDS[m]][name] for m in range(l)) + (name in FROM_ONE)
            return before + k + b * PER[KINDS[l]][name]

        def before_last(name, l, b):
            return at(name, l, b) - (0 if isinstance(b, int) and b == 0 else PER[KINDS[l]][name])

        def pipeline(eng, early, late):
            q = BLK // TILE
            early(0, q, 0)
            with eng.Fori(0, NBLK // 2 - 1) as j:
                for r in (1, 2):
                    early(j * 2 + r, q, r % 2)
                    late(j * 2 + r - 1, q, (r - 1) % 2)
            early(NBLK - 1, q, 1)
            late(NBLK - 2, q, 0)
            early(NBLK, (N - NBLK * BLK) // TILE, 0)
            late(NBLK - 1, q, 1)
            late(NBLK, (N - NBLK * BLK) // TILE, 0)

        def over_blocks(eng, body):
            with eng.Fori(0, NBLK) as b:
                body(b, BLK // TILE)
            body(NBLK, (N - NBLK * BLK) // TILE)

        BIAS_STEPS = 8
        counts_saved = sem("counts_saved")
        deg_cols = sem("deg_cols")
        deg_step = sem("deg_step")

        def layers(ls):
            sl = ExitStack()
            with sl:
                t = lambda name, shape, dt: sb(name, shape, dt, sl)
                tag = f"_{ls[0]}"
                q = BLK // TILE
                agg_sb = t("agg_sb" + tag, [C, BLK], fp32)
                xt_sb = t("xt_sb" + tag, [C, BLK], fp32)
                z = t("z" + tag, [TILE, q, C], fp32)
                u = t("u" + tag, [TILE, q, C], fp32)
                stats = t("stats" + tag, [TILE, q, 6], fp32)
                mv = t("mv" + tag, [TILE, q, 2], fp32)
                std = t("std" + tag, [TILE, q], fp32)
                rstd = t("rstd" + tag, [TILE, q], fp32)
                lnw = t("lnw" + tag, [TILE, C], fp32)
                lnb = t("lnb" + tag, [TILE, C], fp32)
                x0 = t("x0" + tag, [TILE, q, C], fp32) if 3 in ls else None
                wt = t("wt" + tag, [C, 2, C], fp32)
                ones3 = t("ones3" + tag, [3, TILE], bf16)
                bias = t("bias" + tag, [3, C], fp32)
                bias_rest = t("bias_rest" + tag, [3, C], fp32)
                bias_part = t("bias_part" + tag, [3, 3, C], bf16)
                bias_row = t("bias_row" + tag, [3, C], bf16)
                bias_step = sem("bias_step" + tag)
                layer_in = sem("layer_in" + tag)
                stats_taken = sem("stats_taken" + tag)
                agg_ps, xt_ps, y_ps = ps[0:2], ps[2:4], ps[4:6]
                LOADS = {"sage": 5, "sage_res": 5, "message": 2, "final": 3}
                loaded = lambda l: 16 * sum(LOADS[KINDS[m]] for m in ls if m <= l)
                w_S = lambda name: SEMS[name]

                with nc.Block() as block:
                    @block.tensor
                    def _(pe):
                        def sums(l, b, nt, p):
                            pin, w = parts[PIN[l]], nt * TILE
                            pe.wait_ge(w_S("agg_scaled"), before_last("agg_scaled", l, b))
                            for s in range(NT):
                                if l > ls[0] and s % q == 0:
                                    pe.wait_ge(w_S("parts_ready"), at("parts_ready", l - 1, s // q, 1))
                                for part in range(2):
                                    last = T.matmul(agg_ps[p][:, 0:w], pin[:, s, part, :], counts[:, s, bass.ds(b * BLK, w)],
                                                    start=(s + part == 0), stop=(s + part == NT))
                            last.then_inc(w_S("agg_done"), 1)
                            if W_SELF[l] is not None:
                                pe.wait_ge(w_S("xt_copied"), before_last("xt_copied", l, b))
                                for j in range(nt):
                                    for part in range(2):
                                        last = T.matmul(xt_ps[p][:, j * TILE:(j + 1) * TILE], pin[:, b * q + j, part, :],
                                                        ident_a[0:TILE, min(l, 4), :], start=(part == 0), stop=(part == 1))
                                last.then_inc(w_S("xt_done"), 1)

                        def project(l, b, nt, p):
                            if W_SELF[l] is not None:
                                pe.wait_ge(w_S("xt_copied"), at("xt_copied", l, b, 1))
                            pe.wait_ge(w_S("agg_scaled"), at("agg_scaled", l, b, 1))
                            pe.wait_ge(w_S("y_free"), before_last("y_free", l, b))
                            pe.wait_ge(layer_in, loaded(l))
                            if W_SELF[l] is not None:
                                pe.wait_ge(bias_step, BIAS_STEPS * (ls.index(l) + 1))
                            for j in range(nt):
                                y = y_ps[p][0:TILE, j * C:(j + 1) * C]
                                cols = slice(j * TILE, (j + 1) * TILE)
                                last = T.matmul(y, agg_sb[:, cols], wt[:, 0, :], start=True, stop=W_SELF[l] is None)
                                if W_SELF[l] is not None:
                                    T.matmul(y, xt_sb[:, cols], wt[:, 1, :], start=False, stop=False)
                                    last = T.matmul(y, ones3[:, :], bias_row[:, :], start=False, stop=True)
                            last.then_inc(w_S("y_done"), 1)

                        if ls[0] == 0:
                            pe.sem_inc(w_S("y_done"), 1)
                            for j in range(NT):
                                last = T.matmul(ps[6][0:TILE, j:j + 1], inv_deg[0:1, j * TILE:(j + 1) * TILE],
                                                ones_row[0:1, 0:1], start=True, stop=True)
                            last.then_inc(deg_cols, 1)
                        for l in ls:
                            pipeline(pe, lambda b, nt, p: sums(l, b, nt, p), lambda b, nt, p: project(l, b, nt, p))

                    @block.scalar
                    def _(act):
                        def take_own(l, b, nt, p):
                            if W_SELF[l] is not None:
                                w = nt * TILE
                                act.wait_ge(w_S("xt_done"), at("xt_done", l, b, 1))
                                act.wait_ge(w_S("y_done"), at("y_done", l, b))
                                S.copy(xt_sb[:, 0:w], xt_ps[p][:, 0:w]).then_inc(w_S("xt_copied"), 1)

                        def finish(l, b, nt, p):
                            pout, kind = parts[1 - PIN[l]], KINDS[l]
                            tiles = bass.ds(b * q, nt)
                            z_, u_ = z[:, 0:nt, :], u[:, 0:nt, :]

                            def std_of(k):
                                act.wait_ge(w_S("stats_ready"), at("stats_ready", l, b, k))
                                S.activation(std[:, 0:nt], mv[:, 0:nt, 1], ACT.Sqrt, bias=eps_t[0:TILE, 0:1]).then_inc(w_S("std_ready"), 1)

                            if kind == "sage":
                                std_of(1)
                                act.wait_ge(w_S("z_ready"), at("z_ready", l, b, 1))
                                S.activation(pout[:, tiles, 0, :], z_, ACT.Relu, scale=alpha[0:TILE, l + 1:l + 2])
                                S.activation(u_, z_, ACT.Relu).then_inc(w_S("relu_ready"), 1)
                                return
                            if kind == "sage_res":
                                std_of(1)
                            if kind == "final":
                                act.wait_ge(w_S("y_done"), at("y_done", l, b, 1))
                                act.wait_ge(w_S("z_ready"), at("z_ready", l, b))
                                S.activation(u_, y_ps[p][0:TILE, 0:nt * C].rearrange("p (j c) -> p j c", c=C),
                                             ACT.Relu).then_inc(w_S("relu_ready"), 1)
                            else:
                                act.wait_ge(w_S("z_ready"), at("z_ready", l, b, 1))
                                S.activation(u_, z_, ACT.Relu).then_inc(w_S("relu_ready"), 1)
                            std_of(PER[kind]["stats_ready"])
                            if kind != "final":
                                act.wait_ge(w_S("z_ready"), at("z_ready", l, b, 2))
                                S.activation(pout[:, tiles, 0, :], z_, ACT.Copy, scale=ALPHA_LN).then_inc(w_S("relu_ready"), 1)

                        if ls[0] == 0:
                            act.sem_inc(w_S("xt_copied"), 1)
                        for l in ls:
                            pipeline(act, lambda b, nt, p: take_own(l, b, nt, p), lambda b, nt, p: finish(l, b, nt, p))

                    @block.vector
                    def _(dve):
                        st = Steps(dve, w_S("ln_step"))

                        def scale(l, b, nt, p):
                            w = nt * TILE
                            if l == 0:
                                deg = inv_deg[:, bass.ds(b * BLK, w)]
                                V.tensor_scalar(deg, deg, 1.0, None, ALU.max).then_inc(deg_step, 1)
                                dve.wait_ge(deg_step, b * 2 + 1)
                                dve.sem_inc(stats_taken, 1)
                                V.reciprocal(deg, deg).then_inc(deg_step, 1)
                                dve.wait_ge(deg_step, b * 2 + 2)
                            dve.wait_ge(w_S("agg_done"), at("agg_done", l, b, 1))
                            dve.wait_ge(w_S("y_done"), at("y_done", l, b))
                            V.scalar_tensor_tensor(agg_sb[:, 0:w], agg_ps[p][:, 0:w], inv_alpha[:, l:l + 1],
                                                   inv_deg[:, bass.ds(b * BLK, w)], ALU.mult, ALU.mult).then_inc(w_S("agg_scaled"), 1)

                        def finish(l, b, nt, p):
                            pin, pout, kind = parts[PIN[l]], parts[1 - PIN[l]], KINDS[l]
                            tiles = bass.ds(b * q, nt)
                            z_, u_ = z[:, 0:nt, :], u[:, 0:nt, :]
                            y = lambda j: y_ps[p][0:TILE, j * C:(j + 1) * C]
                            st.n, st.base = at("ln_step", l, 0), b * PER[kind]["ln_step"]

                            def statistics(of, k):
                                for j in range(nt):
                                    last = V.bn_stats(stats[:, j, :], of(j))
                                st.run(last)
                                dve.sem_inc(stats_taken, 1)
                                for j in range(nt):
                                    last = V.bn_aggr(mv[:, j, :], stats[:, j, :])
                                last.then_inc(w_S("stats_ready"), 1)
                                dve.wait_ge(w_S("std_ready"), at("std_ready", l, b, k))
                                st.run(V.reciprocal(rstd[:, 0:nt], std[:, 0:nt]))

                            def normalize(of):
                                for j in range(nt):
                                    last = V.tensor_scalar(z[:, j, :], of(j), mv[:, j, 0:1], rstd[:, j:j + 1], ALU.subtract, ALU.mult)
                                return last

                            if kind != "final":
                                dve.wait_ge(w_S("y_done"), at("y_done", l, b, 1))
                            if kind in ("sage", "sage_res"):
                                statistics(y, 1)
                                normalize(y).then_inc(w_S("y_free"), 1)
                                dve.wait_ge(w_S("y_free"), at("y_free", l, b, 1))
                                st.run(V.tensor_tensor(z_, z_, lnw[:, :].unsqueeze(1).to_broadcast([TILE, nt, C]), ALU.mult))
                                V.tensor_tensor(z_, z_, lnb[:, :].unsqueeze(1).to_broadcast([TILE, nt, C]), ALU.add).then_inc(w_S("z_ready"), 1)
                            if kind == "sage":
                                dve.wait_ge(w_S("relu_ready"), at("relu_ready", l, b, 1))
                                V.scalar_tensor_tensor(pout[:, tiles, 1, :], u_, alpha[0:TILE, l + 1:l + 2], pout[:, tiles, 0, :],
                                                       ALU.mult, ALU.subtract).then_inc(w_S("parts_ready"), 1)
                                return
                            if kind == "sage_res":
                                dve.wait_ge(w_S("x0_in"), at("x0_in", l, b, 16))
                                dve.wait_ge(w_S("relu_ready"), at("relu_ready", l, b, 1))
                                st.run(V.tensor_tensor(u_, u_, x0[:, 0:nt, :], ALU.add))
                            if kind == "message":
                                dve.wait_ge(w_S("parts_ready"), at("parts_ready", l, b))
                                for j in range(nt):
                                    last = V.scalar_tensor_tensor(z[:, j, :], lnw[:, :], has_edge[:, bass.ds(b * q + j, 1)], y(j),
                                                                  ALU.mult, ALU.add)
                                last.then_inc(w_S("z_ready"), 1)
                                V.memset(stats[:, 0, 0:1], 0.0).then_inc(w_S("y_free"), 1)
                            if kind in ("message", "final"):
                                dve.wait_ge(w_S("relu_ready"), at("relu_ready", l, b, 1))
                                if kind == "final":
                                    V.memset(stats[:, 0, 0:1], 0.0).then_inc(w_S("y_free"), 1)
                                    dve.wait_ge(w_S("out_done"), at("out_done", l, b))
                                st.run(V.tensor_tensor(z_, pin[:, tiles, 0, :], pin[:, tiles, 1, :], ALU.add))
                                st.run(V.scalar_tensor_tensor(u_, z_, 1.0 / ALPHA_LN, u_, ALU.mult, ALU.add))
                            statistics(lambda j: u[:, j, :], PER[kind]["std_ready"])
                            normalize(lambda j: u[:, j, :]).then_inc(w_S("z_ready"), 1)
                            if kind == "final":
                                return
                            dve.wait_ge(w_S("relu_ready"), at("relu_ready", l, b, 2))
                            V.scalar_tensor_tensor(pout[:, tiles, 1, :], z_, ALPHA_LN, pout[:, tiles, 0, :],
                                                   ALU.mult, ALU.subtract).then_inc(w_S("parts_ready"), 1)

                        if ls[0] == 0:
                            dve.sem_inc(w_S("agg_scaled"), 1)
                            dve.sem_inc(w_S("y_free"), 1)
                            dve.wait_ge(deg_cols, 1)
                            V.tensor_scalar(has_edge[:, :], ps[6][0:TILE, 0:NT], 1.0, None, ALU.min)
                        V.memset(ones3[:, :], 1.0)
                        for n, l in enumerate(ls):
                            dve.wait_ge(layer_in, loaded(l))
                            if W_SELF[l] is not None:
                                sb_ = Steps(dve, bias_step)
                                sb_.n = BIAS_STEPS * n
                                part = [bias_part[:, i, :] for i in range(3)]
                                sb_.run(V.tensor_copy(part[0], bias[:, :]))
                                sb_.run(V.tensor_tensor(bias_rest[:, :], bias[:, :], part[0], ALU.subtract))
                                sb_.run(V.tensor_copy(part[1], bias_rest[:, :]))
                                sb_.run(V.tensor_tensor(bias_rest[:, :], bias_rest[:, :], part[1], ALU.subtract))
                                sb_.run(V.tensor_copy(part[2], bias_rest[:, :]))
                                sb_.run(V.tensor_scalar(bias_row[:, :], part[0], ident[0:3, 0:1], None, ALU.mult))
                                for i in (1, 2):
                                    sb_.run(V.scalar_tensor_tensor(bias_row[:, :], part[i], ident[0:3, i:i + 1], bias_row[:, :],
                                                                   ALU.mult, ALU.add))
                                assert sb_.n == BIAS_STEPS * (n + 1)
                            pipeline(dve, lambda b, nt, p: scale(l, b, nt, p), lambda b, nt, p: finish(l, b, nt, p))

                    @block.sync
                    def _(sp):
                        if ls[0] == 0:
                            sp.sem_inc(w_S("out_done"), 1)
                            sp.dma_start(counts_d, counts_all[0:TILE, SPILL * N:NT * N]).then_inc(counts_saved, 16)
                        for n, l in enumerate(ls):
                            if l > ls[0]:
                                sp.wait_ge(w_S("parts_ready"), at("parts_ready", l, 0))
                            sp.dma_start(wt[:, 0, :], wt_d[:, W_AGG[l], :]).then_inc(layer_in, 16)
                            if W_SELF[l] is None:
                                sp.dma_start(lnw[:, :], b1g.unsqueeze(0).to_broadcast([TILE, C])).then_inc(layer_in, 16)
                            else:
                                sp.dma_start(wt[:, 1, :], wt_d[:, W_SELF[l], :]).then_inc(layer_in, 16)
                                sp.dma_start(bias[:, :], (bl[l, :] if l < 4 else b3g).unsqueeze(0).to_broadcast([3, C])).then_inc(layer_in, 16)
                            if l < 4:
                                sp.dma_start(lnw[:, :], ln_w[l, :].unsqueeze(0).to_broadcast([TILE, C])).then_inc(layer_in, 16)
                                sp.dma_start(lnb[:, :], ln_b[l, :].unsqueeze(0).to_broadcast([TILE, C])).then_inc(layer_in, 16)
                            if KINDS[l] == "sage_res":
                                def body(b, nt):
                                    sp.wait_ge(w_S("parts_ready"), at("parts_ready", l, b))
                                    sp.dma_start(x0[:, 0:nt, :], x[bass.ds(b * BLK, nt * TILE), :].rearrange("(t p) c -> p t c", p=TILE)
                                                 ).then_inc(w_S("x0_in"), 16)
                                over_blocks(sp, body)
                            if KINDS[l] == "final":
                                def body(b, nt):
                                    sp.wait_ge(w_S("z_ready"), at("z_ready", l, b, 1))
                                    sp.dma_start(out[bass.ds(b * BLK, nt * TILE), :].rearrange("(t p) c -> p t c", p=TILE),
                                                 z[:, 0:nt, :]).then_inc(w_S("out_done"), 16)
                                over_blocks(sp, body)
                                sp.wait_ge(w_S("out_done"), at("out_done", l, NBLK, 16))

        layers([0, 1, 2, 3, 4])

        arena_at = [SPILL * N + 16 - (SPILL * N) % 16]

        def carve(shape, dt=fp32):
            lanes, dims = shape[0], shape[1:]
            n = 2 * int(np.prod(dims))
            view = counts_all[0:lanes, arena_at[0]:arena_at[0] + n].bitcast(dt)
            arena_at[0] += n + (-n) % 16
            assert arena_at[0] <= NT * N + 3
            names = "abcde"[:len(dims)]
            if len(dims) == 1:
                return view
            return view.rearrange(f"p ({' '.join(names)}) -> p {' '.join(names)}", **{k: d for k, d in zip(names, dims)})

        Q = carve([TILE, NT + 1, C])
        acc = carve([TILE, NT + 1, VW])
        arena_mid = arena_at[0]
        x2 = parts[1]

        def transposed(pe, out_ps, tiles, nt):
            for j in range(nt):
                for part in range(2):
                    last = T.matmul(out_ps[:, j * TILE:(j + 1) * TILE], x2[:, tiles + j, part, :], ident_a[0:TILE, 4, :],
                                    start=(part == 0), stop=(part == 1))
            return last

        def blocks():
            for b in range(NBLK + 1):
                yield b, b * BLK, min(BLK, N - b * BLK), b * (BLK // TILE), min(BLK, N - b * BLK) // TILE

        def column(ap):
            return ap.unsqueeze(1)

        s5 = ExitStack()
        with s5:
            t = lambda name, shape, dt: sb(name, shape, dt, s5)
            RING = 4
            kv = carve([LANES, RING, GRP, 2 * C])
            prod = carve([LANES, GRP, C])
            VA = [carve([LANES, GRP, VW]) for _ in range(2)]
            ohT = [carve([TILE, 2, GRP, LANES]) for _ in range(2)]
            oh16 = parts_all[0][:, :, :, :].rearrange("p t h c -> p (t h c)")[:, 0:4 * GRP * 2 * TILE].rearrange(
                "p (r k n) -> p r k n", r=4, k=GRP)
            oh32 = [t(f"oh32_{i}", [LANES, GRP, 2 * TILE], fp32) for i in range(2)]
            iota_n = t("iota_n", [LANES, 2 * TILE], fp16)
            ident_h = t("ident_h", [LANES, LANES], fp16)
            idx = [t(f"idx{i}", [LANES, 4 * GRP], i32) for i in range(2)]
            score = [t(f"score{i}", [LANES, GRP * HEADS], fp32) for i in range(2)]
            wtab = t("wtab", [1, 128], i32)
            srcidx = carve([LANES, CHP], i32)
            reldst = carve([LANES, CHP])
            dst_l = t("dst_l", [LANES, CH], fp32)
            qidx = t("qidx", [LANES, CH], i32)
            qidx_f = t("qidx_f", [LANES, CH], fp32)
            win_start = t("win_start", [LANES, NT], fp32)
            rel_all = t("rel_all", [LANES, NT], fp32)

            att_in = sem("att_in")
            acc_step = sem("acc_step")
            q_out_done = sem("q_out_done")
            att_consts = sem("att_consts")
            kv_in = [sem(f"kv_in{i}") for i in range(RING)]
            idx_ready = sem("idx_ready")
            pool_waits = sem("pool_waits")
            prod_ready = sem("prod_ready")
            score_sum = sem("score_sum")
            score_ready = sem("score_ready")
            a_ready = sem("a_ready")
            va_ready = sem("va_ready")
            oh_ready = sem("oh_ready")
            tr_done = sem("tr_done")
            ohT_ready = sem("ohT_ready")
            qe_done = sem("qe_done")
            oh32_ready = sem("oh32_ready")
            seg_done = sem("seg_done")
            seg_added = sem("seg_added")
            gen_idx = sem("gen_idx")
            gen_in = sem("gen_in")
            gen_score = sem("gen_score")
            gen_a = sem("gen_a")
            gen_oh = sem("gen_oh")
            gen_seg = sem("gen_seg")
            gen_added = sem("gen_added")

            arena_at[0] = arena_mid
            s4 = ExitStack()
            with s4:
                wkvq = carve([C, 3, C])
                hn_T = [carve([C, BLK]) for _ in range(2)]
                x2T = parts_all[0][:, :, :, :].rearrange("p t h c -> p (t h c)").bitcast(fp32)
                kv_out = [carve([TILE, 4, 2 * C]) for _ in range(2)]
                bst = carve([C, NBLK + 1, 6])
                bmv = carve([C, 2])
                bcol = carve([C, 8])
                bn_in = sem("bn_in")
                xb_done = sem("xb_done")
                xb_taken = sem("xb_taken")
                xb_stats = sem("xb_stats")
                bn_step = sem("bn_step")
                bn_var = sem("bn_var")
                bn_std = sem("bn_std")
                bn_ready = sem("bn_ready")
                hn_ready = sem("hn_ready")
                qkv_done = sem("qkv_done")
                kv_copied = sem("kv_copied")
                q_copied = sem("q_copied")
                kv_out_done = [sem("kv_out_done0"), sem("kv_out_done1")]
                with nc.Block() as block:
                    @block.sync
                    def _(sp):
                        sp.wait_ge(counts_saved, 16)
                        for tile, source in ((wtab[0:1, :], win_table_d), (srcidx[:, :], srcidx_d), (reldst[:, :], reldst_d),
                                             (dst_l[:, :], dstf_d[:, 0:CH])):
                            sp.dma_start(tile, source).then_inc(att_in, 16)
                        for i, w in enumerate((Wk, Wv, Wq)):
                            sp.dma_start(wkvq[:, i, :], w).then_inc(bn_in, 16)
                        sp.dma_start(bcol[:, 0:1], column(bn1_g)).then_inc(bn_in, 16)
                        sp.dma_start(bcol[:, 1:2], column(bn1_b)).then_inc(bn_in, 16)
                        for b, d0, w, t0, nt in blocks():
                            sp.wait_ge(kv_copied, t0 + nt)
                            sp.dma_start(kv_d[d0:d0 + w, :].rearrange("(t p) c -> p t c", p=TILE),
                                         kv_out[b % 2][:, 0:nt, :]).then_inc(kv_out_done[b % 2], 16)
                        sp.wait_ge(q_copied, NT)
                        sp.dma_start(q_d.rearrange("(t p) c -> p t c", p=TILE), Q[:, 0:NT, :]).then_inc(q_out_done, 16)
                        sp.wait_ge(kv_out_done[0], 16 * (NBLK // 2 + 1))
                        sp.wait_ge(kv_out_done[1], 16 * (NBLK // 2))

                    @block.gpsimd
                    def _(pool):
                        G.iota(iota_n[:, :], pattern=[[1, 2 * TILE]], base=0, channel_multiplier=0,
                               allow_small_or_imprecise_dtypes=True)
                        G.iota(win_start[:, :], pattern=[[-TILE, NT]], base=0, channel_multiplier=0,
                               allow_small_or_imprecise_dtypes=True)

                    @block.tensor
                    def _(pe):
                        for b, d0, w, t0, nt in blocks():
                            if b >= 2:
                                pe.wait_ge(xb_taken, b - 1)
                            transposed(pe, ps[b % 2], t0, nt).then_inc(xb_done, 1)
                        for b, d0, w, t0, nt in blocks():
                            if b == 0:
                                pe.wait_ge(bn_in, 80)
                            pe.wait_ge(hn_ready, b + 1)
                            for j in range(nt):
                                tile = t0 + j
                                hn = hn_T[b % 2][:, j * TILE:(j + 1) * TILE]
                                if tile >= 3:
                                    pe.wait_ge(kv_copied, tile - 2)
                                    pe.wait_ge(q_copied, tile - 2)
                                T.matmul(ps[2 + tile % 3][0:TILE, 0:2 * C], hn, wkvq[:, 0:2, :].rearrange("p w c -> p (w c)"),
                                         start=True, stop=True)
                                T.matmul(ps[5 + tile % 3][0:TILE, 0:C], hn, wkvq[:, 2, :], start=True, stop=True).then_inc(qkv_done, 1)

                    @block.vector
                    def _(dve):
                        st = Steps(dve, acc_step)
                        dve.wait_ge(counts_saved, 16)
                        st.done(V.memset(acc[:, :, :], 0.0))
                        st.done(V.memset(oh32[1][:, :, :], 0.0))
                        V.tensor_copy(ident_h[:, :], ident[:, :])
                        dve.wait_ge(att_in, 64)
                        st.run(V.tensor_scalar(qidx_f[:, :], dst_l[:, :], float(N - 1), None, ALU.min))
                        st.run(V.tensor_copy(qidx[:, :], qidx_f[:, :]))
                        st = Steps(dve, bn_step)
                        for b, d0, w, t0, nt in blocks():
                            dve.wait_ge(xb_taken, b + 1)
                            V.bn_stats(bst[:, b, :], x2T[:, d0:d0 + w]).then_inc(xb_stats, 1)
                        dve.wait_ge(xb_stats, NBLK + 1)
                        V.bn_aggr(bmv[:, :], bst[:, :, :].rearrange("p b s -> p (b s)")).then_inc(bn_var, 1)
                        dve.wait_ge(bn_var, 1)
                        dve.wait_ge(bn_std, 1)
                        dve.wait_ge(bn_in, 80)
                        st.run(V.reciprocal(bcol[:, 3:4], bcol[:, 2:3]))
                        st.run(V.tensor_tensor(bcol[:, 4:5], bcol[:, 3:4], bcol[:, 0:1], ALU.mult))
                        st.run(V.tensor_tensor(bcol[:, 6:7], bmv[:, 0:1], bcol[:, 4:5], ALU.mult))
                        V.tensor_tensor(bcol[:, 5:6], bcol[:, 1:2], bcol[:, 6:7], ALU.subtract).then_inc(bn_ready, 1)
                        V.memset(Q[:, NT, :], 0.0)
                        for b, d0, w, t0, nt in blocks():
                            for j in range(nt):
                                dve.wait_ge(qkv_done, t0 + j + 1)
                                V.tensor_scalar(Q[:, t0 + j, :], ps[5 + (t0 + j) % 3][0:TILE, 0:C], 1.0 / float(np.sqrt(HD)),
                                                None, ALU.mult).then_inc(q_copied, 1)

                    @block.scalar
                    def _(act):
                        for b, d0, w, t0, nt in blocks():
                            act.wait_ge(xb_done, b + 1)
                            S.copy(x2T[:, d0:d0 + w], ps[b % 2][:, 0:w]).then_inc(xb_taken, 1)
                        act.wait_ge(bn_var, 1)
                        S.activation(bcol[:, 2:3], bmv[:, 1:2], ACT.Sqrt, bias=eps_t[:, 0:1]).then_inc(bn_std, 1)
                        act.wait_ge(bn_ready, 1)
                        act.wait_ge(xb_taken, NBLK + 1)
                        every = list(blocks())

                        def norm(b, d0, w):
                            if b >= 2:
                                act.wait_ge(qkv_done, 4 * (b - 1))
                            S.activation(hn_T[b % 2][:, 0:w], x2T[:, d0:d0 + w], ACT.Identity,
                                         scale=bcol[:, 4:5], bias=bcol[:, 5:6]).then_inc(hn_ready, 1)

                        norm(*every[0][:3])
                        for b, d0, w, t0, nt in every:
                            if b < NBLK:
                                norm(*every[b + 1][:3])
                            if b >= 2:
                                act.wait_ge(kv_out_done[b % 2], 16 * (b // 2))
                            for j in range(nt):
                                act.wait_ge(qkv_done, t0 + j + 1)
                                S.copy(kv_out[b % 2][:, j, :], ps[2 + (t0 + j) % 3][0:TILE, 0:2 * C]).then_inc(kv_copied, 1)

            def windows_spanned(engine):
                return load_registers(nc, engine, wtab[0:1, 124:128], NT)[3]

            with nc.Block() as block:
                @block.sync
                def _(sp):
                    sp.wait_ge(q_out_done, 16)

                @block.gpsimd
                def _(pool):
                    wide = windows_spanned(ET.Pool)

                    def gather(out_rows, table_d, index, signal):
                        G.indirect_dma_start(out=out_rows, out_offset=None, in_=table_d,
                                             in_offset=bass.IndirectOffsetOnAxis(ap=index, axis=0)).then_inc(signal, 16)

                    with pool.If(wide <= 1):
                        with pool.Fori(0, NG // (2 * RING)) as i:
                            for h in range(2):
                                g0 = i * 2 * RING + h * RING
                                pool.wait_ge(va_ready, g0)
                                pool.sem_inc(pool_waits, 1)
                                G.tensor_copy(idx[h][:, :], srcidx[:, bass.ds(i * (2 * RING * GRP) + h * RING * GRP, RING * GRP)]
                                              ).then_inc(idx_ready, 1)
                                pool.wait_ge(idx_ready, i * 2 + h + 1)
                                pool.sem_inc(pool_waits, 1)
                                for r in range(RING):
                                    pool.wait_ge(va_ready, g0 + r + 1)
                                    pool.sem_inc(pool_waits, 1)
                                    for k in range(GRP):
                                        gather(kv[:, r, k, :], kv_d, idx[h][:, r * GRP + k:r * GRP + k + 1], kv_in[r])
                    with pool.Else():
                        pool.wait_ge(oh_ready, 1)
                        with pool.Fori(0, CH) as c:
                            pool.wait_ge(gen_added, c * NT)
                            pool.sem_inc(pool_waits, 1)
                            G.tensor_copy(idx[0][:, 0:1], srcidx[:, bass.ds(c, 1)]).then_inc(gen_idx, 1)
                            G.tensor_copy(idx[0][:, 1:2], qidx[:, bass.ds(c, 1)]).then_inc(gen_idx, 1)
                            pool.wait_ge(gen_idx, c * 2 + 2)
                            pool.sem_inc(pool_waits, 1)
                            gather(kv[:, 0, 0, :], kv_d, idx[0][:, 0:1], gen_in)
                            gather(kv[:, 0, 1, 0:C], q_d, idx[0][:, 1:2], gen_in)

                @block.vector
                def _(dve):
                    wide = windows_spanned(ET.DVE)
                    V.memset(VA[1][:, :, :], 0.0)
                    V.memset(ps[4][:, :], 0.0).then_inc(att_consts, 1)
                    dve.wait_ge(att_consts, 1)

                    def one_hots(column, place):
                        for k in range(GRP):
                            last = V.tensor_scalar(oh16[:, place, k, :], iota_n[:, :], reldst[:, bass.ds(column + k, 1)],
                                                   None, ALU.is_equal)
                        last.then_inc(oh_ready, 1)

                    def add(w0, bank, added):
                        dve.wait_ge(seg_added, added)
                        V.tensor_tensor(acc[:, bass.ds(w0, 2), :], acc[:, bass.ds(w0, 2), :],
                                        ps[4 + bank][0:TILE, 0:2 * VW].rearrange("p (w c) -> p w c", w=2),
                                        ALU.add).then_inc(seg_added, 1)

                    with dve.If(wide <= 1):
                        dve.sem_inc(va_ready, RING)
                        one_hots(0, 0)
                        one_hots(GRP, 1)
                        with dve.Fori(0, NG // 4) as i:
                            w0 = load_registers(nc, ET.DVE, wtab[0:1, bass.ds(i * 4, 4)], NT - 1)
                            for r in range(4):
                                g = i * 4 + r
                                dve.wait_ge(kv_in[r], (i + 1) * 16 * GRP)
                                dve.wait_ge(qe_done, g + 1)
                                dve.wait_ge(score_sum, g)
                                V.tensor_tensor(prod[:, :, :], kv[:, r, :, 0:C],
                                                ps[2 + r % 2][:, 0:GRP * C].rearrange("p (k c) -> p k c", k=GRP),
                                                ALU.mult).then_inc(prod_ready, 1)
                                dve.wait_ge(prod_ready, g + 1)
                                V.tensor_reduce(out=score[r % 2][:, :], in_=prod[:, :, :].rearrange("p k (h c) -> p (k h) c", h=HEADS),
                                                axis=AX.X, op=ALU.add).then_inc(score_sum, 1)
                                dve.wait_ge(score_sum, g + 1)
                                V.tensor_scalar(score[r % 2][:, :], score[r % 2][:, :], 5.0, -5.0, ALU.min, ALU.max).then_inc(score_ready, 1)
                                dve.wait_ge(seg_done, g)
                                add(w0[r], r % 2, g)
                                one_hots((g + 2) * GRP, (r + 2) % 4)
                                dve.wait_ge(a_ready, g + 1)
                                V.tensor_tensor(VA[r % 2][:, :, 0:C].rearrange("p k (h c) -> p k h c", h=HEADS),
                                                kv[:, r, :, C:2 * C].rearrange("p k (h c) -> p k h c", h=HEADS),
                                                VA[r % 2][:, :, C:VW].unsqueeze(3).to_broadcast([LANES, GRP, HEADS, HD]),
                                                ALU.mult).then_inc(va_ready, 1)
                        w0 = load_registers(nc, ET.DVE, wtab[0:1, NG:NG + 4], NT - 1)
                        for r in range(2):
                            dve.wait_ge(seg_done, NG + r)
                            add(w0[r], r, NG + r)
                    with dve.Else():
                        dve.sem_inc(oh_ready, 1)
                        with dve.Fori(0, CH) as c:
                            dve.wait_ge(gen_in, (c + 1) * 32)
                            V.tensor_tensor(prod[:, 0, :], kv[:, 0, 0, 0:C], kv[:, 0, 1, 0:C], ALU.mult).then_inc(prod_ready, 1)
                            V.tensor_scalar(rel_all[:, :], win_start[:, :], dst_l[:, bass.ds(c, 1)], None, ALU.add)
                            dve.wait_ge(prod_ready, c + 1)
                            V.tensor_reduce(out=score[0][:, 0:HEADS], in_=prod[:, 0, :].rearrange("p (h c) -> p h c", h=HEADS),
                                            axis=AX.X, op=ALU.add).then_inc(score_sum, 1)
                            dve.wait_ge(score_sum, c + 1)
                            V.tensor_scalar(score[0][:, 0:HEADS], score[0][:, 0:HEADS], 5.0, -5.0, ALU.min, ALU.max).then_inc(gen_score, 1)
                            dve.wait_ge(gen_a, c + 1)
                            V.tensor_tensor(VA[0][:, 0, 0:C].rearrange("p (h c) -> p h c", h=HEADS),
                                            kv[:, 0, 0, C:2 * C].rearrange("p (h c) -> p h c", h=HEADS),
                                            VA[0][:, 0, C:VW].unsqueeze(2).to_broadcast([LANES, HEADS, HD]), ALU.mult)
                            with dve.Fori(0, NT) as w:
                                dve.wait_ge(gen_added, c * NT + w)
                                V.tensor_scalar(oh32[0][:, 0, 0:TILE], iota_n[:, 0:TILE], rel_all[:, bass.ds(w, 1)], None,
                                                ALU.is_equal).then_inc(gen_oh, 1)
                                dve.wait_ge(gen_seg, c * NT + w + 1)
                                V.tensor_tensor(acc[:, bass.ds(w, 1), :], acc[:, bass.ds(w, 1), :],
                                                ps[4][0:TILE, 0:VW].unsqueeze(1), ALU.add).then_inc(gen_added, 1)

                @block.tensor
                def _(pe):
                    pe.wait_ge(att_consts, 1)
                    wide = windows_spanned(ET.PE)

                    def turn(place, n):
                        pe.wait_ge(oh_ready, n + 1)
                        bank = ps[place % 2][:, :].bitcast(fp16)
                        for w in range(2):
                            for k in range(GRP):
                                last = T.transpose(bank[0:TILE, (w * GRP + k) * LANES:(w * GRP + k + 1) * LANES],
                                                   oh16[:, place, k, w * TILE:(w + 1) * TILE], ident_h[:, :])
                        last.then_inc(tr_done, 1)

                    def pick(place, n, w0):
                        pe.wait_ge(ohT_ready, n + 1)
                        for k in range(GRP):
                            for w in range(2):
                                last = T.matmul(ps[2 + place % 2][:, k * C:(k + 1) * C], ohT[place % 2][:, w, k, :],
                                                Q[:, bass.ds(w0 + w, 1), :].rearrange("p w c -> p (w c)"), start=(w == 0), stop=(w == 1))
                        last.then_inc(qe_done, 1)

                    def sums(place, n):
                        pe.wait_ge(va_ready, RING + n + 1)
                        pe.wait_ge(oh32_ready, n + 1)
                        pe.wait_ge(seg_added, n + 1)
                        for w in range(2):
                            for k in range(GRP):
                                last = T.matmul(ps[4 + place % 2][0:TILE, w * VW:(w + 1) * VW],
                                                oh32[place % 2][:, k, w * TILE:(w + 1) * TILE], VA[place % 2][:, k, :],
                                                start=(k == 0), stop=(k == GRP - 1))
                        last.then_inc(seg_done, 1)

                    with pe.If(wide <= 1):
                        w0 = load_registers(nc, ET.PE, wtab[0:1, 0:4], NT - 1)
                        for r in range(2):
                            turn(r, r)
                            pick(r, r, w0[2 + r])
                        with pe.Fori(0, NG // 4) as i:
                            w0 = load_registers(nc, ET.PE, wtab[0:1, bass.ds(i * 4 + 4, 4)], NT - 1)
                            for r in range(4):
                                g = i * 4 + r
                                pe.wait_ge(ohT_ready, g + 1)
                                turn((r + 2) % 4, g + 2)
                                sums(r + 3, g - 1)
                                pe.wait_ge(prod_ready, g + 1)
                                pick((r + 2) % 4, g + 2, w0[r])
                        sums(3, NG - 1)
                    with pe.Else():
                        with pe.Fori(0, CH) as c:
                            with pe.Fori(0, NT) as w:
                                pe.wait_ge(gen_oh, c * NT + w + 1)
                                T.matmul(ps[4][0:TILE, 0:VW], oh32[0][:, 0, 0:TILE], VA[0][:, 0, :], start=True,
                                         stop=True).then_inc(gen_seg, 1)

                @block.scalar
                def _(act):
                    wide = windows_spanned(ET.Activation)

                    def copy_turned(place, n):
                        act.wait_ge(tr_done, n + 1)
                        S.copy(ohT[place % 2][:, :, :, :].rearrange("p w k n -> p (w k n)"),
                               ps[place % 2][:, :].bitcast(fp16)[0:TILE, :]).then_inc(ohT_ready, 1)

                    def widen(place, n):
                        act.wait_ge(oh_ready, n + 1)
                        S.copy(oh32[place % 2][:, :, :], oh16[:, place, :, :]).then_inc(oh32_ready, 1)

                    with act.If(wide <= 1):
                        copy_turned(0, 0)
                        copy_turned(1, 1)
                        widen(0, 0)
                        with act.Fori(0, NG // 4) as i:
                            for r in range(4):
                                g = i * 4 + r
                                act.wait_ge(score_ready, g + 1)
                                act.wait_ge(seg_done, g)
                                S.activation(VA[r % 2][:, :, C:VW], score[r % 2][:, :].rearrange("p (k h) -> p k h", h=HEADS),
                                             ACT.Exp).then_inc(a_ready, 1)
                                act.wait_ge(qe_done, g + 1)
                                copy_turned(r + 2, g + 2)
                                act.wait_ge(seg_done, g + 1)
                                widen((r + 1) % 4, g + 1)
                    with act.Else():
                        with act.Fori(0, CH) as c:
                            act.wait_ge(gen_score, c + 1)
                            S.activation(VA[0][:, 0, C:VW], score[0][:, 0:HEADS], ACT.Exp).then_inc(gen_a, 1)

        arena_at[0] = arena_mid
        s6 = ExitStack()
        with s6:
            t = lambda name, shape, dt: sb(name, shape, dt, s6)
            wvT = [carve([C, BLK]) for _ in range(2)]
            h2T = parts_all[0][:, :, :, :].rearrange("p t h c -> p (t h c)").bitcast(fp32)
            rden = carve([TILE, NT, HEADS])
            wo = carve([C, C])
            w1 = t("w1", [C, 2 * C], fp32)
            w2 = t("w2", [C, 2, C], fp32)
            b2_row = t("b2_row", [1, C], fp32)
            hn = t("hn", [C, BLK], fp32)
            hid = [t(f"hid{i}", [C, 2, BLK], fp32) for i in range(2)]
            u = t("u6", [TILE, BLK // TILE, C], fp32)
            bst = t("bst6", [C, NBLK + 1, 6], fp32)
            bmv = t("bmv6", [C, 2], fp32)
            bcol = t("bcol6", [C, 10], fp32)
            stats = t("stats6", [TILE, 4, 6], fp32)
            mv = t("mv6", [TILE, 4, 2], fp32)
            std = t("std6", [TILE, 4], fp32)
            rstd = t("rstd6", [TILE, 4], fp32)
            ff_in = sem("ff_in")
            rden_step = sem("rden_step")
            wv_ready = sem("wv_ready")
            wvt_done = sem("wvt_done")
            wvt_copied = sem("wvt_copied")
            h2_done = sem("h2_done")
            h2_copied = sem("h2_copied")
            h2_stats = sem("h2_stats")
            bn2_step = sem("bn2_step")
            bn2_var = sem("bn2_var")
            bn2_std = sem("bn2_std")
            bn2_ready = sem("bn2_ready")
            hn2_ready = sem("hn2_ready")
            hid_done = sem("hid_done")
            hid_copied = sem("hid_copied")
            ff_done = sem("ff_done")
            u_ready = sem("u_ready")
            u_stats = sem("u_stats")
            u_std = sem("u_std")
            u_normed = sem("u_normed")
            hi_ready = sem("hi_ready")
            u_step = sem("u_step")
            counts_back = sem("counts_back")
            with nc.Block() as block:
                @block.sync
                def _(sp):
                    sp.dma_start(wo[:, :], Wo).then_inc(ff_in, 16)
                    sp.dma_start(w1[:, :], W1).then_inc(ff_in, 16)
                    sp.dma_start(w2[:, :, :], W2.rearrange("(j f) c -> f j c", j=2)).then_inc(ff_in, 16)
                    sp.dma_start(b2_row[0:1, :], b2.unsqueeze(0)).then_inc(ff_in, 16)
                    for i, col in ((0, bn2_g), (1, bn2_b), (7, bo), (8, b1[0:C]), (9, b1[C:2 * C])):
                        sp.dma_start(bcol[:, i:i + 1], column(col)).then_inc(ff_in, 16)
                    sp.wait_ge(h2_copied, NBLK + 1)
                    sp.dma_start(counts_all[0:TILE, SPILL * N:NT * N], counts_d).then_inc(counts_back, 16)
                    sp.wait_ge(counts_back, 16)

                @block.tensor
                def _(pe):
                    def turn(b, nt, t0):
                        pe.wait_ge(wv_ready, b + 1)
                        if b >= 2:
                            pe.wait_ge(wvt_copied, b - 1)
                        for j in range(nt):
                            last = T.transpose(ps[b % 2][:, j * TILE:(j + 1) * TILE], acc[:, t0 + j, 0:C], ident[0:TILE, 0:TILE])
                        last.then_inc(wvt_done, 1)

                    def hidden(b, w):
                        pe.wait_ge(hn2_ready, b + 1)
                        if b:
                            pe.wait_ge(hid_copied, b)
                        for j in range(2):
                            last = T.matmul(ps[4 + j][:, 0:w], w1[:, j * C:(j + 1) * C], hn[:, 0:w], start=True, stop=True)
                        last.then_inc(hid_done, 1)

                    every = list(blocks())
                    pe.wait_ge(ff_in, 16 * 9)
                    turn(0, 4, 0)
                    for b, d0, w, t0, nt in every:
                        if b < NBLK:
                            turn(b + 1, every[b + 1][4], every[b + 1][3])
                        pe.wait_ge(wvt_copied, b + 1)
                        if b >= 2:
                            pe.wait_ge(h2_copied, b - 1)
                        for j in range(nt):
                            o = ps[2 + b % 2][:, j * TILE:(j + 1) * TILE]
                            T.matmul(o, wo[:, :], wvT[b % 2][:, j * TILE:(j + 1) * TILE], start=True, stop=False)
                            for part in range(2):
                                last = T.matmul(o, x2[:, t0 + j, part, :], ident_a[0:TILE, 4, :], start=False, stop=(part == 1))
                        last.then_inc(h2_done, 1)
                    hidden(0, BLK)
                    for b, d0, w, t0, nt in every:
                        if b < NBLK:
                            hidden(b + 1, every[b + 1][2])
                        pe.wait_ge(hid_copied, b + 1)
                        if b >= 2:
                            pe.wait_ge(u_ready, b - 1)
                        for j in range(nt):
                            y = ps[6 + b % 2][0:TILE, j * C:(j + 1) * C]
                            cols = slice(j * TILE, (j + 1) * TILE)
                            T.matmul(y, hid[b % 2][:, 0, cols], w2[:, 0, :], start=True, stop=False)
                            T.matmul(y, hid[b % 2][:, 1, cols], w2[:, 1, :], start=False, stop=False)
                            T.matmul(y, h2T[:, d0 + j * TILE:d0 + (j + 1) * TILE], ident[:, :], start=False, stop=False)
                            last = T.matmul(y, ones_row[0:1, :], b2_row[0:1, :], start=False, stop=True)
                        last.then_inc(ff_done, 1)

                @block.scalar
                def _(act):
                    act.wait_ge(ff_in, 16 * 9)
                    for b, d0, w, t0, nt in blocks():
                        act.wait_ge(wvt_done, b + 1)
                        if b >= 2:
                            act.wait_ge(h2_done, b - 1)
                        S.copy(wvT[b % 2][:, 0:w], ps[b % 2][:, 0:w]).then_inc(wvt_copied, 1)
                        act.wait_ge(h2_done, b + 1)
                        S.activation(h2T[:, d0:d0 + w], ps[2 + b % 2][:, 0:w], ACT.Identity, bias=bcol[:, 7:8]).then_inc(h2_copied, 1)
                    act.wait_ge(bn2_var, 1)
                    S.activation(bcol[:, 2:3], bmv[:, 1:2], ACT.Sqrt, bias=eps_t[:, 0:1]).then_inc(bn2_std, 1)
                    act.wait_ge(bn2_ready, 1)
                    act.wait_ge(h2_copied, NBLK + 1)
                    every = list(blocks())

                    def norm(b, d0, w):
                        if b:
                            act.wait_ge(hid_done, b)
                        S.activation(hn[:, 0:w], h2T[:, d0:d0 + w], ACT.Identity, scale=bcol[:, 4:5],
                                     bias=bcol[:, 5:6]).then_inc(hn2_ready, 1)

                    def relu(b, w):
                        act.wait_ge(hid_done, b + 1)
                        if b >= 2:
                            act.wait_ge(ff_done, b - 1)
                        for j in range(2):
                            last = S.activation(hid[b % 2][:, j, 0:w], ps[4 + j][:, 0:w], ACT.Relu, bias=bcol[:, 8 + j:9 + j])
                        last.then_inc(hid_copied, 1)

                    norm(*every[0][:3])
                    relu(0, BLK)
                    norm(*every[1][:3])
                    for b, d0, w, t0, nt in every:
                        if b < NBLK:
                            relu(b + 1, every[b + 1][2])
                        if b < NBLK - 1:
                            norm(*every[b + 2][:3])
                        act.wait_ge(u_stats, b + 1)
                        S.activation(std[:, 0:nt], mv[:, 0:nt, 1], ACT.Sqrt, bias=eps_t[0:TILE, 0:1]).then_inc(u_std, 1)
                        act.wait_ge(u_normed, b + 1)
                        S.activation(x2[:, t0:t0 + nt, 0, :], u[:, 0:nt, :], ACT.Copy, scale=ALPHA_LN).then_inc(hi_ready, 1)

                @block.vector
                def _(dve):
                    st = Steps(dve, rden_step)
                    st.run(V.tensor_scalar(rden[:, :, :], acc[:, 0:NT, C:VW], 1e-30, None, ALU.max))
                    st.run(V.reciprocal(rden[:, :, :], rden[:, :, :]))
                    for b, d0, w, t0, nt in blocks():
                        wv = acc[:, t0:t0 + nt, 0:C].rearrange("p t (h c) -> p t h c", h=HEADS)
                        V.tensor_tensor(wv, wv, rden[:, t0:t0 + nt, :].unsqueeze(3).to_broadcast([TILE, nt, HEADS, HD]),
                                        ALU.mult).then_inc(wv_ready, 1)
                    for b, d0, w, t0, nt in blocks():
                        dve.wait_ge(h2_copied, b + 1)
                        V.bn_stats(bst[:, b, :], h2T[:, d0:d0 + w]).then_inc(h2_stats, 1)
                    dve.wait_ge(h2_stats, NBLK + 1)
                    V.bn_aggr(bmv[:, :], bst[:, :, :].rearrange("p b s -> p (b s)")).then_inc(bn2_var, 1)
                    dve.wait_ge(bn2_var, 1)
                    dve.wait_ge(bn2_std, 1)
                    dve.wait_ge(ff_in, 16 * 9)
                    s2_ = Steps(dve, bn2_step)
                    s2_.run(V.reciprocal(bcol[:, 3:4], bcol[:, 2:3]))
                    s2_.run(V.tensor_tensor(bcol[:, 4:5], bcol[:, 3:4], bcol[:, 0:1], ALU.mult))
                    s2_.run(V.tensor_tensor(bcol[:, 6:7], bmv[:, 0:1], bcol[:, 4:5], ALU.mult))
                    V.tensor_tensor(bcol[:, 5:6], bcol[:, 1:2], bcol[:, 6:7], ALU.subtract).then_inc(bn2_ready, 1)
                    s3_ = Steps(dve, u_step)
                    for b, d0, w, t0, nt in blocks():
                        u_ = u[:, 0:nt, :]
                        s3_.run(V.tensor_tensor(u_, x2[:, t0:t0 + nt, 0, :], x2[:, t0:t0 + nt, 1, :], ALU.add))
                        dve.wait_ge(ff_done, b + 1)
                        V.scalar_tensor_tensor(u_, u_, 1.0 / ALPHA_LN,
                                               ps[6 + b % 2][0:TILE, 0:nt * C].rearrange("p (j c) -> p j c", c=C),
                                               ALU.mult, ALU.add).then_inc(u_ready, 1)
                        dve.wait_ge(u_ready, b + 1)
                        for j in range(nt):
                            last = V.bn_stats(stats[:, j, :], u[:, j, :])
                        s3_.run(last)
                        for j in range(nt):
                            last = V.bn_aggr(mv[:, j, :], stats[:, j, :])
                        last.then_inc(u_stats, 1)
                        dve.wait_ge(u_std, b + 1)
                        s3_.run(V.reciprocal(rstd[:, 0:nt], std[:, 0:nt]))
                        for j in range(nt):
                            last = V.tensor_scalar(u[:, j, :], u[:, j, :], mv[:, j, 0:1], rstd[:, j:j + 1], ALU.subtract, ALU.mult)
                        last.then_inc(u_normed, 1)
                        dve.wait_ge(hi_ready, b + 1)
                        s3_.run(V.scalar_tensor_tensor(x2[:, t0:t0 + nt, 1, :], u_, ALPHA_LN, x2[:, t0:t0 + nt, 0, :],
                                                       ALU.mult, ALU.subtract))
        layers([5])


_INS = ["x", "src", "dst", "L0_gnn_Wl", "L0_gnn_bl", "L0_gnn_Wr", "L0_gnn_ln_w", "L0_gnn_ln_b", "L1_gnn_W", "L1_gnn_b",
        "L2_gnn_Wq", "L2_gnn_Wk", "L2_gnn_Wv", "L2_gnn_Wo", "L2_gnn_bo", "L2_gnn_bn1_g", "L2_gnn_bn1_b",
        "L2_gnn_bn2_g", "L2_gnn_bn2_b", "L2_gnn_W1", "L2_gnn_b1", "L2_gnn_W2", "L2_gnn_b2", "L3_gnn_W", "L3_gnn_b"]


def kernel(**inputs):
    import concourse.bacc as bacc
    from concourse.bass_utils import run_bass_kernel_spmd

    nc = bacc.Bacc("TRN2", target_bir_lowering=False, num_devices=1)
    arrays, args = {}, []
    for name in _INS:
        a = np.ascontiguousarray(inputs[name])
        arrays[f"in_{name}"] = a
        args.append(nc.dram_tensor(f"in_{name}", a.shape, mybir.dt.from_np(a.dtype), kind="ExternalInput").ap())
    out = nc.dram_tensor("out", (N, C), fp32, kind="ExternalOutput").ap()
    build(nc, *args, out)
    return run_bass_kernel_spmd(nc, [arrays], core_ids=[0]).results[0]["out"]
```

```python
import numpy as np
import concourse.bass as bass
from concourse import mybir
from contextlib import ExitStack, contextmanager

fp32, fp16, bf16, i32 = mybir.dt.float32, mybir.dt.float16, mybir.dt.bfloat16, mybir.dt.int32
ALU = mybir.AluOpType
ACT = mybir.ActivationFunctionType
AX = mybir.AxisListType

N, E, C = 3125, 53125, 128
HEADS, HD = 8, 16
TILE = 125
NT = N // TILE
LANES = 128
CH = -(-E // LANES)
CHP = CH + 24
ROWS, ROWG = 104, CH // 104
NO_NODE = 4000.0
BWN = 25
BW = N // BWN
BKEYS = BWN * NT
BHALF = 13 * NT
BK = 5
AK = 2
DS = 5
DW = 4 * BWN
CHUNK_OFF = 60000
BLK = 500
NBLK = N // BLK
EPS = 1e-5
GRP = 4
NG = CH // GRP
VW = C + HEADS
SPILL = 15
ALPHA_LN = 4096.0
LN_BOUND = 11.4


FIRSTS_CLAMPED = "a first chunk is a minimum over chunk numbers from 0, and at most CH - 1 by its last step"
WINDOWS_CLAMPED = "a first window is a target node's tile, and the padding's entries are 0"


class Steps:

    def __init__(self, eng, sem):
        self.eng, self.sem, self.n, self.base = eng, sem, 0, 0

    def done(self, ins):
        ins.then_inc(self.sem, 1)
        self.n += 1

    def wait(self):
        self.eng.wait_ge(self.sem, self.base + self.n)

    def run(self, ins):
        self.done(ins)
        self.wait()

    @contextmanager
    def loop(self, count, per):
        n0, base0 = self.n, self.base
        with self.eng.Fori(0, count) as i:
            self.base = base0 + i * per
            yield i
            assert self.n - n0 == per, (self.n - n0, per)
        self.base = base0
        self.n = n0 + per * count


def load_registers(nc, engine, row, hi, in_range=None):
    _, vals = nc.values_load_multi_w_load_instructions(row, engines=[engine], min_val=0, max_val=hi,
                                                       skip_runtime_bounds_check_because=in_range)
    return vals


def build(nc, x, src, dst, Wl, bl, Wr, ln_w, ln_b, W1g, b1g, Wq, Wk, Wv, Wo, bo, bn1_g, bn1_b,
          bn2_g, bn2_b, W1, b1, W2, b2, W3g, b3g, out):
    ET = mybir.EngineType
    V, S, G, T = nc.vector, nc.scalar, nc.gpsimd, nc.tensor
    dram = lambda name, shape, dt: nc.dram_tensor(name, shape, dt, kind="Internal").ap()
    deg_d = dram("deg_d", (N,), fp32)
    build_table_d = dram("build_table_d", (BW, 4), i32)
    key_d = dram("key_d", (LANES, CHP), fp32)
    sl_d = dram("sl_d", (LANES, CHP), fp32)
    wt_d = dram("wt_d", (C, 10, C), fp32)
    srcidx_d = dram("srcidx_d", (LANES, CHP), i32)
    dstf_d = dram("dstf_d", (LANES, CHP), fp32)
    reldst_d = dram("reldst_d", (LANES, CHP), fp32)
    win_table_d = dram("win_table_d", (1, 128), i32)
    kv_d = dram("kv_d", (N, 2 * C), fp32)
    q_d = dram("q_d", (N, C), fp32)
    counts_d = dram("counts_d", (TILE, (NT - SPILL) * N), fp16)

    ctx = ExitStack()
    with ctx:
        def sb(name, shape, dt, scope=ctx):
            return scope.enter_context(nc.sbuf_tensor(name, shape, dt))

        def sem(name):
            return ctx.enter_context(nc.semaphore(name))

        ps = [ctx.enter_context(nc.psum_tensor(f"bank{i}", [128, 512], fp32)) for i in range(8)]

        ident = sb("ident", [128, 128], fp32)
        alpha = sb("alpha", [128, 8], fp32)
        inv_alpha = sb("inv_alpha", [128, 8], fp32)
        ident_a = sb("ident_a", [128, 5, TILE], bf16)
        eps_t = sb("eps_t", [128, 1], fp32)
        has_edge = sb("has_edge", [TILE, NT], fp32)
        parts_all = [sb(f"parts{i}", [128, NT, 2, C], fp16) for i in range(2)]  
        parts = [p[0:TILE] for p in parts_all]
        inv_deg = sb("inv_deg", [128, NT * C], fp32)
        xf = inv_deg[0:TILE, :].rearrange("p (t c) -> p t c", c=C)

        s1 = ExitStack()
        with s1:
            t = lambda name, shape, dt: sb(name, shape, dt, s1)
            src_rows = t("src_rows", [ROWS, ROWG, LANES], i32)
            dst_rows = t("dst_rows", [ROWS, ROWG, LANES], i32)
            src_rf = t("src_rf", [ROWS, ROWG, LANES], fp32)
            dst_rf = t("dst_rf", [ROWS, ROWG, LANES], fp32)
            real = t("real", [ROWS, ROWG, LANES], fp32)
            mm = t("mm", [ROWS, 2, ROWG], fp32)
            diag = t("diag", [ROWS, 2, ROWG, ROWS], fp32)
            ones = t("ones", [128, 128], fp32)
            iota_f = t("iota_f", [128, 128], fp32)
            iota_p = t("iota_p", [128, 1], fp32)
            iota_c1 = t("iota_c1", [128, CH], fp32)
            tri = t("tri", [128, 128], fp32)
            win = t("win", [128, 2], fp32)
            hit1 = t("hit1", [128, CH], fp32)
            hit = t("hit", [128, CH], fp32)
            cand = t("cand", [128, CH], fp32)
            cand2 = t("cand2", [128, CH], fp32)
            lohi = t("lohi", [128, 8], fp32)
            ng_i = t("ng_i", [128, 2], i32)
            tab_i = t("tab_i", [128, 4], i32)
            srcN = t("srcN", [LANES, CHP], fp32)
            dstN = t("dstN", [LANES, CHP], fp32)
            src_i = t("src_i", [LANES, CHP], i32)
            shi = t("shi", [LANES, CHP], i32)
            shf = t("shf", [LANES, CHP], fp32)
            fix = t("fix", [LANES, CHP], fp32)
            slN0 = t("slN0", [LANES, CHP], fp32)
            keyN0 = t("keyN0", [LANES, CHP], fp32)
            w_raw = t("w_raw", [128, 10, C], fp32)
            lnw_all = t("lnw_all", [128, 4, C], fp32)
            lnb_all = t("lnb_all", [128, 4, C], fp32)
            absmax = t("absmax", [128, 16], fp32)
            absmax_r = t("absmax_r", [128, 16], fp32)
            bound = t("bound", [128, 8], fp32)
            WT = t("WT", [128, 10, C], fp32)

            rows_cleared = sem("rows_cleared")
            edges_in = sem("edges_in")
            x_in = sem("x_in")
            w_in = sem("w_in")
            consts_ready = sem("consts_ready")
            setup_step = sem("setup_step")
            edges_f = sem("edges_f")
            edges_t = sem("edges_t")
            diag_ready = sem("diag_ready")
            minmax_bc = sem("minmax_bc")
            ng_ready = sem("ng_ready")
            base_ready = sem("base_ready")
            wt_done = sem("wt_done")
            wt_copied = sem("wt_copied")
            absmax_ready = sem("absmax_ready")
            absmax_all = sem("absmax_all")
            alpha_ready = sem("alpha_ready")
            setup_out = sem("setup_out")
            keys_ready = sem("keys_ready")
            table_ready = sem("table_ready")
            table_out = sem("table_out")

            with nc.Block() as block:
                @block.sync
                def _(sp):
                    for rows, arr in ((dst_rows, dst), (src_rows, src)):
                        n3 = (ROWG - 1) * ROWS * LANES
                        sp.dma_start(rows[:, 0:ROWG - 1, :],
                                     arr[0:n3].rearrange("(t r p) -> r t p", r=ROWS, p=LANES)).then_inc(edges_in, 16)
                        full = (E - n3) // LANES
                        sp.wait_ge(rows_cleared, 1)
                        sp.dma_start(rows[0:full, ROWG - 1, :],
                                     arr[n3:n3 + full * LANES].rearrange("(r p) -> r p", p=LANES)).then_inc(edges_in, 16)
                        rest = E - n3 - full * LANES
                        sp.dma_start(rows[full:full + 1, ROWG - 1, 0:rest],
                                     arr[E - rest:E].unsqueeze(0)).then_inc(edges_in, 16)
                    sp.dma_start(xf[:, :, :], x.rearrange("(t p) c -> p t c", p=TILE)).then_inc(x_in, 16)
                    sp.wait_ge(keys_ready, 1)
                    sp.dma_start(key_d, keyN0[:, :]).then_inc(setup_out, 16)
                    sp.dma_start(sl_d, slN0[:, :]).then_inc(setup_out, 16)
                    sp.dma_start(srcidx_d, src_i[:, :]).then_inc(setup_out, 16)
                    sp.dma_start(dstf_d, dstN[:, :]).then_inc(setup_out, 16)
                    sp.wait_ge(table_ready, 1)
                    sp.dma_start(build_table_d, tab_i[0:BW, :]).then_inc(table_out, 16)
                    sp.wait_ge(wt_copied, 3)
                    sp.dma_start(wt_d, WT[:, :, :]).then_inc(setup_out, 16)
                    sp.wait_ge(table_out, 16)
                    sp.wait_ge(setup_out, 80)

                @block.scalar
                def _(act):
                    act.dma_start(w_raw[:, 0:4, :], Wl.rearrange("l o c -> o l c")).then_inc(w_in, 16)
                    act.dma_start(w_raw[:, 4:8, :], Wr.rearrange("l o c -> o l c")).then_inc(w_in, 16)
                    act.dma_start(w_raw[:, 8, :], W1g).then_inc(w_in, 16)
                    act.dma_start(w_raw[:, 9, :], W3g).then_inc(w_in, 16)
                    act.dma_start(lnw_all[:, :, :].rearrange("p l c -> p (l c)"),
                                  ln_w.rearrange("l c -> (l c)").unsqueeze(0).to_broadcast([128, 4 * C])).then_inc(w_in, 16)
                    act.dma_start(lnb_all[:, :, :].rearrange("p l c -> p (l c)"),
                                  ln_b.rearrange("l c -> (l c)").unsqueeze(0).to_broadcast([128, 4 * C])).then_inc(w_in, 16)
                    for j in range(3):
                        k = min(4, 10 - 4 * j)
                        act.wait_ge(wt_done, j + 1)
                        S.copy(WT[:, 4 * j:4 * j + k, :].rearrange("p w c -> p (w c)"), ps[j][:, 0:k * C]).then_inc(wt_copied, 1)
                    act.wait_ge(w_in, 16 * 6)

                @block.gpsimd
                def _(pool):
                    iota = lambda o, pat, b, cm: G.iota(o, pattern=pat, base=b, channel_multiplier=cm,
                                                        allow_small_or_imprecise_dtypes=True)
                    iota(iota_f[:, :], [[1, 128]], 0, 0).then_inc(consts_ready, 1)
                    iota(iota_p[:, :], [[0, 1]], 0, 1).then_inc(consts_ready, 1)
                    iota(iota_c1[:, :], [[1, CH]], 1, 0).then_inc(consts_ready, 1)
                    pool.wait_ge(absmax_ready, 1)
                    G.partition_all_reduce(absmax_r[:, :], absmax[:, :], 128,
                                           bass.bass_isa.ReduceOp.absmax).then_inc(absmax_all, 1)

                @block.vector
                def _(dve):
                    st = Steps(dve, setup_step)
                    st.done(V.memset(src_rows[:, ROWG - 1, :], 0))
                    st.done(V.memset(absmax[:, :], 0.0))
                    V.memset(dst_rows[:, ROWG - 1, :], int(NO_NODE)).then_inc(rows_cleared, 1)
                    st.done(V.memset(ones[:, :], 1.0))
                    st.done(V.memset(eps_t[:, :], EPS))
                    st.done(V.memset(srcN[:, :], 0.0))
                    st.done(V.memset(dstN[:, :], NO_NODE))
                    dve.wait_ge(consts_ready, 3)
                    st.done(V.tensor_scalar(ident[:, :], iota_f[:, :], iota_p[:, 0:1], None, ALU.is_equal))
                    st.done(V.tensor_scalar(tri[:, :], iota_f[:, :], iota_p[:, 0:1], None, ALU.is_gt))
                    st.done(V.tensor_scalar(win[:, 0:1], iota_p[:, :], float(BWN), None, ALU.mult))
                    st.done(V.tensor_scalar(win[:, 1:2], iota_p[:, :], float(BWN), float(BWN), ALU.mult, ALU.add))
                    st.wait()
                    dve.wait_ge(edges_in, 16 * 6)
                    st.done(V.tensor_copy(dst_rf[:, :, :], dst_rows[:, :, :]))
                    st.wait()
                    V.tensor_copy(src_rf[:, :, :], src_rows[:, :, :]).then_inc(edges_f, 1)
                    st.done(V.tensor_reduce(out=mm[:, 0, :], in_=dst_rf[:, :, :], axis=AX.X, op=ALU.min))
                    st.run(V.scalar_tensor_tensor(real[:, :, :], dst_rf[:, :, :], NO_NODE - 1, dst_rf[:, :, :],
                                                  ALU.is_lt, ALU.mult))
                    st.run(V.tensor_reduce(out=mm[:, 1, :], in_=real[:, :, :], axis=AX.X, op=ALU.max))
                    for m in range(2):
                        for g in range(ROWG):
                            last = V.tensor_scalar(diag[:, m, g, :], ident[0:ROWS, 0:ROWS], mm[:, m, g:g + 1], None, ALU.mult)
                            if (m, g) == (1, ROWG - 1):
                                last.then_inc(diag_ready, 1)
                    dve.wait_ge(edges_t, 2)
                    st.done(V.tensor_copy(dstN[:, 0:CH], ps[4][:, 0:CH]))
                    st.run(V.tensor_copy(srcN[:, 0:CH], ps[5][:, 0:CH]))
                    st.done(V.tensor_copy(src_i[:, :], srcN[:, :]))
                    st.run(V.tensor_scalar(fix[:, :], srcN[:, :], 1.0 / TILE, None, ALU.mult))
                    st.run(V.tensor_copy(shi[:, :], fix[:, :]))
                    st.run(V.tensor_copy(shf[:, :], shi[:, :]))
                    st.run(V.scalar_tensor_tensor(slN0[:, :], shf[:, :], -float(TILE), srcN[:, :], ALU.mult, ALU.add))
                    st.run(V.tensor_scalar(fix[:, :], slN0[:, :], 0.0, None, ALU.is_lt))
                    st.run(V.tensor_tensor(shf[:, :], shf[:, :], fix[:, :], ALU.subtract))
                    st.run(V.tensor_scalar(fix[:, :], slN0[:, :], float(TILE), None, ALU.is_ge))
                    st.run(V.tensor_tensor(shf[:, :], shf[:, :], fix[:, :], ALU.add))
                    st.run(V.scalar_tensor_tensor(slN0[:, :], shf[:, :], -float(TILE), srcN[:, :], ALU.mult, ALU.add))
                    V.scalar_tensor_tensor(keyN0[:, :], dstN[:, :], float(NT), shf[:, :], ALU.mult, ALU.add).then_inc(keys_ready, 1)
                    dve.wait_ge(minmax_bc, 2)
                    st.run(V.tensor_scalar(hit1[:, :], ps[7][:, 0:CH], win[:, 0:1], None, ALU.is_ge))
                    st.run(V.scalar_tensor_tensor(hit[:, :], ps[6][:, 0:CH], win[:, 1:2], hit1[:, :], ALU.is_lt, ALU.mult))
                    st.done(V.tensor_tensor(cand[:, :], hit[:, :], iota_c1[:, :], ALU.mult))
                    st.run(V.scalar_tensor_tensor(cand2[:, :], hit[:, :], -1.0e6, iota_c1[:, :], ALU.mult, ALU.add))
                    st.done(V.tensor_reduce(out=lohi[:, 1:2], in_=cand[:, :], axis=AX.X, op=ALU.max))
                    st.run(V.tensor_reduce(out=lohi[:, 0:1], in_=cand2[:, :], axis=AX.X, op=ALU.min))
                    st.run(V.tensor_scalar(lohi[:, 0:1], lohi[:, 0:1], 1.0e6 - 1.0, float(CH - 1), ALU.add, ALU.min))
                    st.run(V.tensor_tensor(lohi[:, 2:3], lohi[:, 1:2], lohi[:, 0:1], ALU.subtract))
                    st.run(V.tensor_scalar(lohi[:, 2:3], lohi[:, 2:3], 1.0, float(BK - 1), ALU.max, ALU.add))
                    st.run(V.tensor_scalar(lohi[:, 3:4], lohi[:, 2:3], 205.0, None, ALU.mult))
                    st.run(V.tensor_copy(ng_i[:, 0:1], lohi[:, 3:4]))
                    st.run(V.tensor_scalar(ng_i[:, 1:2], ng_i[:, 0:1], 10, None, ALU.logical_shift_right))
                    V.tensor_copy(lohi[:, 4:5], ng_i[:, 1:2]).then_inc(ng_ready, 1)
                    dve.wait_ge(base_ready, 1)
                    dve.wait_ge(ng_ready, 1)
                    st.run(V.tensor_copy(lohi[:, 5:6], ps[3][:, 0:1]))
                    st.done(V.tensor_tensor(lohi[:, 6:7], lohi[:, 5:6], lohi[:, 4:5], ALU.add))
                    st.run(V.scalar_tensor_tensor(lohi[:, 7:8], lohi[:, 5:6], -float(BK), lohi[:, 0:1], ALU.mult, ALU.add))
                    st.run(V.tensor_scalar(lohi[:, 4:5], lohi[:, 7:8], float(CHUNK_OFF), None, ALU.add))
                    st.done(V.tensor_copy(tab_i[:, 3:4], lohi[:, 0:1]))
                    V.tensor_copy(tab_i[:, 0:3], lohi[:, 4:7]).then_inc(table_ready, 1)
                    dve.wait_ge(x_in, 16)
                    dve.wait_ge(w_in, 16 * 6)
                    st.run(V.tensor_reduce(out=absmax[0:TILE, 0:1], in_=xf[:, :, :], axis=AX.XY, op=ALU.max,
                                           apply_absolute_value=True))
                    for l in range(3):
                        st.done(V.tensor_reduce(out=bound[:, l:l + 1], in_=lnw_all[:, l, :], axis=AX.X, op=ALU.max,
                                                apply_absolute_value=True))
                        st.run(V.tensor_reduce(out=bound[:, 4 + l:5 + l], in_=lnb_all[:, l, :], axis=AX.X, op=ALU.max,
                                               apply_absolute_value=True))
                        if l == 0:
                            V.tensor_copy(absmax[:, 1:2], absmax[:, 0:1]).then_inc(absmax_ready, 1)
                    st.run(V.tensor_scalar(cand[:, 0:3], bound[:, 0:3], LN_BOUND, None, ALU.mult))
                    st.run(V.tensor_tensor(cand[:, 4:7], cand[:, 0:3], bound[:, 4:7], ALU.add))
                    st.run(V.tensor_copy(bound[:, 1:4], cand[:, 4:7]))
                    dve.wait_ge(absmax_all, 1)
                    st.run(V.tensor_copy(bound[:, 0:1], absmax_r[:, 0:1]))
                    st.run(V.tensor_scalar(bound[:, 0:4], bound[:, 0:4], 1e-30, None, ALU.max))
                    st.run(V.tensor_scalar(bound[:, 0:4].bitcast(i32), bound[:, 0:4].bitcast(i32), 0x7F800000, None, ALU.bitwise_and))
                    st.done(V.tensor_scalar(inv_alpha[:, 0:4], bound[:, 0:4], 2.0 ** -13, None, ALU.mult))
                    st.done(V.memset(inv_alpha[:, 4:8], 1.0 / ALPHA_LN))
                    st.wait()
                    st.run(V.reciprocal(alpha[:, :], inv_alpha[:, :]))
                    for l in range(5):
                        last = V.tensor_scalar(ident_a[:, l, :], ident[:, 0:TILE], inv_alpha[:, l:l + 1], None, ALU.mult)
                    last.then_inc(alpha_ready, 1)

                @block.tensor
                def _(pe):
                    pe.wait_ge(w_in, 16 * 6)
                    pe.wait_ge(setup_step, 11)
                    for j in range(3):
                        for k in range(min(4, 10 - 4 * j)):
                            last = T.transpose(ps[j][:, k * C:(k + 1) * C], w_raw[:, 4 * j + k, :], ident[:, :])
                        last.then_inc(wt_done, 1)
                    pe.wait_ge(edges_f, 1)
                    for p, rows in ((4, dst_rf), (5, src_rf)):
                        for g in range(ROWG):
                            last = T.transpose(ps[p][:, g * ROWS:(g + 1) * ROWS], rows[:, g, :], ident[0:ROWS, 0:ROWS])
                        last.then_inc(edges_t, 1)
                    pe.wait_ge(diag_ready, 1)
                    for m in range(2):
                        for g in range(ROWG):
                            last = T.matmul(ps[6 + m][:, g * ROWS:(g + 1) * ROWS], ones[0:ROWS, :], diag[:, m, g, :],
                                            start=True, stop=True)
                        last.then_inc(minmax_bc, 1)
                    pe.wait_ge(ng_ready, 1)
                    pe.wait_ge(wt_copied, 3)
                    T.matmul(ps[3][0:128, 0:1], tri[0:128, 0:128], lohi[0:128, 4:5], start=True, stop=True).then_inc(base_ready, 1)

        counts_all = sb("counts_all", [128, NT * N + 3], fp16)
        counts = counts_all[0:TILE, 0:NT * N].rearrange("p (s d) -> p s d", s=NT)
        s2 = ExitStack()
        with s2:
            t = lambda name, shape, dt: sb(name, shape, dt, s2)
            keyN = t("keyN", [LANES, CHP], fp32)
            slN = t("slN", [LANES, CHP], fp32)
            iota_k = t("iota_k", [LANES, BKEYS], fp16)
            win_off = t("win_off", [LANES, BW], fp32)
            rel_key = [t(f"rel_key{i}", [LANES, BK], fp32) for i in range(2)]
            rel_sl = t("rel_sl", [LANES, BK], fp32)
            oh_key = parts_all[1][:, :, :, :].rearrange("p t h c -> p (t h c)")[:, 0:2 * BK * (BKEYS + 1)].rearrange(
                "p (u k n) -> p u k n", u=2, k=BK)
            oh_key = [oh_key[:, i] for i in range(2)]
            ones_h = t("ones_h", [TILE, 128], fp16)
            ones_col = t("ones_col", [LANES, 1], fp32)
            dist = t("dist", [LANES, AK, TILE + 1], fp16)
            oh_sl = [t(f"oh_sl{i}", [LANES, BK, TILE + 1], fp16) for i in range(2)]
            sl_h = t("sl_h", [LANES, CHP], fp16)
            zeros = t("zeros", [LANES, TILE], fp16)
            table = t("table", [1, BW * 4], i32)
            firsts = t("firsts", [1, BW + 3], i32)

            def late_columns(row, shape, dt=fp32):
                n = int(np.prod(shape))
                at0 = row * N + N - 1125 + (row * N + N - 1125) % 2
                view = counts_all[:, at0:at0 + 2 * n].bitcast(dt)
                return view.rearrange("p (a b) -> p a b", a=shape[0]) if len(shape) == 2 else view

            gmm = late_columns(16, [2, NG])
            gq = late_columns(17, [2, NG])
            gqi = late_columns(18, [2, NG], i32)
            gr = late_columns(19, [2, NG])
            gf = late_columns(20, [2, NG])
            w0_i = late_columns(21, [128], i32)
            w0_f = late_columns(22, [128])
            dstN = late_columns(23, [CHP])
            reldst = late_columns(15, [CHP])
            win_step = sem("win_step")
            windows_ready = sem("windows_ready")
            windows_out = sem("windows_out")
            dst_in = sem("dst_in")
            keys_in = sem("keys_in")
            build_consts = sem("build_consts")
            rel_ready = sem("rel_ready")
            dist_ready = sem("dist_ready")
            sl_ready = sem("sl_ready")
            split_step = sem("split_step")
            x_hi_ready = sem("x_hi_ready")
            deg_done = sem("deg_done")
            deg_copied = sem("deg_copied")
            pair_ready = sem("pair_ready")
            pair_free = sem("pair_free")
            window_done = sem("window_done")
            window_free = sem("window_free")

            def total_steps(engine):
                return load_registers(nc, engine, table[0:1, (BW - 1) * 4:BW * 4], 2 * CHUNK_OFF)[1]

            def over_windows(eng, engine, body, ahead=0):
                first = load_registers(nc, engine, firsts[0:1, ahead:ahead + 4], CH - 1)
                for r in range(4):
                    body(0, r, r, first[r])
                with eng.Fori(0, (BW // 4 - 1) // 2) as i:
                    for j in (i * 2 + 1, i * 2 + 2):
                        first = load_registers(nc, engine, firsts[0:1, bass.ds(j * 4 + ahead, 4)], CH - 1, FIRSTS_CLAMPED)
                        for r in range(4):
                            body(j, j * 4 + r, r, first[r])
                first = load_registers(nc, engine, firsts[0:1, BW - 1:BW + 3], CH - 1)
                body(BW // 4, BW - 1, 0, first[0])

            def banks(slot):
                return ps[2 * slot][0:TILE, 0:BHALF], ps[2 * slot + 1][0:TILE, 0:BKEYS - BHALF]

            with nc.Block() as block:
                @block.sync
                def _(sp):
                    sp.dma_start(keyN[:, :], key_d).then_inc(keys_in, 16)
                    sp.dma_start(slN[:, :], sl_d).then_inc(keys_in, 16)
                    sp.dma_start(table[0:1, :], build_table_d.rearrange("w f -> (w f)").unsqueeze(0)).then_inc(keys_in, 16)
                    sp.dma_start(dstN, dstf_d).then_inc(dst_in, 16)
                    sp.wait_ge(windows_ready, 1)
                    sp.dma_start(reldst_d, reldst).then_inc(windows_out, 16)
                    sp.dma_start(win_table_d, w0_i[0:1, :]).then_inc(windows_out, 16)

                @block.gpsimd
                def _(pool):
                    G.iota(iota_k[:, :], pattern=[[1, BKEYS]], base=0, channel_multiplier=0,
                           allow_small_or_imprecise_dtypes=True).then_inc(build_consts, 1)
                    G.iota(win_off[:, :], pattern=[[-BKEYS, BW]], base=0, channel_multiplier=0,
                           allow_small_or_imprecise_dtypes=True).then_inc(build_consts, 1)

                    st = Steps(pool, split_step)
                    pool.wait_ge(x_hi_ready, 1)
                    st.run(G.tensor_scalar(xf[:, :, :], xf[:, :, :], alpha[0:TILE, 0:1], None, ALU.mult))
                    st.run(G.tensor_tensor(parts[0][:, :, 1, :], xf[:, :, :], parts[0][:, :, 0, :], ALU.subtract))

                @block.vector
                def _(dve):
                    V.memset(zeros[:, :], 0.0)
                    V.memset(ones_h[:, :], 1.0)
                    V.memset(ones_col[:, :], 1.0)
                    V.memset(firsts[0:1, BW:BW + 3], 0)
                    dve.sem_inc(pair_ready, 1)
                    dve.sem_inc(deg_copied, 1)
                    wst = Steps(dve, win_step)
                    wst.done(V.tensor_reduce(out=gmm[:, 0, :], in_=ps[6][:, 0:CH].rearrange("p (g k) -> p g k", k=GRP),
                                            axis=AX.X, op=ALU.min))
                    wst.run(V.tensor_reduce(out=gmm[:, 1, :], in_=ps[7][:, 0:CH].rearrange("p (g k) -> p g k", k=GRP),
                                           axis=AX.X, op=ALU.max))
                    wst.run(V.tensor_scalar(gr[:, :, :], gmm[:, :, :], 1.0 / TILE, None, ALU.mult))
                    wst.run(V.tensor_copy(gqi[:, :, :], gr[:, :, :]))
                    wst.run(V.tensor_copy(gq[:, :, :], gqi[:, :, :]))
                    wst.run(V.scalar_tensor_tensor(gr[:, :, :], gq[:, :, :], -float(TILE), gmm[:, :, :], ALU.mult, ALU.add))
                    wst.run(V.tensor_scalar(gf[:, :, :], gr[:, :, :], 0.0, None, ALU.is_lt))
                    wst.run(V.tensor_tensor(gq[:, :, :], gq[:, :, :], gf[:, :, :], ALU.subtract))
                    wst.run(V.tensor_scalar(gf[:, :, :], gr[:, :, :], float(TILE), None, ALU.is_ge))
                    wst.run(V.tensor_tensor(gq[:, :, :], gq[:, :, :], gf[:, :, :], ALU.add))
                    wst.run(V.memset(w0_f[:, :], 0.0))
                    wst.done(V.tensor_copy(w0_f[:, 2:2 + NG], gq[:, 0, :]))
                    wst.run(V.tensor_tensor(gf[:, 0, :], gq[:, 1, :], gq[:, 0, :], ALU.subtract))
                    wst.run(V.tensor_reduce(out=w0_f[:, 127:128], in_=gf[:, 0, :], axis=AX.X, op=ALU.max))
                    wst.done(V.tensor_copy(w0_i[:, :], w0_f[:, :]))
                    wst.run(V.memset(reldst[:, :], NO_NODE))
                    dve.wait_ge(dst_in, 16)
                    V.scalar_tensor_tensor(reldst[:, 0:CH].rearrange("p (g k) -> p g k", k=GRP),
                                           gq[:, 0, :].unsqueeze(2).to_broadcast([LANES, NG, GRP]), -float(TILE),
                                           dstN[:, 0:CH].rearrange("p (g k) -> p g k", k=GRP),
                                           ALU.mult, ALU.add).then_inc(windows_ready, 1)
                    dve.wait_ge(keys_in, 48)
                    V.tensor_copy(sl_h[:, :], slN[:, :])
                    V.tensor_copy(firsts[0:1, 0:BW], table[0:1, :].rearrange("p (w f) -> p w f", f=4)[:, :, 3]).then_inc(build_consts, 1)
                    dve.wait_ge(build_consts, 3)
                    total = total_steps(ET.DVE)

                    def add_degrees(j, n):
                        dve.wait_ge(split_step, 2)
                        dve.wait_ge(windows_out, 32)
                        dve.wait_ge(deg_done, j + 1)
                        V.tensor_reduce(out=inv_deg[:, bass.ds(j * DW, n)], in_=ps[4][:, 0:DS * n].rearrange("p (s n) -> p n s", n=n),
                                        axis=AX.X, op=ALU.add).then_inc(deg_copied, 1)

                    def keys(j, w, r, first):
                        slot = r % 2
                        dve.wait_ge(rel_ready, w + 1)
                        dve.wait_ge(window_done, w + 1)
                        for k in range(BK):
                            if k == AK:
                                shape = [LANES, BK - AK, TILE]
                                V.tensor_tensor(oh_sl[slot][:, AK:BK, 0:TILE], iota_k[:, 0:TILE].unsqueeze(1).to_broadcast(shape),
                                                sl_h[:, bass.ds(first + AK, BK - AK)].unsqueeze(2).to_broadcast(shape), ALU.is_equal)
                            V.tensor_scalar(oh_key[slot][:, k, 0:BKEYS], iota_k[:, :], rel_key[slot][:, k:k + 1], None,
                                            ALU.is_equal).then_inc(pair_ready, 1)
                        if r == 3 and not isinstance(j, int):
                            add_degrees(j - 1, DW)

                    with dve.If(total <= BW):
                        over_windows(dve, ET.DVE, keys)
                        add_degrees(BW // 4 - 1, DW)
                        add_degrees(BW // 4, N - BW // 4 * DW)
                    with dve.Else():
                        with dve.Fori(0, BW) as w:
                            off, first, end, _z = load_registers(nc, ET.DVE, table[0:1, bass.ds(w * 4, 4)], 2 * CHUNK_OFF)
                            with dve.Fori(first, end) as i:
                                chunk = nc.s_assert_within(off + i * BK - CHUNK_OFF, 0, CHP - BK)
                                dve.wait_ge(pair_ready, i * BK + 1)
                                V.tensor_scalar(rel_key[0][:, :], keyN[:, bass.ds(chunk, BK)], win_off[:, bass.ds(w, 1)], None,
                                                ALU.add).then_inc(rel_ready, 1)
                                V.tensor_copy(rel_sl[:, :], slN[:, bass.ds(chunk, BK)]).then_inc(rel_ready, 1)
                                dve.wait_ge(rel_ready, i * 2 + 2)
                                for k in range(BK):
                                    dve.wait_ge(pair_free, i * BK + k + 1)
                                    V.tensor_scalar(oh_sl[0][:, k, 0:TILE], iota_k[:, 0:TILE], rel_sl[:, k:k + 1], None, ALU.is_equal)
                                    V.tensor_scalar(oh_key[0][:, k, 0:BKEYS], iota_k[:, :], rel_key[0][:, k:k + 1], None,
                                                    ALU.is_equal).then_inc(pair_ready, 1)
                        with dve.Fori(0, BW // 4) as j:
                            add_degrees(j, DW)
                        add_degrees(BW // 4, N - BW // 4 * DW)

                @block.tensor
                def _(pe):
                    pe.sem_inc(window_done, 2)
                    pe.wait_ge(build_consts, 3)
                    pe.wait_ge(keys_in, 48)
                    total = total_steps(ET.PE)

                    def degrees(j, n):
                        pe.wait_ge(deg_copied, j + 1)
                        for s in range(0, NT, DS):
                            last = T.matmul(ps[4][:, 0:DS * n], ones_h[:, :], counts[:, s:s + DS, bass.ds(j * DW, n)],
                                            start=(s == 0), stop=(s == NT - DS))
                        last.then_inc(deg_done, 1)

                    def count(j, w, r, _first):
                        slot = r % 2
                        a, b = banks(slot)
                        pe.wait_ge(window_free, w + 1)
                        pe.wait_ge(sl_ready, w + 2)
                        for k in range(BK):
                            pe.wait_ge(pair_ready, w * BK + k + 2)
                            for o, cols in ((a, slice(0, BHALF)), (b, slice(BHALF, BKEYS))):
                                last = T.matmul(o, oh_sl[slot][:, k, 0:TILE], oh_key[slot][:, k, cols], start=(k == 0),
                                                stop=(k == BK - 1))
                        last.then_inc(window_done, 1)
                        if r == 1 and not isinstance(j, int):
                            degrees(j - 1, DW)

                    def window(w, slot):
                        a, b = banks(slot)
                        _o, first, end, _z = load_registers(nc, ET.PE, table[0:1, bass.ds(w * 4, 4)], 2 * CHUNK_OFF)
                        pe.wait_ge(window_free, w + 1)
                        for o in (a, b):
                            T.matmul(o, zeros[:, :], iota_k[:, 0:o.shape[1]], start=True, stop=False, skip_group_check=True)
                        with pe.Fori(first, end) as i:
                            for k in range(BK):
                                pe.wait_ge(pair_ready, i * BK + k + 2)
                                T.matmul(a, oh_sl[0][:, k, 0:TILE], oh_key[0][:, k, 0:BHALF], start=False, stop=False,
                                         skip_group_check=True)
                                T.matmul(b, oh_sl[0][:, k, 0:TILE], oh_key[0][:, k, BHALF:BKEYS], start=False,
                                         stop=False, skip_group_check=True).then_inc(pair_free, 1)
                        for o in (a, b):
                            last = T.matmul(o[:, 0:2], zeros[:, :], iota_k[:, 0:2], start=False, stop=True, skip_group_check=True)
                        last.then_inc(window_done, 1)

                    with pe.If(total <= BW):
                        over_windows(pe, ET.PE, count)
                        pe.wait_ge(window_free, BW + 2)
                        degrees(BW // 4 - 1, DW)
                        degrees(BW // 4, N - BW // 4 * DW)
                    with pe.Else():
                        pe.sem_inc(pair_free, BK)
                        with pe.Fori(0, BW // 2) as j:
                            window(j * 2, 0)
                            window(j * 2 + 1, 1)
                        window(BW - 1, 0)
                        pe.wait_ge(window_free, BW + 2)
                        with pe.Fori(0, BW // 4) as j:
                            degrees(j, DW)
                        degrees(BW // 4, N - BW // 4 * DW)

                @block.scalar
                def _(act):
                    act.sem_inc(window_free, 2)
                    S.activation(parts[0][:, :, 0, :], xf[:, :, :], ACT.Identity, scale=alpha[0:TILE, 0:1]).then_inc(x_hi_ready, 1)
                    act.wait_ge(build_consts, 3)
                    act.wait_ge(keys_in, 48)
                    total = total_steps(ET.Activation)

                    def evacuate(w, slot, _first=None):
                        h = BHALF // NT
                        a, b = banks(slot)
                        act.wait_ge(window_done, w + 3)
                        S.copy(counts[:, :, bass.ds(w * BWN, h)].rearrange("p s d -> p d s"), a.rearrange("p (d s) -> p d s", s=NT))
                        S.copy(counts[:, :, bass.ds(w * BWN + h, BWN - h)].rearrange("p s d -> p d s"),
                               b.rearrange("p (d s) -> p d s", s=NT)).then_inc(window_free, 1)

                    def prepare(w, slot, first):
                        act.wait_ge(window_done, w + 1)
                        S.activation(rel_key[slot][:, :], keyN[:, bass.ds(first, BK)], ACT.Identity,
                                     bias=win_off[:, bass.ds(w, 1)]).then_inc(rel_ready, 1)
                        act.wait_ge(sl_ready, w + 1)
                        for k in range(AK):
                            last = S.activation(dist[:, k, 0:TILE], iota_k[:, 0:TILE], ACT.Abs, scale=-1.0,
                                                bias=slN[:, bass.ds(first + k, 1)])
                        last.then_inc(dist_ready, 1)
                        act.wait_ge(dist_ready, w + 1)
                        S.activation(oh_sl[slot][:, 0:AK, 0:TILE], dist[:, :, 0:TILE], ACT.Relu, scale=-1.0,
                                     bias=ones_col[:, 0:1]).then_inc(sl_ready, 1)

                    def step(j, w, r, first):
                        if not (isinstance(w, int) and w == BW - 1):
                            prepare(w + 1, (r + 1) % 2, first)
                        evacuate(w, r % 2)

                    with act.If(total <= BW):
                        act.sem_inc(sl_ready, 1)
                        first = load_registers(nc, ET.Activation, firsts[0:1, 0:4], CH - 1)
                        prepare(0, 0, first[0])
                        over_windows(act, ET.Activation, step, ahead=1)
                    with act.Else():
                        act.wait_ge(windows_out, 32)
                        with act.Fori(0, BW // 2) as j:
                            evacuate(j * 2, 0)
                            evacuate(j * 2 + 1, 1)
                        evacuate(BW - 1, 0)

        PER = {
            "sage": dict(agg_done=1, agg_scaled=1, xt_done=1, xt_copied=1, y_done=1, y_free=1, stats_ready=1,
                         std_ready=1, z_ready=1, relu_ready=1, parts_ready=1, ln_step=3, x0_in=0, out_done=0),
            "sage_res": dict(agg_done=1, agg_scaled=1, xt_done=1, xt_copied=1, y_done=1, y_free=1, stats_ready=2,
                             std_ready=2, z_ready=2, relu_ready=2, parts_ready=1, ln_step=6, x0_in=16, out_done=0),
            "message": dict(agg_done=1, agg_scaled=1, xt_done=0, xt_copied=0, y_done=1, y_free=1, stats_ready=1,
                            std_ready=1, z_ready=2, relu_ready=2, parts_ready=1, ln_step=4, x0_in=0, out_done=0),
            "final": dict(agg_done=1, agg_scaled=1, xt_done=1, xt_copied=1, y_done=1, y_free=1, stats_ready=1,
                          std_ready=1, z_ready=1, relu_ready=1, parts_ready=0, ln_step=4, x0_in=0, out_done=16),
        }
        KINDS = ["sage", "sage", "sage", "sage_res", "message", "final"]
        PIN = [0, 1, 0, 1, 0, 1]
        W_AGG = [0, 1, 2, 3, 8, 9]
        W_SELF = [4, 5, 6, 7, None, 9]
        SEMS = {name: sem(name) for name in PER["sage"]}
        FROM_ONE = ("agg_scaled", "y_free", "y_done", "xt_copied", "out_done")

        def at(name, l, b, k=0):
            before = sum((NBLK + 1) * PER[KINDS[m]][name] for m in range(l)) + (name in FROM_ONE)
            return before + k + b * PER[KINDS[l]][name]

        def wait_before_last(eng, name, l, b):
            if not (isinstance(b, int) and l == b == 0):
                eng.wait_ge(SEMS[name], at(name, l, b) - 1)

        def pipeline(eng, l, early, late, start=None, between=None):
            q = BLK // TILE
            first, second = l % 2, (l + 1) % 2
            if start:
                start()
            else:
                early(0, q, first)
            with eng.Fori(0, NBLK // 2 - 1) as j:
                early(j * 2 + 1, q, second)
                late(j * 2, q, first)
                early(j * 2 + 2, q, first)
                late(j * 2 + 1, q, second)
            early(NBLK - 1, q, second)
            late(NBLK - 2, q, first)
            early(NBLK, (N - NBLK * BLK) // TILE, first)
            late(NBLK - 1, q, second)
            if between:
                between()
            late(NBLK, (N - NBLK * BLK) // TILE, first)

        def over_blocks(eng, body):
            with eng.Fori(0, NBLK) as b:
                body(b, BLK // TILE)
            body(NBLK, (N - NBLK * BLK) // TILE)

        BIAS_STEPS = 8
        counts_saved = sem("counts_saved")
        counts_back = sem("counts_back")
        deg_stored = sem("deg_stored")
        deg_cols = sem("deg_cols")
        has_edge_ready = sem("has_edge_ready")
        deg_step = sem("deg_step")

        def layers(ls):
            sl = ExitStack()
            with sl:
                t = lambda name, shape, dt: sb(name, shape, dt, sl)
                tag = f"_{ls[0]}"
                q = BLK // TILE
                agg_sb = t("agg_sb" + tag, [C, BLK], fp32)
                xt_sb = t("xt_sb" + tag, [C, BLK], fp32)
                z = t("z" + tag, [TILE, q, C], fp32)
                u = t("u" + tag, [TILE, q, C], fp32)
                stats = t("stats" + tag, [TILE, q, 6], fp32)
                mv = t("mv" + tag, [TILE, q, 2], fp32)
                std = t("std" + tag, [TILE, q], fp32)
                rstd = t("rstd" + tag, [TILE, q], fp32)
                lnw = t("lnw" + tag, [TILE, C], fp32)
                lnb = t("lnb" + tag, [TILE, C], fp32)
                x0 = t("x0" + tag, [TILE, q, C], fp32) if 3 in ls else None
                wt = t("wt" + tag, [C, 2, C], fp32)
                ones3 = t("ones3" + tag, [3, TILE], bf16)
                bias = t("bias" + tag, [3, C], fp32)
                bias_rest = t("bias_rest" + tag, [3, C], fp32)
                bias_part = t("bias_part" + tag, [3, 3, C], bf16)
                bias_row = t("bias_row" + tag, [3, C], bf16)
                bias_step = sem("bias_step" + tag)
                layer_in = sem("layer_in" + tag)
                stats_taken = sem("stats_taken" + tag)
                agg_ps, xt_ps, y_ps = ps[0:2], ps[2:4], ps[4:6]
                LOADS = {"sage": 5, "sage_res": 5, "message": 2, "final": 3}
                loaded = lambda l: 16 * sum(LOADS[KINDS[m]] for m in ls if m <= l)
                w_S = lambda name: SEMS[name]

                with nc.Block() as block:
                    @block.tensor
                    def _(pe):
                        def sums(l, b, nt, p, sources=range(NT)):
                            pin, w = parts[PIN[l]], nt * TILE
                            if sources[0] == 0:
                                wait_before_last(pe, "agg_scaled", l, b)
                            for s in sources:
                                if KINDS[l] == "final" and s == NT - 1 and isinstance(b, int) and b == 0:
                                    pe.wait_ge(counts_back, 32)
                                if l > ls[0] and s % q == 0:
                                    pe.wait_ge(w_S("parts_ready"), at("parts_ready", l - 1, s // q, 1))
                                for part in range(2):
                                    last = T.matmul(agg_ps[p][:, 0:w], pin[:, s, part, :], counts[:, s, bass.ds(b * BLK, w)],
                                                    start=(s + part == 0), stop=(s + part == NT))
                            if sources[-1] < NT - 1:
                                return
                            last.then_inc(w_S("agg_done"), 1)
                            if W_SELF[l] is not None:
                                wait_before_last(pe, "xt_copied", l, b)
                                for j in range(nt):
                                    for part in range(2):
                                        last = T.matmul(xt_ps[p][:, j * TILE:(j + 1) * TILE], pin[:, b * q + j, part, :],
                                                        ident_a[0:TILE, min(l, 4), :], start=(part == 0), stop=(part == 1))
                                last.then_inc(w_S("xt_done"), 1)

                        def project(l, b, nt, p):
                            if W_SELF[l] is not None:
                                pe.wait_ge(w_S("xt_copied"), at("xt_copied", l, b, 1))
                            pe.wait_ge(w_S("agg_scaled"), at("agg_scaled", l, b, 1))
                            wait_before_last(pe, "y_free", l, b)
                            pe.wait_ge(layer_in, loaded(l))
                            if W_SELF[l] is not None:
                                pe.wait_ge(bias_step, BIAS_STEPS * (ls.index(l) + 1))
                            for j in range(nt):
                                y = y_ps[p][0:TILE, j * C:(j + 1) * C]
                                cols = slice(j * TILE, (j + 1) * TILE)
                                last = T.matmul(y, agg_sb[:, cols], wt[:, 0, :], start=True, stop=W_SELF[l] is None)
                                if W_SELF[l] is not None:
                                    T.matmul(y, xt_sb[:, cols], wt[:, 1, :], start=False, stop=False)
                                    last = T.matmul(y, ones3[:, :], bias_row[:, :], start=False, stop=True)
                            last.then_inc(w_S("y_done"), 1)

                        if ls[0] == 0:
                            pe.sem_inc(w_S("y_done"), 1)
                        ahead = 4 * q
                        for l in ls:
                            pipeline(pe, l, lambda b, nt, p: sums(l, b, nt, p), lambda b, nt, p: project(l, b, nt, p),
                                     (lambda: sums(l, 0, q, l % 2, range(ahead, NT))) if l > ls[0] else None,
                                     (lambda: sums(l + 1, 0, q, (l + 1) % 2, range(ahead))) if l < ls[-1] else None)

                    @block.scalar
                    def _(act):
                        def take_own(l, b, nt, p):
                            if W_SELF[l] is not None:
                                w = nt * TILE
                                act.wait_ge(w_S("xt_done"), at("xt_done", l, b, 1))
                                act.wait_ge(w_S("y_done"), at("y_done", l, b))
                                S.copy(xt_sb[:, 0:w], xt_ps[p][:, 0:w]).then_inc(w_S("xt_copied"), 1)

                        def finish(l, b, nt, p):
                            pout, kind = parts[1 - PIN[l]], KINDS[l]
                            tiles = bass.ds(b * q, nt)
                            z_, u_ = z[:, 0:nt, :], u[:, 0:nt, :]

                            def std_of(k):
                                act.wait_ge(w_S("stats_ready"), at("stats_ready", l, b, k))
                                S.activation(std[:, 0:nt], mv[:, 0:nt, 1], ACT.Sqrt, bias=eps_t[0:TILE, 0:1]).then_inc(w_S("std_ready"), 1)

                            if kind == "sage":
                                std_of(1)
                                act.wait_ge(w_S("z_ready"), at("z_ready", l, b, 1))
                                S.activation(pout[:, tiles, 0, :], z_, ACT.Relu, scale=alpha[0:TILE, l + 1:l + 2])
                                S.activation(u_, z_, ACT.Relu).then_inc(w_S("relu_ready"), 1)
                                return
                            if kind == "sage_res":
                                std_of(1)
                            if kind == "final":
                                act.wait_ge(w_S("y_done"), at("y_done", l, b, 1))
                                act.wait_ge(w_S("z_ready"), at("z_ready", l, b))
                                S.activation(u_, y_ps[p][0:TILE, 0:nt * C].rearrange("p (j c) -> p j c", c=C),
                                             ACT.Relu).then_inc(w_S("relu_ready"), 1)
                            else:
                                act.wait_ge(w_S("z_ready"), at("z_ready", l, b, 1))
                                S.activation(u_, z_, ACT.Relu).then_inc(w_S("relu_ready"), 1)
                            std_of(PER[kind]["stats_ready"])
                            if kind != "final":
                                act.wait_ge(w_S("z_ready"), at("z_ready", l, b, 2))
                                S.activation(pout[:, tiles, 0, :], z_, ACT.Copy, scale=ALPHA_LN).then_inc(w_S("relu_ready"), 1)

                        if ls[0] == 0:
                            act.sem_inc(w_S("xt_copied"), 1)
                        for l in ls:
                            pipeline(act, l, lambda b, nt, p: take_own(l, b, nt, p), lambda b, nt, p: finish(l, b, nt, p))

                    @block.vector
                    def _(dve):
                        st = Steps(dve, w_S("ln_step"))

                        def scale(l, b, nt, p):
                            w = nt * TILE
                            if l == 0:
                                dve.wait_ge(deg_stored, 16)
                                deg = inv_deg[:, bass.ds(b * BLK, w)]
                                V.tensor_scalar(deg, deg, 1.0, None, ALU.max).then_inc(deg_step, 1)
                                dve.wait_ge(deg_step, b * 2 + 1)
                                dve.sem_inc(stats_taken, 1)
                                V.reciprocal(deg, deg).then_inc(deg_step, 1)
                                dve.wait_ge(deg_step, b * 2 + 2)
                            dve.wait_ge(w_S("agg_done"), at("agg_done", l, b, 1))
                            dve.wait_ge(w_S("y_done"), at("y_done", l, b))
                            V.scalar_tensor_tensor(agg_sb[:, 0:w], agg_ps[p][:, 0:w], inv_alpha[:, l:l + 1],
                                                   inv_deg[:, bass.ds(b * BLK, w)], ALU.mult, ALU.mult).then_inc(w_S("agg_scaled"), 1)

                        def finish(l, b, nt, p):
                            pin, pout, kind = parts[PIN[l]], parts[1 - PIN[l]], KINDS[l]
                            tiles = bass.ds(b * q, nt)
                            z_, u_ = z[:, 0:nt, :], u[:, 0:nt, :]
                            y = lambda j: y_ps[p][0:TILE, j * C:(j + 1) * C]
                            st.n, st.base = at("ln_step", l, 0), b * PER[kind]["ln_step"]

                            def statistics(of, k):
                                for j in range(nt):
                                    last = V.bn_stats(stats[:, j, :], of(j))
                                st.run(last)
                                dve.sem_inc(stats_taken, 1)
                                for j in range(nt):
                                    last = V.bn_aggr(mv[:, j, :], stats[:, j, :])
                                last.then_inc(w_S("stats_ready"), 1)
                                dve.wait_ge(w_S("std_ready"), at("std_ready", l, b, k))
                                st.run(V.reciprocal(rstd[:, 0:nt], std[:, 0:nt]))

                            def normalize(of):
                                for j in range(nt):
                                    last = V.tensor_scalar(z[:, j, :], of(j), mv[:, j, 0:1], rstd[:, j:j + 1], ALU.subtract, ALU.mult)
                                return last

                            if kind != "final":
                                dve.wait_ge(w_S("y_done"), at("y_done", l, b, 1))
                            if kind in ("sage", "sage_res"):
                                statistics(y, 1)
                                normalize(y).then_inc(w_S("y_free"), 1)
                                dve.wait_ge(w_S("y_free"), at("y_free", l, b, 1))
                                st.run(V.tensor_tensor(z_, z_, lnw[:, :].unsqueeze(1).to_broadcast([TILE, nt, C]), ALU.mult))
                                V.tensor_tensor(z_, z_, lnb[:, :].unsqueeze(1).to_broadcast([TILE, nt, C]), ALU.add).then_inc(w_S("z_ready"), 1)
                            if kind == "sage":
                                dve.wait_ge(w_S("relu_ready"), at("relu_ready", l, b, 1))
                                V.scalar_tensor_tensor(pout[:, tiles, 1, :], u_, alpha[0:TILE, l + 1:l + 2], pout[:, tiles, 0, :],
                                                       ALU.mult, ALU.subtract).then_inc(w_S("parts_ready"), 1)
                                return
                            if kind == "sage_res":
                                dve.wait_ge(w_S("x0_in"), at("x0_in", l, b, 16))
                                dve.wait_ge(w_S("relu_ready"), at("relu_ready", l, b, 1))
                                st.run(V.tensor_tensor(u_, u_, x0[:, 0:nt, :], ALU.add))
                            if kind == "message":
                                dve.wait_ge(w_S("parts_ready"), at("parts_ready", l, b))
                                for j in range(nt):
                                    last = V.scalar_tensor_tensor(z[:, j, :], lnw[:, :], has_edge[:, bass.ds(b * q + j, 1)], y(j),
                                                                  ALU.mult, ALU.add)
                                last.then_inc(w_S("z_ready"), 1)
                                V.memset(stats[:, 0, 0:1], 0.0).then_inc(w_S("y_free"), 1)
                            if kind in ("message", "final"):
                                dve.wait_ge(w_S("relu_ready"), at("relu_ready", l, b, 1))
                                if kind == "final":
                                    V.memset(stats[:, 0, 0:1], 0.0).then_inc(w_S("y_free"), 1)
                                    dve.wait_ge(w_S("out_done"), at("out_done", l, b))
                                st.run(V.tensor_tensor(z_, pin[:, tiles, 0, :], pin[:, tiles, 1, :], ALU.add))
                                st.run(V.scalar_tensor_tensor(u_, z_, 1.0 / ALPHA_LN, u_, ALU.mult, ALU.add))
                            statistics(lambda j: u[:, j, :], PER[kind]["std_ready"])
                            normalize(lambda j: u[:, j, :]).then_inc(w_S("z_ready"), 1)
                            if kind == "final":
                                return
                            dve.wait_ge(w_S("relu_ready"), at("relu_ready", l, b, 2))
                            V.scalar_tensor_tensor(pout[:, tiles, 1, :], z_, ALPHA_LN, pout[:, tiles, 0, :],
                                                   ALU.mult, ALU.subtract).then_inc(w_S("parts_ready"), 1)

                        if ls[0] == 0:
                            dve.sem_inc(w_S("agg_scaled"), 1)
                            dve.sem_inc(w_S("y_free"), 1)
                        V.memset(ones3[:, :], 1.0)
                        for n, l in enumerate(ls):
                            if KINDS[l] == "message":
                                dve.wait_ge(deg_cols, 16)
                                V.tensor_scalar(has_edge[:, :], has_edge[:, :], 1.0, None, ALU.min).then_inc(has_edge_ready, 1)
                                dve.wait_ge(has_edge_ready, 1)
                            dve.wait_ge(layer_in, loaded(l))
                            if W_SELF[l] is not None:
                                bias_st = Steps(dve, bias_step)
                                bias_st.n = BIAS_STEPS * n
                                part = [bias_part[:, i, :] for i in range(3)]
                                bias_st.run(V.tensor_copy(part[0], bias[:, :]))
                                bias_st.run(V.tensor_tensor(bias_rest[:, :], bias[:, :], part[0], ALU.subtract))
                                bias_st.run(V.tensor_copy(part[1], bias_rest[:, :]))
                                bias_st.run(V.tensor_tensor(bias_rest[:, :], bias_rest[:, :], part[1], ALU.subtract))
                                bias_st.run(V.tensor_copy(part[2], bias_rest[:, :]))
                                bias_st.run(V.tensor_scalar(bias_row[:, :], part[0], ident[0:3, 0:1], None, ALU.mult))
                                for i in (1, 2):
                                    bias_st.run(V.scalar_tensor_tensor(bias_row[:, :], part[i], ident[0:3, i:i + 1], bias_row[:, :],
                                                                   ALU.mult, ALU.add))
                                assert bias_st.n == BIAS_STEPS * (n + 1)
                            pipeline(dve, l, lambda b, nt, p: scale(l, b, nt, p), lambda b, nt, p: finish(l, b, nt, p))

                    @block.sync
                    def _(sp):
                        if ls[0] == 0:
                            sp.sem_inc(w_S("out_done"), 1)
                            sp.dma_start(deg_d.unsqueeze(0), inv_deg[0:1, 0:N]).then_inc(deg_stored, 16)
                        else:
                            sp.dma_start(counts_all[0:TILE, (NT - 1) * N:NT * N],
                                         counts_d[:, (NT - 1 - SPILL) * N:(NT - SPILL) * N]).then_inc(counts_back, 16)
                        for l in ls:
                            if l > ls[0]:
                                sp.wait_ge(w_S("parts_ready"), at("parts_ready", l, 0))
                            sp.dma_start(wt[:, 0, :], wt_d[:, W_AGG[l], :]).then_inc(layer_in, 16)
                            if W_SELF[l] is None:
                                sp.dma_start(lnw[:, :], b1g.unsqueeze(0).to_broadcast([TILE, C])).then_inc(layer_in, 16)
                            else:
                                sp.dma_start(wt[:, 1, :], wt_d[:, W_SELF[l], :]).then_inc(layer_in, 16)
                                sp.dma_start(bias[:, :], (bl[l, :] if l < 4 else b3g).unsqueeze(0).to_broadcast([3, C])).then_inc(layer_in, 16)
                            if l < 4:
                                sp.dma_start(lnw[:, :], ln_w[l, :].unsqueeze(0).to_broadcast([TILE, C])).then_inc(layer_in, 16)
                                sp.dma_start(lnb[:, :], ln_b[l, :].unsqueeze(0).to_broadcast([TILE, C])).then_inc(layer_in, 16)
                            if l == 0:
                                sp.wait_ge(deg_stored, 16)
                                sp.dma_start(has_edge[:, :], deg_d.rearrange("(t p) -> p t", p=TILE), allow_slow_non_contiguous=True
                                             ).then_inc(deg_cols, 16)
                                sp.dma_start(counts_d, counts_all[0:TILE, SPILL * N:NT * N]).then_inc(counts_saved, 16)
                            if KINDS[l] == "sage_res":
                                def body(b, nt):
                                    sp.wait_ge(w_S("parts_ready"), at("parts_ready", l, b))
                                    sp.dma_start(x0[:, 0:nt, :], x[bass.ds(b * BLK, nt * TILE), :].rearrange("(t p) c -> p t c", p=TILE)
                                                 ).then_inc(w_S("x0_in"), 16)
                                over_blocks(sp, body)
                            if KINDS[l] == "final":
                                def body(b, nt):
                                    sp.wait_ge(w_S("z_ready"), at("z_ready", l, b, 1))
                                    sp.dma_start(out[bass.ds(b * BLK, nt * TILE), :].rearrange("(t p) c -> p t c", p=TILE),
                                                 z[:, 0:nt, :]).then_inc(w_S("out_done"), 16)
                                over_blocks(sp, body)
                                sp.wait_ge(w_S("out_done"), at("out_done", l, NBLK, 16))

        layers([0, 1, 2, 3, 4])

        arena_at = [SPILL * N + 16 - (SPILL * N) % 16]

        def carve(shape, dt=fp32):
            lanes, dims = shape[0], shape[1:]
            n = 2 * int(np.prod(dims))
            view = counts_all[0:lanes, arena_at[0]:arena_at[0] + n].bitcast(dt)
            arena_at[0] += n + (-n) % 16
            assert arena_at[0] <= NT * N + 3
            names = "abcde"[:len(dims)]
            if len(dims) == 1:
                return view
            return view.rearrange(f"p ({' '.join(names)}) -> p {' '.join(names)}", **{k: d for k, d in zip(names, dims)})

        Q = carve([TILE, NT + 1, C])
        acc = carve([TILE, NT + 1, VW])
        arena_mid = arena_at[0]
        x2 = parts[1]

        def transposed(pe, out_ps, tiles, nt):
            for j in range(nt):
                for part in range(2):
                    last = T.matmul(out_ps[:, j * TILE:(j + 1) * TILE], x2[:, tiles + j, part, :], ident_a[0:TILE, 4, :],
                                    start=(part == 0), stop=(part == 1))
            return last

        def blocks():
            for b in range(NBLK + 1):
                yield b, b * BLK, min(BLK, N - b * BLK), b * (BLK // TILE), min(BLK, N - b * BLK) // TILE

        def column(ap):
            return ap.unsqueeze(1)

        wo = sb("wo", [C, C], fp32)
        bcol6 = sb("bcol6", [C, 11], fp32)
        cols_in = sem("cols_in")
        s5 = ExitStack()
        with s5:
            t = lambda name, shape, dt: sb(name, shape, dt, s5)
            RING = 4
            kv = carve([LANES, RING, GRP, 2 * C])
            prod = carve([LANES, GRP, C])
            VA = [carve([LANES, GRP, VW]) for _ in range(2)]
            ohT = [carve([TILE, 2, GRP, LANES]) for _ in range(2)]
            oh16 = parts_all[0][:, :, :, :].rearrange("p t h c -> p (t h c)")[:, 0:4 * GRP * 2 * TILE].rearrange(
                "p (r k n) -> p r k n", r=4, k=GRP)
            oh32 = [t(f"oh32_{i}", [LANES, GRP, 2 * TILE], fp32) for i in range(2)]
            iota_n = t("iota_n", [LANES, 2 * TILE], fp16)
            ident_h = t("ident_h", [LANES, LANES], fp16)
            idx = [t(f"idx{i}", [LANES, 4 * GRP], i32) for i in range(2)]
            score = [t(f"score{i}", [LANES, GRP * HEADS], fp32) for i in range(2)]
            wtab = t("wtab", [1, 128], i32)
            srcidx = carve([LANES, CHP], i32)
            reldst = carve([LANES, CHP])
            dst_l = t("dst_l", [LANES, CH], fp32)
            qidx = t("qidx", [LANES, CH], i32)
            qidx_f = t("qidx_f", [LANES, CH], fp32)
            win_start = t("win_start", [LANES, NT], fp32)
            rel_all = t("rel_all", [LANES, NT], fp32)

            att_in = sem("att_in")
            acc_step = sem("acc_step")
            q_out_done = sem("q_out_done")
            att_consts = sem("att_consts")
            kv_in = [sem(f"kv_in{i}") for i in range(RING)]
            idx_ready = sem("idx_ready")
            pool_waits = sem("pool_waits")
            prod_ready = sem("prod_ready")
            score_sum = sem("score_sum")
            score_ready = sem("score_ready")
            a_ready = sem("a_ready")
            va_ready = sem("va_ready")
            oh_ready = sem("oh_ready")
            tr_done = sem("tr_done")
            ohT_ready = sem("ohT_ready")
            qe_done = sem("qe_done")
            oh32_ready = sem("oh32_ready")
            seg_done = sem("seg_done")
            seg_added = sem("seg_added")
            gen_idx = sem("gen_idx")
            gen_in = sem("gen_in")
            gen_score = sem("gen_score")
            gen_a = sem("gen_a")
            gen_oh = sem("gen_oh")
            gen_seg = sem("gen_seg")
            gen_added = sem("gen_added")

            arena_at[0] = arena_mid
            s4 = ExitStack()
            with s4:
                wkvq = carve([C, 3, C])
                hn_T = [carve([C, BLK]) for _ in range(2)]
                x2T = parts_all[0][:, :, :, :].rearrange("p t h c -> p (t h c)").bitcast(fp32)
                kv_out = [carve([TILE, 4, 2 * C]) for _ in range(2)]
                bst = carve([C, NBLK + 1, 6])
                bmv = carve([C, 2])
                bcol = carve([C, 8])
                bn_in = sem("bn_in")
                xb_done = sem("xb_done")
                xb_taken = sem("xb_taken")
                xb_stats = sem("xb_stats")
                bn_step = sem("bn_step")
                bn_var = sem("bn_var")
                bn_std = sem("bn_std")
                bn_ready = sem("bn_ready")
                hn_ready = sem("hn_ready")
                qkv_done = sem("qkv_done")
                kv_copied = sem("kv_copied")
                q_copied = sem("q_copied")
                kv_out_done = [sem("kv_out_done0"), sem("kv_out_done1")]
                with nc.Block() as block:
                    @block.sync
                    def _(sp):
                        sp.wait_ge(counts_saved, 16)
                        for tile, source in ((wtab[0:1, :], win_table_d), (srcidx[:, :], srcidx_d), (reldst[:, :], reldst_d),
                                             (dst_l[:, :], dstf_d[:, 0:CH])):
                            sp.dma_start(tile, source).then_inc(att_in, 16)
                        for i, w in enumerate((Wk, Wv, Wq)):
                            sp.dma_start(wkvq[:, i, :], w).then_inc(bn_in, 16)
                        sp.dma_start(bcol[:, 0:1], column(bn1_g)).then_inc(bn_in, 16)
                        sp.dma_start(bcol[:, 1:2], column(bn1_b)).then_inc(bn_in, 16)
                        for b, d0, w, t0, nt in blocks():
                            sp.wait_ge(kv_copied, t0 + nt)
                            sp.dma_start(kv_d[d0:d0 + w, :].rearrange("(t p) c -> p t c", p=TILE),
                                         kv_out[b % 2][:, 0:nt, :]).then_inc(kv_out_done[b % 2], 16)
                        sp.wait_ge(kv_out_done[0], 16 * (NBLK // 2 + 1))
                        sp.wait_ge(kv_out_done[1], 16 * (NBLK // 2))

                    @block.gpsimd
                    def _(pool):
                        G.iota(iota_n[:, :], pattern=[[1, 2 * TILE]], base=0, channel_multiplier=0,
                               allow_small_or_imprecise_dtypes=True)
                        G.iota(win_start[:, :], pattern=[[-TILE, NT]], base=0, channel_multiplier=0,
                               allow_small_or_imprecise_dtypes=True)
                        pool.wait_ge(counts_saved, 16)
                        G.memset(acc[:, :, :], 0.0)
                        G.memset(oh32[1][:, :, :], 0.0)

                    @block.tensor
                    def _(pe):
                        for b, d0, w, t0, nt in blocks():
                            if b >= 2:
                                pe.wait_ge(xb_taken, b - 1)
                            transposed(pe, ps[b % 2], t0, nt).then_inc(xb_done, 1)
                        for b, d0, w, t0, nt in blocks():
                            if b == 0:
                                pe.wait_ge(bn_in, 80)
                            pe.wait_ge(hn_ready, b + 1)
                            for j in range(nt):
                                tile = t0 + j
                                hn = hn_T[b % 2][:, j * TILE:(j + 1) * TILE]
                                if tile >= 3:
                                    pe.wait_ge(kv_copied, tile - 2)
                                    pe.wait_ge(q_copied, tile - 2)
                                T.matmul(ps[2 + tile % 3][0:TILE, 0:2 * C], hn, wkvq[:, 0:2, :].rearrange("p w c -> p (w c)"),
                                         start=True, stop=True)
                                T.matmul(ps[5 + tile % 3][0:TILE, 0:C], hn, wkvq[:, 2, :], start=True, stop=True).then_inc(qkv_done, 1)

                    @block.vector
                    def _(dve):
                        st = Steps(dve, bn_step)
                        for b, d0, w, t0, nt in blocks():
                            dve.wait_ge(xb_taken, b + 1)
                            V.bn_stats(bst[:, b, :], x2T[:, d0:d0 + w]).then_inc(xb_stats, 1)
                        dve.wait_ge(xb_stats, NBLK + 1)
                        V.bn_aggr(bmv[:, :], bst[:, :, :].rearrange("p b s -> p (b s)")).then_inc(bn_var, 1)
                        dve.wait_ge(bn_var, 1)
                        dve.wait_ge(bn_std, 1)
                        dve.wait_ge(bn_in, 80)
                        st.run(V.reciprocal(bcol[:, 3:4], bcol[:, 2:3]))
                        st.run(V.tensor_tensor(bcol[:, 4:5], bcol[:, 3:4], bcol[:, 0:1], ALU.mult))
                        st.run(V.tensor_tensor(bcol[:, 6:7], bmv[:, 0:1], bcol[:, 4:5], ALU.mult))
                        V.tensor_tensor(bcol[:, 5:6], bcol[:, 1:2], bcol[:, 6:7], ALU.subtract).then_inc(bn_ready, 1)
                        V.memset(Q[:, NT, :], 0.0)
                        V.tensor_copy(ident_h[:, :], ident[:, :])
                        dve.wait_ge(att_in, 64)
                        st = Steps(dve, acc_step)
                        st.run(V.tensor_scalar(qidx_f[:, :], dst_l[:, :], float(N - 1), None, ALU.min))
                        st.run(V.tensor_copy(qidx[:, :], qidx_f[:, :]))
                        for b, d0, w, t0, nt in blocks():
                            for j in range(nt):
                                dve.wait_ge(qkv_done, t0 + j + 1)
                                V.tensor_scalar(Q[:, t0 + j, :], ps[5 + (t0 + j) % 3][0:TILE, 0:C], 1.0 / float(np.sqrt(HD)),
                                                None, ALU.mult).then_inc(q_copied, 1)

                    @block.scalar
                    def _(act):
                        for b, d0, w, t0, nt in blocks():
                            act.wait_ge(xb_done, b + 1)
                            S.copy(x2T[:, d0:d0 + w], ps[b % 2][:, 0:w]).then_inc(xb_taken, 1)
                        act.wait_ge(bn_var, 1)
                        S.activation(bcol[:, 2:3], bmv[:, 1:2], ACT.Sqrt, bias=eps_t[:, 0:1]).then_inc(bn_std, 1)
                        act.wait_ge(bn_ready, 1)
                        act.wait_ge(xb_taken, NBLK + 1)
                        every = list(blocks())

                        def norm(b, d0, w):
                            if b >= 2:
                                act.wait_ge(qkv_done, 4 * (b - 1))
                            S.activation(hn_T[b % 2][:, 0:w], x2T[:, d0:d0 + w], ACT.Identity,
                                         scale=bcol[:, 4:5], bias=bcol[:, 5:6]).then_inc(hn_ready, 1)

                        norm(*every[0][:3])
                        for b, d0, w, t0, nt in every:
                            if b < NBLK:
                                norm(*every[b + 1][:3])
                            if b >= 2:
                                act.wait_ge(kv_out_done[b % 2], 16 * (b // 2))
                            for j in range(nt):
                                act.wait_ge(qkv_done, t0 + j + 1)
                                S.copy(kv_out[b % 2][:, j, :], ps[2 + (t0 + j) % 3][0:TILE, 0:2 * C]).then_inc(kv_copied, 1)

            a_ps = [ps[7][:, 32 * i:32 * i + 32].rearrange("p (k h) -> p k h", h=HEADS) for i in range(2)]

            def windows_spanned(engine):
                return load_registers(nc, engine, wtab[0:1, 124:128], NT)[3]

            with nc.Block() as block:
                @block.sync
                def _(sp):
                    sp.dma_start(q_d.rearrange("(t p) c -> p t c", p=TILE), Q[:, 0:NT, :]).then_inc(q_out_done, 16)
                    sp.dma_start(wo[:, :], Wo).then_inc(cols_in, 16)
                    for i, col in ((0, bn2_g), (1, bn2_b), (7, bo), (8, b1[0:C]), (9, b1[C:2 * C]), (10, b2)):
                        sp.dma_start(bcol6[:, i:i + 1], column(col)).then_inc(cols_in, 16)
                    sp.wait_ge(cols_in, 16 * 7)
                    sp.wait_ge(q_out_done, 16)

                @block.gpsimd
                def _(pool):
                    wide = windows_spanned(ET.Pool)

                    def gather(out_rows, table_d, index, signal):
                        G.indirect_dma_start(out=out_rows, out_offset=None, in_=table_d,
                                             in_offset=bass.IndirectOffsetOnAxis(ap=index, axis=0)).then_inc(signal, 16)

                    with pool.If(wide <= 1):
                        with pool.Fori(0, NG // (2 * RING)) as i:
                            for h in range(2):
                                g0 = i * 2 * RING + h * RING
                                pool.wait_ge(va_ready, g0 + 1)
                                pool.sem_inc(pool_waits, 1)
                                G.tensor_copy(idx[h][:, :], srcidx[:, bass.ds(i * (2 * RING * GRP) + h * RING * GRP, RING * GRP)]
                                              ).then_inc(idx_ready, 1)
                                pool.wait_ge(idx_ready, i * 2 + h + 1)
                                pool.sem_inc(pool_waits, 1)
                                for r in range(RING):
                                    pool.wait_ge(va_ready, g0 + r + 2)
                                    pool.sem_inc(pool_waits, 1)
                                    for k in range(GRP):
                                        gather(kv[:, r, k, :], kv_d, idx[h][:, r * GRP + k:r * GRP + k + 1], kv_in[r])
                    with pool.Else():
                        pool.wait_ge(oh_ready, 1)
                        pool.sem_inc(pool_waits, 1)
                        pool.wait_ge(q_out_done, 16)
                        pool.sem_inc(pool_waits, 1)
                        with pool.Fori(0, CH) as c:
                            pool.wait_ge(gen_added, c * NT + 1)
                            pool.sem_inc(pool_waits, 1)
                            G.tensor_copy(idx[0][:, 0:1], srcidx[:, bass.ds(c, 1)]).then_inc(gen_idx, 1)
                            G.tensor_copy(idx[0][:, 1:2], qidx[:, bass.ds(c, 1)]).then_inc(gen_idx, 1)
                            pool.wait_ge(gen_idx, c * 2 + 2)
                            pool.sem_inc(pool_waits, 1)
                            gather(kv[:, 0, 0, :], kv_d, idx[0][:, 0:1], gen_in)
                            gather(kv[:, 0, 1, 0:C], q_d, idx[0][:, 1:2], gen_in)

                @block.vector
                def _(dve):
                    wide = windows_spanned(ET.DVE)
                    iota_ps = ps[6][:, 0:2 * TILE]
                    sums_ps = [ps[6][:, 256 + 32 * i:288 + 32 * i] for i in range(2)]
                    V.tensor_copy(iota_ps, iota_n[:, :])
                    V.memset(VA[1][:, :, :], 0.0)
                    V.memset(ps[4][:, :], 0.0).then_inc(att_consts, 1)
                    dve.sem_inc(score_sum, 1)
                    dve.sem_inc(seg_added, 1)
                    dve.sem_inc(gen_added, 1)
                    dve.wait_ge(att_consts, 1)

                    def one_hots(column, place, ks=range(GRP)):
                        for k in ks:
                            last = V.tensor_scalar(oh16[:, place, k, :], iota_ps, reldst[:, bass.ds(column + k, 1)],
                                                   None, ALU.is_equal)
                        if GRP - 1 in ks:
                            last.then_inc(oh_ready, 1)

                    def add(w0, bank, added):
                        dve.wait_ge(seg_added, added + 1)
                        V.tensor_tensor(acc[:, bass.ds(w0, 2), :], acc[:, bass.ds(w0, 2), :],
                                        ps[4 + bank][0:TILE, 0:2 * VW].rearrange("p (w c) -> p w c", w=2),
                                        ALU.add).then_inc(seg_added, 1)

                    with dve.If(wide <= 1):
                        dve.sem_inc(va_ready, RING + 1)
                        one_hots(0, 0)
                        one_hots(GRP, 1)
                        with dve.Fori(0, NG // 8) as pair:
                            for half in range(2):
                                i = pair * 2 + half
                                w0 = load_registers(nc, ET.DVE, wtab[0:1, bass.ds(i * 4, 4)], NT - 1, WINDOWS_CLAMPED)
                                for r in range(4):
                                    g = i * 4 + r
                                    dve.wait_ge(kv_in[r], (i + 1) * 16 * GRP)
                                    dve.wait_ge(qe_done, g + 1)
                                    dve.wait_ge(score_sum, g + 1)
                                    V.tensor_tensor(prod[:, :, :], kv[:, r, :, 0:C],
                                                    ps[2 + r % 2][:, 0:GRP * C].rearrange("p (k c) -> p k c", k=GRP),
                                                    ALU.mult).then_inc(prod_ready, 1)
                                    one_hots((g + 2) * GRP, (r + 2) % 4, range(0, GRP // 2))
                                    dve.wait_ge(prod_ready, g + 1)
                                    V.tensor_reduce(out=sums_ps[r % 2], in_=prod[:, :, :].rearrange("p k (h c) -> p (k h) c", h=HEADS),
                                                    axis=AX.X, op=ALU.add).then_inc(score_sum, 1)
                                    one_hots((g + 2) * GRP, (r + 2) % 4, range(GRP // 2, GRP))
                                    dve.wait_ge(score_sum, g + 2)
                                    V.tensor_scalar(score[r % 2][:, :], sums_ps[r % 2], 5.0, -5.0, ALU.min, ALU.max).then_inc(score_ready, 1)
                                    dve.wait_ge(seg_done, g + 1)
                                    add(w0[r], r % 2, g)
                                    dve.wait_ge(a_ready, g + 1)
                                    V.tensor_tensor(VA[r % 2][:, :, 0:C].rearrange("p k (h c) -> p k h c", h=HEADS),
                                                    kv[:, r, :, C:2 * C].rearrange("p k (h c) -> p k h c", h=HEADS),
                                                    a_ps[r % 2].unsqueeze(3).to_broadcast([LANES, GRP, HEADS, HD]),
                                                    ALU.mult).then_inc(va_ready, 1)
                        w0 = load_registers(nc, ET.DVE, wtab[0:1, NG:NG + 4], NT - 1)
                        for r in range(2):
                            dve.wait_ge(seg_done, NG + r + 1)
                            add(w0[r], r, NG + r)
                    with dve.Else():
                        dve.sem_inc(oh_ready, 1)
                        with dve.Fori(0, CH) as c:
                            dve.wait_ge(gen_in, (c + 1) * 32)
                            V.tensor_tensor(prod[:, 0, :], kv[:, 0, 0, 0:C], kv[:, 0, 1, 0:C], ALU.mult).then_inc(prod_ready, 1)
                            V.tensor_scalar(rel_all[:, :], win_start[:, :], dst_l[:, bass.ds(c, 1)], None, ALU.add)
                            dve.wait_ge(prod_ready, c + 1)
                            V.tensor_reduce(out=score[0][:, 0:HEADS], in_=prod[:, 0, :].rearrange("p (h c) -> p h c", h=HEADS),
                                            axis=AX.X, op=ALU.add).then_inc(score_sum, 1)
                            dve.wait_ge(score_sum, c + 2)
                            V.tensor_scalar(score[0][:, 0:HEADS], score[0][:, 0:HEADS], 5.0, -5.0, ALU.min, ALU.max).then_inc(gen_score, 1)
                            dve.wait_ge(gen_a, c + 1)
                            V.tensor_tensor(VA[0][:, 0, 0:C].rearrange("p (h c) -> p h c", h=HEADS),
                                            kv[:, 0, 0, C:2 * C].rearrange("p (h c) -> p h c", h=HEADS),
                                            VA[0][:, 0, C:VW].unsqueeze(2).to_broadcast([LANES, HEADS, HD]), ALU.mult)
                            with dve.Fori(0, NT) as w:
                                dve.wait_ge(gen_added, c * NT + w + 1)
                                V.tensor_scalar(oh32[0][:, 0, 0:TILE], iota_n[:, 0:TILE], rel_all[:, bass.ds(w, 1)], None,
                                                ALU.is_equal).then_inc(gen_oh, 1)
                                dve.wait_ge(gen_seg, c * NT + w + 1)
                                V.tensor_tensor(acc[:, bass.ds(w, 1), :], acc[:, bass.ds(w, 1), :],
                                                ps[4][0:TILE, 0:VW].unsqueeze(1), ALU.add).then_inc(gen_added, 1)

                @block.tensor
                def _(pe):
                    pe.wait_ge(att_consts, 1)
                    pe.sem_inc(seg_done, 1)
                    wide = windows_spanned(ET.PE)

                    def turn(place, n):
                        pe.wait_ge(oh_ready, n + 1)
                        bank = ps[place % 2][:, :].bitcast(fp16)
                        for w in range(2):
                            for k in range(GRP):
                                last = T.transpose(bank[0:TILE, (w * GRP + k) * LANES:(w * GRP + k + 1) * LANES],
                                                   oh16[:, place, k, w * TILE:(w + 1) * TILE], ident_h[:, :])
                        last.then_inc(tr_done, 1)

                    def pick(place, n, w0):
                        pe.wait_ge(ohT_ready, n + 1)
                        for k in range(GRP):
                            for w in range(2):
                                last = T.matmul(ps[2 + place % 2][:, k * C:(k + 1) * C], ohT[place % 2][:, w, k, :],
                                                Q[:, bass.ds(w0 + w, 1), :].rearrange("p w c -> p (w c)"), start=(w == 0), stop=(w == 1))
                        last.then_inc(qe_done, 1)

                    def sums(place, n):
                        pe.wait_ge(va_ready, RING + n + 2)
                        pe.wait_ge(oh32_ready, n + 2)
                        pe.wait_ge(seg_added, n + 2)
                        for w in range(2):
                            for k in range(GRP):
                                last = T.matmul(ps[4 + place % 2][0:TILE, w * VW:(w + 1) * VW],
                                                oh32[place % 2][:, k, w * TILE:(w + 1) * TILE], VA[place % 2][:, k, :],
                                                start=(k == 0), stop=(k == GRP - 1))
                        last.then_inc(seg_done, 1)

                    with pe.If(wide <= 1):
                        w0 = load_registers(nc, ET.PE, wtab[0:1, 0:4], NT - 1)
                        for r in range(2):
                            turn(r, r)
                            pick(r, r, w0[2 + r])
                        with pe.Fori(0, NG // 8) as pair:
                            for half in range(2):
                                i = pair * 2 + half
                                w0 = load_registers(nc, ET.PE, wtab[0:1, bass.ds(i * 4 + 4, 4)], NT - 1, WINDOWS_CLAMPED)
                                for r in range(4):
                                    g = i * 4 + r
                                    pe.wait_ge(ohT_ready, g + 1)
                                    turn((r + 2) % 4, g + 2)
                                    sums(r + 3, g - 1)
                                    pe.wait_ge(prod_ready, g + 1)
                                    pick((r + 2) % 4, g + 2, w0[r])
                        sums(3, NG - 1)
                    with pe.Else():
                        with pe.Fori(0, CH) as c:
                            with pe.Fori(0, NT) as w:
                                pe.wait_ge(gen_oh, c * NT + w + 1)
                                T.matmul(ps[4][0:TILE, 0:VW], oh32[0][:, 0, 0:TILE], VA[0][:, 0, :], start=True,
                                         stop=True).then_inc(gen_seg, 1)

                @block.scalar
                def _(act):
                    act.sem_inc(oh32_ready, 1)
                    wide = windows_spanned(ET.Activation)

                    def copy_turned(place, n):
                        act.wait_ge(tr_done, n + 1)
                        S.copy(ohT[place % 2][:, :, :, :].rearrange("p w k n -> p (w k n)"),
                               ps[place % 2][:, :].bitcast(fp16)[0:TILE, :]).then_inc(ohT_ready, 1)

                    def widen(place, n):
                        act.wait_ge(oh_ready, n + 1)
                        S.copy(oh32[place % 2][:, :, :], oh16[:, place, :, :]).then_inc(oh32_ready, 1)

                    with act.If(wide <= 1):
                        copy_turned(0, 0)
                        copy_turned(1, 1)
                        widen(0, 0)
                        with act.Fori(0, NG // 8) as pair:
                            for half in range(2):
                                i = pair * 2 + half
                                for r in range(4):
                                    g = i * 4 + r
                                    act.wait_ge(score_ready, g + 1)
                                    act.wait_ge(seg_done, g + 1)
                                    by_head = score[r % 2][:, :].rearrange("p (k h) -> p k h", h=HEADS)
                                    S.activation(a_ps[r % 2], by_head, ACT.Exp)
                                    S.activation(VA[r % 2][:, :, C:VW], by_head, ACT.Exp).then_inc(a_ready, 1)
                                    act.wait_ge(qe_done, g + 1)
                                    copy_turned(r + 2, g + 2)
                                    act.wait_ge(seg_done, g + 2)
                                    widen((r + 1) % 4, g + 1)
                    with act.Else():
                        with act.Fori(0, CH) as c:
                            act.wait_ge(gen_score, c + 1)
                            S.activation(VA[0][:, 0, C:VW], score[0][:, 0:HEADS], ACT.Exp).then_inc(gen_a, 1)

        arena_at[0] = arena_mid
        s6 = ExitStack()
        with s6:
            t = lambda name, shape, dt: sb(name, shape, dt, s6)
            wvT = [carve([C, BLK]) for _ in range(2)]
            h2T = parts_all[0][:, :, :, :].rearrange("p t h c -> p (t h c)").bitcast(fp32)
            rden = carve([TILE, NT, HEADS])
            w1 = t("w1", [C, 2 * C], fp32)
            w2 = t("w2", [C, 2, C], fp32)
            hn = t("hn", [C, BLK], fp32)
            hid = [t(f"hid{i}", [C, 2, BLK], fp32) for i in range(2)]
            arena_at[0] = (NT - 1) * N + 16 - (NT - 1) * N % 16
            u = [carve([TILE, BLK // TILE, C]) for _ in range(2)]
            bst = t("bst6", [C, NBLK + 1, 6], fp32)
            bmv = t("bmv6", [C, 2], fp32)
            bcol = bcol6
            b2_added = sem("b2_added")
            stats = t("stats6", [TILE, 4, 6], fp32)
            mv = t("mv6", [TILE, 4, 2], fp32)
            std = t("std6", [TILE, 4], fp32)
            rstd = t("rstd6", [TILE, 4], fp32)
            ff_in = sem("ff_in")
            rden_step = sem("rden_step")
            wv_ready = sem("wv_ready")
            wvt_done = sem("wvt_done")
            wvt_copied = sem("wvt_copied")
            h2_done = sem("h2_done")
            h2_copied = sem("h2_copied")
            h2_stats = sem("h2_stats")
            bn2_step = sem("bn2_step")
            bn2_var = sem("bn2_var")
            bn2_std = sem("bn2_std")
            bn2_ready = sem("bn2_ready")
            hn2_ready = sem("hn2_ready")
            hid_done = sem("hid_done")
            hid_copied = sem("hid_copied")
            ff_done = sem("ff_done")
            u_ready = sem("u_ready")
            u_stats = sem("u_stats")
            u_std = sem("u_std")
            u_normed = sem("u_normed")
            hi_ready = sem("hi_ready")
            u_step = sem("u_step")
            with nc.Block() as block:
                @block.sync
                def _(sp):
                    sp.dma_start(w1[:, :], W1).then_inc(ff_in, 16)
                    sp.dma_start(w2[:, :, :], W2.rearrange("(j f) c -> f j c", j=2)).then_inc(ff_in, 16)
                    sp.wait_ge(h2_copied, NBLK + 1)
                    sp.dma_start(counts_all[0:TILE, SPILL * N:(NT - 1) * N], counts_d[:, 0:(NT - 1 - SPILL) * N]).then_inc(counts_back, 16)
                    sp.wait_ge(counts_back, 16)

                @block.tensor
                def _(pe):
                    def turn(b, nt, t0):
                        pe.wait_ge(wv_ready, b + 1)
                        if b >= 2:
                            pe.wait_ge(wvt_copied, b - 1)
                        for j in range(nt):
                            last = T.transpose(ps[b % 2][:, j * TILE:(j + 1) * TILE], acc[:, t0 + j, 0:C], ident[0:TILE, 0:TILE])
                        last.then_inc(wvt_done, 1)

                    def hidden(b, w):
                        pe.wait_ge(hn2_ready, b + 1)
                        if b:
                            pe.wait_ge(hid_copied, b)
                        for j in range(2):
                            last = T.matmul(ps[4 + j][:, 0:w], w1[:, j * C:(j + 1) * C], hn[:, 0:w], start=True, stop=True)
                        last.then_inc(hid_done, 1)

                    every = list(blocks())
                    turn(0, 4, 0)
                    for b, d0, w, t0, nt in every:
                        if b < NBLK:
                            turn(b + 1, every[b + 1][4], every[b + 1][3])
                        pe.wait_ge(wvt_copied, b + 1)
                        if b >= 2:
                            pe.wait_ge(h2_copied, b - 1)
                        for j in range(nt):
                            o = ps[2 + b % 2][:, j * TILE:(j + 1) * TILE]
                            T.matmul(o, wo[:, :], wvT[b % 2][:, j * TILE:(j + 1) * TILE], start=True, stop=False)
                            for part in range(2):
                                last = T.matmul(o, x2[:, t0 + j, part, :], ident_a[0:TILE, 4, :], start=False, stop=(part == 1))
                        last.then_inc(h2_done, 1)
                    pe.wait_ge(ff_in, 32)
                    hidden(0, BLK)
                    for b, d0, w, t0, nt in every:
                        if b < NBLK:
                            hidden(b + 1, every[b + 1][2])
                        pe.wait_ge(hid_copied, b + 1)
                        if b >= 2:
                            pe.wait_ge(u_ready, b - 1)
                        for j in range(nt):
                            y = ps[6 + b % 2][0:TILE, j * C:(j + 1) * C]
                            cols = slice(j * TILE, (j + 1) * TILE)
                            T.matmul(y, hid[b % 2][:, 0, cols], w2[:, 0, :], start=True, stop=False)
                            T.matmul(y, hid[b % 2][:, 1, cols], w2[:, 1, :], start=False, stop=False)
                            last = T.matmul(y, h2T[:, d0 + j * TILE:d0 + (j + 1) * TILE], ident[:, :], start=False, stop=True)
                        last.then_inc(ff_done, 1)

                @block.scalar
                def _(act):
                    act.wait_ge(b2_added, 1)
                    every = list(blocks())

                    def copy_turned(b, w):
                        act.wait_ge(wvt_done, b + 1)
                        if b >= 2:
                            act.wait_ge(h2_done, b - 1)
                        S.copy(wvT[b % 2][:, 0:w], ps[b % 2][:, 0:w]).then_inc(wvt_copied, 1)

                    copy_turned(0, BLK)
                    for b, d0, w, t0, nt in every:
                        if b < NBLK:
                            copy_turned(b + 1, every[b + 1][2])
                        act.wait_ge(h2_done, b + 1)
                        S.activation(h2T[:, d0:d0 + w], ps[2 + b % 2][:, 0:w], ACT.Identity, bias=bcol[:, 7:8]).then_inc(h2_copied, 1)
                    act.wait_ge(bn2_var, 1)
                    S.activation(bcol[:, 2:3], bmv[:, 1:2], ACT.Sqrt, bias=eps_t[:, 0:1]).then_inc(bn2_std, 1)
                    act.wait_ge(bn2_ready, 1)
                    act.wait_ge(h2_copied, NBLK + 1)

                    def norm(b, d0, w):
                        if b:
                            act.wait_ge(hid_done, b)
                        S.activation(hn[:, 0:w], h2T[:, d0:d0 + w], ACT.Identity, scale=bcol[:, 4:5],
                                     bias=bcol[:, 5:6]).then_inc(hn2_ready, 1)

                    def relu(b, w):
                        act.wait_ge(hid_done, b + 1)
                        if b >= 2:
                            act.wait_ge(ff_done, b - 1)
                        for j in range(2):
                            last = S.activation(hid[b % 2][:, j, 0:w], ps[4 + j][:, 0:w], ACT.Relu, bias=bcol[:, 8 + j:9 + j])
                        last.then_inc(hid_copied, 1)

                    norm(*every[0][:3])
                    relu(0, BLK)
                    norm(*every[1][:3])
                    def high_part(b, t0, nt):
                        act.wait_ge(u_normed, b + 1)
                        S.activation(x2[:, t0:t0 + nt, 0, :], u[b % 2][:, 0:nt, :], ACT.Copy, scale=ALPHA_LN).then_inc(hi_ready, 1)

                    for b, d0, w, t0, nt in every:
                        if b < NBLK:
                            relu(b + 1, every[b + 1][2])
                        if b:
                            high_part(b - 1, t0 - BLK // TILE, BLK // TILE)
                        if b < NBLK - 1:
                            norm(*every[b + 2][:3])
                        act.wait_ge(u_stats, b + 1)
                        S.activation(std[:, 0:nt], mv[:, 0:nt, 1], ACT.Sqrt, bias=eps_t[0:TILE, 0:1]).then_inc(u_std, 1)
                    high_part(NBLK, NBLK * BLK // TILE, NT - NBLK * BLK // TILE)

                @block.vector
                def _(dve):
                    V.tensor_tensor(bcol[:, 7:8], bcol[:, 7:8], bcol[:, 10:11], ALU.add).then_inc(b2_added, 1)
                    st = Steps(dve, rden_step)
                    st.run(V.tensor_scalar(rden[:, :, :], acc[:, 0:NT, C:VW], 1e-30, None, ALU.max))
                    st.run(V.reciprocal(rden[:, :, :], rden[:, :, :]))
                    for b, d0, w, t0, nt in blocks():
                        wv = acc[:, t0:t0 + nt, 0:C].rearrange("p t (h c) -> p t h c", h=HEADS)
                        V.tensor_tensor(wv, wv, rden[:, t0:t0 + nt, :].unsqueeze(3).to_broadcast([TILE, nt, HEADS, HD]),
                                        ALU.mult).then_inc(wv_ready, 1)
                    for b, d0, w, t0, nt in blocks():
                        dve.wait_ge(h2_copied, b + 1)
                        V.bn_stats(bst[:, b, :], h2T[:, d0:d0 + w]).then_inc(h2_stats, 1)
                    dve.wait_ge(h2_stats, NBLK + 1)
                    V.bn_aggr(bmv[:, :], bst[:, :, :].rearrange("p b s -> p (b s)")).then_inc(bn2_var, 1)
                    dve.wait_ge(bn2_var, 1)
                    dve.wait_ge(bn2_std, 1)
                    bn_st = Steps(dve, bn2_step)
                    bn_st.run(V.reciprocal(bcol[:, 3:4], bcol[:, 2:3]))
                    bn_st.run(V.tensor_tensor(bcol[:, 4:5], bcol[:, 3:4], bcol[:, 0:1], ALU.mult))
                    bn_st.run(V.tensor_tensor(bcol[:, 6:7], bmv[:, 0:1], bcol[:, 4:5], ALU.mult))
                    V.tensor_tensor(bcol[:, 5:6], bcol[:, 1:2], bcol[:, 6:7], ALU.subtract).then_inc(bn2_ready, 1)
                    u_st = Steps(dve, u_step)

                    def low_part(b, t0, nt):
                        dve.wait_ge(hi_ready, b + 1)
                        u_st.run(V.scalar_tensor_tensor(x2[:, t0:t0 + nt, 1, :], u[b % 2][:, 0:nt, :], ALPHA_LN,
                                                       x2[:, t0:t0 + nt, 0, :], ALU.mult, ALU.subtract))

                    for b, d0, w, t0, nt in blocks():
                        u_ = u[b % 2][:, 0:nt, :]
                        u_st.run(V.tensor_tensor(u_, x2[:, t0:t0 + nt, 0, :], x2[:, t0:t0 + nt, 1, :], ALU.add))
                        dve.wait_ge(ff_done, b + 1)
                        V.scalar_tensor_tensor(u_, u_, 1.0 / ALPHA_LN,
                                               ps[6 + b % 2][0:TILE, 0:nt * C].rearrange("p (j c) -> p j c", c=C),
                                               ALU.mult, ALU.add).then_inc(u_ready, 1)
                        dve.wait_ge(u_ready, b + 1)
                        for j in range(nt):
                            last = V.bn_stats(stats[:, j, :], u[b % 2][:, j, :])
                        u_st.run(last)
                        for j in range(nt):
                            last = V.bn_aggr(mv[:, j, :], stats[:, j, :])
                        last.then_inc(u_stats, 1)
                        if b:
                            low_part(b - 1, t0 - BLK // TILE, BLK // TILE)
                        dve.wait_ge(u_std, b + 1)
                        u_st.run(V.reciprocal(rstd[:, 0:nt], std[:, 0:nt]))
                        for j in range(nt):
                            last = V.tensor_scalar(u[b % 2][:, j, :], u[b % 2][:, j, :], mv[:, j, 0:1], rstd[:, j:j + 1],
                                                   ALU.subtract, ALU.mult)
                        last.then_inc(u_normed, 1)
                    low_part(NBLK, NBLK * BLK // TILE, NT - NBLK * BLK // TILE)
        layers([5])


_INS = ["x", "src", "dst", "L0_gnn_Wl", "L0_gnn_bl", "L0_gnn_Wr", "L0_gnn_ln_w", "L0_gnn_ln_b", "L1_gnn_W", "L1_gnn_b",
        "L2_gnn_Wq", "L2_gnn_Wk", "L2_gnn_Wv", "L2_gnn_Wo", "L2_gnn_bo", "L2_gnn_bn1_g", "L2_gnn_bn1_b",
        "L2_gnn_bn2_g", "L2_gnn_bn2_b", "L2_gnn_W1", "L2_gnn_b1", "L2_gnn_W2", "L2_gnn_b2", "L3_gnn_W", "L3_gnn_b"]


def kernel(**inputs):
    import concourse.bacc as bacc
    from concourse.bass_utils import run_bass_kernel_spmd

    nc = bacc.Bacc("TRN2", target_bir_lowering=False, num_devices=1)
    arrays, args = {}, []
    for name in _INS:
        a = np.ascontiguousarray(inputs[name])
        arrays[f"in_{name}"] = a
        args.append(nc.dram_tensor(f"in_{name}", a.shape, mybir.dt.from_np(a.dtype), kind="ExternalInput").ap())
    out = nc.dram_tensor("out", (N, C), fp32, kind="ExternalOutput").ap()
    build(nc, *args, out)
    return run_bass_kernel_spmd(nc, [arrays], core_ids=[0]).results[0]["out"]
```
